# Optimizing a Trainium2 kernel written in Bass

```python
import numpy as np
import jax
import jax.numpy as jnp

def _softmax(x, axis=-1):
    return jax.nn.softmax(x, axis=axis)

def _gelu(x):
    return jax.nn.gelu(x, approximate=True)

def _silu(x):
    return jax.nn.silu(x)

def _sigmoid(x):
    return jax.nn.sigmoid(x)

def _layernorm(x, axis=-1, eps=1e-05):
    m = jnp.mean(x, axis=axis, keepdims=True)
    v = jnp.var(x, axis=axis, keepdims=True)
    return (x - m) / jnp.sqrt(v + eps)

def _scatter_add(tgt, idx, src, axis=0):
    return tgt.at[idx].add(src)

def _segment_sum(src, seg, n):
    return jax.ops.segment_sum(src, seg, n)
kernel_name = 'mk_decoder_postln_d1_seqx_r4_91d84b'

def setup_inputs(seed: int=0):
    np.random.seed(seed)
    _w = jnp.asarray

    def _rec_inputs():
        import jax
        import jax.numpy as jnp
        _rk = jax.random.key(seed)
        x = -0.0002928 + 1 * jax.random.normal(jax.random.fold_in(_rk, 1), (16, 512, 256), jnp.float32)
        _lenS = 512 - jax.random.randint(jax.random.fold_in(_rk, 7), (16,), 0, max(1, 512 // 4) + 1, jnp.int32)
        _lenS2 = 64 - jax.random.randint(jax.random.fold_in(_rk, 8), (16,), 0, max(1, 64 // 4) + 1, jnp.int32)
        _ctx_1024P = jax.random.normal(jax.random.fold_in(_rk, 11), (16, 16, 256), jnp.float32)
        _ctx_1024c = jax.random.dirichlet(jax.random.fold_in(_rk, 511), 0.3 * jnp.ones((16,), jnp.float32), (16, 64))
        _ctx_1024t = jnp.einsum('bsk,bkd->bsd', _ctx_1024c, _ctx_1024P)
        _ctx_1024t = _ctx_1024t * jax.lax.rsqrt(jnp.mean(jnp.square(_ctx_1024t)) + 1e-12) * 0.953939
        ctx_1024 = -1.39393e-06 + 0.999914 * (_ctx_1024t + 0.3 * jax.random.normal(jax.random.fold_in(_rk, 611), (16, 64, 256), jnp.float32))
        _validS = jnp.arange(512)[None, :] < _lenS[:, None]
        _validS2 = jnp.arange(64)[None, :] < _lenS2[:, None]
        _causal = jnp.tril(jnp.ones((512, 512), dtype=bool))
        mask_1x1xSxS2_ik0 = jnp.where(jnp.broadcast_to(_validS2[0:1, None, None, :], (1, 1, 512, 64)), 0, 1).astype(jnp.int32)
        return (x, ctx_1024, mask_1x1xSxS2_ik0)
    x, ctx_1024, mask_1x1xSxS2_ik0 = _rec_inputs()

    def _L0_attn_setup():
        import jax, jax.numpy as jnp
        import numpy as np
        NUM_HEADS = 16
        MAX_REL = 128

        def _rel_embeds(table, q_len, k_len):
            dist = jnp.arange(q_len)[:, None] - jnp.arange(k_len)[None, :]
            idx = jnp.clip(dist, -MAX_REL, MAX_REL) + MAX_REL
            return table[idx]
        key = jax.random.key(seed)
        ks = jax.random.split(key, 11)
        B, T, E = (4, 256, 256)
        D = E // NUM_HEADS
        P = 2 * MAX_REL + 1
        s = 0.02
        return {'hidden_states': jax.random.normal(ks[0], (B, T, E), jnp.float32), 'Wq': jax.random.normal(ks[1], (E, E), jnp.float32) * s, 'bq': jax.random.normal(ks[2], (E,), jnp.float32) * s, 'Wk': jax.random.normal(ks[3], (E, E), jnp.float32) * s, 'bk': jax.random.normal(ks[4], (E,), jnp.float32) * s, 'Wv': jax.random.normal(ks[5], (E, E), jnp.float32) * s, 'bv': jax.random.normal(ks[6], (E,), jnp.float32) * s, 'Wo': jax.random.normal(ks[7], (E, E), jnp.float32) * s, 'bo': jax.random.normal(ks[8], (E,), jnp.float32) * s, 'rel_k_emb': jax.random.normal(ks[9], (P, D), jnp.float32) * s, 'rel_v_emb': jax.random.normal(ks[10], (P, D), jnp.float32) * s}
    _L0_attn_all = _L0_attn_setup()
    _L0_attn_in = {k: v for k, v in _L0_attn_all.items() if k in ('Wq', 'bq', 'Wk', 'bk', 'Wv', 'bv', 'Wo', 'bo', 'rel_k_emb', 'rel_v_emb')}
    del _L0_attn_all

    def _L0_xattn_setup():
        import jax, jax.numpy as jnp
        import numpy as np
        B, S, D, H = (2, 512, 256, 16)
        DK = D // H
        key = jax.random.key(seed)
        ks = jax.random.split(key, 12)
        sc = 1.0 / np.sqrt(D)
        inp = {'q': jax.random.normal(ks[0], (B, S, D), jnp.float32), 'k': jax.random.normal(ks[1], (B, S, D), jnp.float32), 'v': jax.random.normal(ks[2], (B, S, D), jnp.float32), 'mask': jnp.tril(jnp.ones((S, S), jnp.int32))[None, None], 'Wq': jax.random.normal(ks[3], (D, D), jnp.float32) * sc, 'bq': jax.random.normal(ks[4], (D,), jnp.float32) * 0.02, 'Wk': jax.random.normal(ks[5], (D, D), jnp.float32) * sc, 'bk': jax.random.normal(ks[6], (D,), jnp.float32) * 0.02, 'Wv': jax.random.normal(ks[7], (D, D), jnp.float32) * sc, 'bv': jax.random.normal(ks[8], (D,), jnp.float32) * 0.02, 'Wo': jax.random.normal(ks[9], (D, D), jnp.float32) * sc, 'bo': jax.random.normal(ks[10], (D,), jnp.float32) * 0.02}
        return inp
    _L0_xattn_all = _L0_xattn_setup()
    _L0_xattn_in = {k: v for k, v in _L0_xattn_all.items() if k in ('Wq', 'bq', 'Wk', 'bk', 'Wv', 'bv', 'Wo', 'bo')}
    del _L0_xattn_all

    def _L0_ffn_setup():
        import jax, jax.numpy as jnp
        import numpy as np
        B, S, H, I = (2, 512, 256, 128)
        E, K, G, TG = (64, 8, 8, 4)
        SCALE = 2.5
        CAP = 256
        key = jax.random.key(seed)
        ks = jax.random.split(key, 6)
        hidden_states = jax.random.normal(ks[0], (B, S, H), jnp.float32)
        gate_w = jax.random.normal(ks[1], (E, H), jnp.float32) * 0.02
        gate_bias = jax.random.normal(ks[2], (E,), jnp.float32) * 0.02
        w_gate = jax.random.normal(ks[3], (E, H, I), jnp.float32) * (1.0 / np.sqrt(H))
        w_up = jax.random.normal(ks[4], (E, H, I), jnp.float32) * (1.0 / np.sqrt(H))
        w_down = jax.random.normal(ks[5], (E, I, H), jnp.float32) * (1.0 / np.sqrt(I))
        return {'hidden_states': hidden_states, 'gate_w': gate_w, 'gate_bias': gate_bias, 'w_gate': w_gate, 'w_up': w_up, 'w_down': w_down}
    _L0_ffn_all = _L0_ffn_setup()
    _L0_ffn_in = {k: v for k, v in _L0_ffn_all.items() if k in ('gate_w', 'gate_bias', 'w_gate', 'w_up', 'w_down')}
    del _L0_ffn_all
    return {'x': x, 'ctx_1024': ctx_1024, 'mask_1x1xSxS2_ik0': mask_1x1xSxS2_ik0, 'L0_attn_Wq': _L0_attn_in['Wq'], 'L0_attn_bq': _L0_attn_in['bq'], 'L0_attn_Wk': _L0_attn_in['Wk'], 'L0_attn_bk': _L0_attn_in['bk'], 'L0_attn_Wv': _L0_attn_in['Wv'], 'L0_attn_bv': _L0_attn_in['bv'], 'L0_attn_Wo': _L0_attn_in['Wo'], 'L0_attn_bo': _L0_attn_in['bo'], 'L0_attn_rel_k_emb': _L0_attn_in['rel_k_emb'], 'L0_attn_rel_v_emb': _L0_attn_in['rel_v_emb'], 'L0_xattn_Wq': _L0_xattn_in['Wq'], 'L0_xattn_bq': _L0_xattn_in['bq'], 'L0_xattn_Wk': _L0_xattn_in['Wk'], 'L0_xattn_bk': _L0_xattn_in['bk'], 'L0_xattn_Wv': _L0_xattn_in['Wv'], 'L0_xattn_bv': _L0_xattn_in['bv'], 'L0_xattn_Wo': _L0_xattn_in['Wo'], 'L0_xattn_bo': _L0_xattn_in['bo'], 'L0_ffn_gate_w': _L0_ffn_in['gate_w'], 'L0_ffn_gate_bias': _L0_ffn_in['gate_bias'], 'L0_ffn_w_gate': _L0_ffn_in['w_gate'], 'L0_ffn_w_up': _L0_ffn_in['w_up'], 'L0_ffn_w_down': _L0_ffn_in['w_down']}

def reference(x, ctx_1024, mask_1x1xSxS2_ik0, L0_attn_Wq, L0_attn_bq, L0_attn_Wk, L0_attn_bk, L0_attn_Wv, L0_attn_bv, L0_attn_Wo, L0_attn_bo, L0_attn_rel_k_emb, L0_attn_rel_v_emb, L0_xattn_Wq, L0_xattn_bq, L0_xattn_Wk, L0_xattn_bk, L0_xattn_Wv, L0_xattn_bv, L0_xattn_Wo, L0_xattn_bo, L0_ffn_gate_w, L0_ffn_gate_bias, L0_ffn_w_gate, L0_ffn_w_up, L0_ffn_w_down):
    import jax
    import jax.numpy as jnp

    def _L0_attn_ref(hidden_states, Wq, bq, Wk, bk, Wv, bv, Wo, bo, rel_k_emb, rel_v_emb):
        import jax, jax.numpy as jnp
        import numpy as np
        NUM_HEADS = 16
        MAX_REL = 128

        def _rel_embeds(table, q_len, k_len):
            dist = jnp.arange(q_len)[:, None] - jnp.arange(k_len)[None, :]
            idx = jnp.clip(dist, -MAX_REL, MAX_REL) + MAX_REL
            return table[idx]
        B, T, E = hidden_states.shape
        H = NUM_HEADS
        D = E // H
        scaling = jnp.sqrt(jnp.asarray(D, hidden_states.dtype))
        q = hidden_states @ Wq.T + bq
        k = hidden_states @ Wk.T + bk
        v = hidden_states @ Wv.T + bv
        qh = q.reshape(B, T, H, D).transpose(0, 2, 1, 3)
        kh = k.reshape(B, T, H, D).transpose(0, 2, 1, 3)
        vh = v.reshape(B, T, H, D).transpose(0, 2, 1, 3)
        score1 = jnp.einsum('bhqd,bhkd->bhqk', qh, kh)
        rel_k = _rel_embeds(rel_k_emb, T, T)
        s2 = jnp.einsum('bhqd,qkd->qbhk', qh, rel_k)
        s2 = s2.reshape(T, H, B, T).transpose(2, 1, 0, 3)
        scores = (score1 + s2) / scaling
        attn = jax.nn.softmax(scores, axis=-1)
        w1 = jnp.einsum('bhqk,bhkd->bhqd', attn, vh)
        rel_v = _rel_embeds(rel_v_emb, T, T)
        se = attn.reshape(B * H, T, T).transpose(1, 0, 2)
        w2 = jnp.einsum('qnk,qkd->qnd', se, rel_v)
        w2 = w2.reshape(T, H, B, D).transpose(2, 1, 0, 3)
        out = (w1 + w2).transpose(0, 2, 1, 3).reshape(B, T, E)
        return out @ Wo.T + bo

    def _L0_xattn_ref(q, k, v, mask, Wq, bq, Wk, bk, Wv, bv, Wo, bo):
        import jax, jax.numpy as jnp
        import numpy as np
        B, S, D, H = (2, 512, 256, 16)
        DK = D // H
        b, s, _ = q.shape
        qh = (q @ Wq.T + bq).reshape(b, s, H, DK).transpose(0, 2, 1, 3)
        kh = (k @ Wk.T + bk).reshape(b, -1, H, DK).transpose(0, 2, 1, 3)
        vh = (v @ Wv.T + bv).reshape(b, -1, H, DK).transpose(0, 2, 1, 3)
        scores = jnp.einsum('bhqd,bhkd->bhqk', qh, kh) / np.sqrt(DK)
        scores = jnp.where(mask == 0, jnp.float32(-1000000000.0), scores)
        attn = jax.nn.softmax(scores, axis=-1)
        x = jnp.einsum('bhqk,bhkd->bhqd', attn, vh)
        x = x.transpose(0, 2, 1, 3).reshape(b, s, H * DK)
        return x @ Wo.T + bo

    def _L0_ffn_ref(hidden_states, gate_w, gate_bias, w_gate, w_up, w_down):
        import jax, jax.numpy as jnp
        import numpy as np
        B, S, H, I = (2, 512, 256, 128)
        E, K, G, TG = (64, 8, 8, 4)
        SCALE = 2.5
        CAP = 256
        b, s, h = hidden_states.shape
        x = hidden_states.reshape(-1, h)
        n = x.shape[0]
        logits = x.astype(jnp.float32) @ gate_w.astype(jnp.float32).T
        scores = jax.nn.sigmoid(logits)
        sfc = scores + gate_bias[None, :]
        group_scores = jax.lax.top_k(sfc.reshape(n, G, E // G), 2)[0].sum(-1)
        gidx = jax.lax.top_k(group_scores, TG)[1]
        gmask = jnp.zeros((n, G), bool).at[jnp.arange(n)[:, None], gidx].set(True)
        smask = jnp.repeat(gmask, E // G, axis=1)
        tmp = jnp.where(smask, sfc, -jnp.inf)
        topk_idx = jax.lax.top_k(tmp, K)[1]
        topk_w = jnp.take_along_axis(scores, topk_idx, axis=1)
        topk_w = topk_w / (topk_w.sum(-1, keepdims=True) + 1e-20)
        topk_w = topk_w * SCALE
        e = topk_idx.reshape(-1)
        token = jnp.repeat(jnp.arange(n), K)
        oh = jax.nn.one_hot(e, E, dtype=jnp.int32)
        pos = jnp.take_along_axis(jnp.cumsum(oh, 0) - 1, e[:, None], 1)[:, 0]
        valid = pos < CAP
        pos_c = jnp.where(valid, pos, CAP)
        buf = jnp.zeros((E, CAP + 1, h), x.dtype).at[e, pos_c].set(x[token])[:, :CAP]
        g = jnp.einsum('ech,ehi->eci', buf, w_gate)
        u = jnp.einsum('ech,ehi->eci', buf, w_up)
        y = jnp.einsum('eci,eih->ech', jax.nn.silu(g) * u, w_down)
        y_slots = y[e, jnp.minimum(pos, CAP - 1)]
        w_slot = topk_w.reshape(-1) * valid.astype(topk_w.dtype)
        out = jnp.zeros((n, h), jnp.float32).at[token].add(y_slots * w_slot[:, None])
        return out.reshape(b, s, h)
    x = _layernorm(x + _L0_attn_ref(x, L0_attn_Wq, L0_attn_bq, L0_attn_Wk, L0_attn_bk, L0_attn_Wv, L0_attn_bv, L0_attn_Wo, L0_attn_bo, L0_attn_rel_k_emb, L0_attn_rel_v_emb), axis=-1)
    x = _layernorm(x + _L0_xattn_ref(x, ctx_1024, ctx_1024, mask_1x1xSxS2_ik0, L0_xattn_Wq, L0_xattn_bq, L0_xattn_Wk, L0_xattn_bk, L0_xattn_Wv, L0_xattn_bv, L0_xattn_Wo, L0_xattn_bo), axis=-1)
    x = _layernorm(x + _L0_ffn_ref(x, L0_ffn_gate_w, L0_ffn_gate_bias, L0_ffn_w_gate, L0_ffn_w_up, L0_ffn_w_down), axis=-1)
    return x

_drawn_inputs = setup_inputs


def setup_inputs(seed=0):
    import zlib

    import numpy as np

    out = dict(_drawn_inputs(seed))
    spreads = {}
    factors = {'L0_attn_Wq': 5.675,
     'L0_attn_bq': 8.0,
     'L0_attn_Wk': 5.67,
     'L0_attn_bk': 8.0,
     'L0_attn_rel_k_emb': 8.0,
     'L0_attn_rel_v_emb': 2.675,
     'L0_xattn_bk': 8.0}
    for name, (base, spread) in spreads.items():
        noise = np.random.default_rng([zlib.crc32(name.encode()), seed]).standard_normal(out[name].shape)
        drawn = base * np.exp(spread * noise) if base else spread * noise
        out[name] = jnp.asarray(drawn.astype(out[name].dtype))
    for name, factor in factors.items():
        out[name] = (out[name] * factor).astype(out[name].dtype)
    return out
```

```python
from contextlib import ExitStack

import numpy as np

import concourse.bass as bass
from concourse import mybir
from concourse.alu_op_type import AluOpType as ALU

ACT = mybir.ActivationFunctionType
F32 = mybir.dt.float32
I32 = mybir.dt.int32
U32 = mybir.dt.uint32
AX_X = mybir.AxisListType.X

P = 128
B, S, E = 16, 512, 256
H, D = 16, 16
MAXREL = 128
HALVES = E // P
QG = P // H
NG = S // QG
KT = S // P
TKW = 2 * S - QG
TVZ = 2 * S - P
SC = D ** -0.5
QT = S // P
SK = 64
TOK = B * S
NT = TOK // P
NX = 64
GE = 8
TOP_GROUPS = 4
CAP = 256
SLOT_A = SLOT_B = 16
SLOT_BITS = 4
ROUTE_SCALE = 2.5
NEG = -1e9
FAR = 1e30
TAKEN = -3e38
UNCHOSEN = 65536.0
EPS = 1e-5
OW = P + E + 1


def self_attention(nc, d, qs, attn, rel):
    with ExitStack() as ctx:
        def sb(name, shape, dt=F32):
            return ctx.enter_context(nc.sbuf_tensor(name, shape, dt))

        def ps(name, shape):
            return ctx.enter_context(nc.psum_tensor(name, shape, F32))

        def sem(name):
            return ctx.enter_context(nc.semaphore(name))

        wk = sb("wk", [P, HALVES, E])
        wv = sb("wv", [P, HALVES, E])
        bk = sb("bk", [P, HALVES])
        bvrow = sb("bvrow", [1, E])
        ones = sb("ones", [1, P])
        head_mask = sb("head_mask", [P, HALVES, H])
        query_mask = sb("query_mask", [P, QG])
        out_mask = sb("out_mask", [P, P + E])
        ident = sb("ident", [P, P])
        relk = sb("relk", [P, TKW])
        relv = sb("relv", [P, TVZ * D])

        xT = sb("xT", [P, HALVES, S])
        kT = sb("kT", [P, HALVES, S])
        qT = sb("qT", [P, HALVES, S])
        qrep = sb("qrep", [P, 2 * H, S])
        v1 = sb("v1", [P, KT, E + 1])
        qdiag = [sb(f"qdiag{i}", [P, 3, QG, H]) for i in range(2)]
        negmax = [sb(f"negmax{i}", [P, 1]) for i in range(2)]
        probs = [sb(f"probs{i}", [P, S]) for i in range(2)]
        probsT = [sb(f"probsT{i}", [P, KT, P]) for i in range(2)]
        picked = [sb(f"picked{i}", [P, P + E]) for i in range(2)]
        sum_inv = sb("sum_inv", [P, NG])
        value_out = sb("value_out", [P, NG, D])
        rel_out = sb("rel_out", [P, NG, D])

        psP = [ps(f"psP{i}", [P, S]) for i in range(2)]
        psS = [ps(f"psS{i}", [P, S]) for i in range(2)]
        psT = [ps(f"psT{i}", [P, KT, P]) for i in range(2)]
        psO = [ps(f"psO{i}", [P, S]) for i in range(2)]

        consts_in = sem("consts_in")
        q_in = sem("q_in")
        qrep_in = sem("qrep_in")
        x_in = sem("x_in")
        projected = sem("projected")
        kept_dve = sem("kept_dve")
        kept_act = sem("kept_act")
        ones_set = sem("ones_set")
        qdiag_ready = sem("qdiag_ready")
        scores_ready = sem("scores_ready")
        max_ready = sem("max_ready")
        probs_ready = sem("probs_ready")
        transposed = sem("transposed")
        probsT_ready = sem("probsT_ready")
        out_ready = sem("out_ready")
        out_read = sem("out_read")
        picked_ready = sem("picked_ready")
        reduced = sem("reduced")
        normed = sem("normed")
        out_free = sem("out_free")
        stored = sem("stored")

        loads = [
            (wk, d["a_wkT"].rearrange("(a p) o -> p a o", p=P)),
            (bk, d["a_bk"]), (bvrow, d["a_bv"]),
            (wv, d["a_wvT"].rearrange("(a p) o -> p a o", p=P)),
            (head_mask, d["head_mask"]), (query_mask, d["query_mask"]),
            (out_mask, d["out_mask"]), (ident, d["ident"]),
            (relk, d["relk"]), (relv, d["relv"]),
        ]
        N_CONST = 16 * len(loads)
        steps = [("k", 0), ("k", 1)] + [("v", t) for t in range(KT)]
        HALF = len(steps) // 2

        def window(kind, n):
            return kT[:, n, :] if kind == "k" else v1[:, n, 0:E]

        block = ctx.enter_context(nc.Block())

        @block.sync
        def _(sp):
            for dst, src in loads:
                sp.dma_start(dst[:], src).then_inc(consts_in, 16)
            x_in_dram = d["a_xT"].rearrange("b (a p) s -> p (b a) s", p=P)
            q_dram = qs.rearrange("b (a p) s -> p (b a) s", p=P)
            sp.sem_inc(out_free, 1)

            def load_x(b):
                sp.dma_start(xT[:], x_in_dram[:, bass.ds(b * HALVES, HALVES), :]).then_inc(x_in, 16)

            def load_q(b):
                sp.dma_start(qT[:], q_dram[:, bass.ds(b * HALVES, HALVES), :]).then_inc(q_in, 16)

            def load_qrep(b, slot):
                head = qs[:, bass.ds(b * D, D), :].rearrange("h e s -> e h s")
                for j in range(QG):
                    sp.dma_start(qrep[j * D:(j + 1) * D, bass.ds(slot * H, H), :], head).then_inc(qrep_in, 16)

            def store(b):
                sp.wait_ge(normed, b + 1)
                out = attn[bass.ds(b, 1), :, :].rearrange("b (g r) c -> (b r c) g", g=NG)
                sp.dma_start(out.rearrange("(p e) g -> p g e", p=P), value_out[:]).then_inc(stored, 16)
                for j in range(QG):
                    out = rel[:, j::QG, bass.ds(b * D, D)]
                    sp.dma_start(out, rel_out[j * H:(j + 1) * H, :, :]).then_inc(stored, 16)
                sp.wait_ge(stored, (1 + QG) * 16 * (b + 1))
                sp.sem_inc(out_free, 1)

            load_x(0)
            load_q(0)
            load_qrep(0, 0)
            with sp.Fori(0, B - 1) as b:
                sp.wait_ge(qdiag_ready, b * NG + 1)
                load_qrep(b + 1, (b + 1) % 2)
                sp.wait_ge(projected, (b + 1) * len(steps))
                load_x(b + 1)
                sp.wait_ge(qdiag_ready, (b + 1) * NG)
                load_q(b + 1)
                store(b)
            store(B - 1)

        @block.gpsimd
        def _(pool):
            pool.memset(v1[:, :, E:E + 1], 1.0).then_inc(ones_set, 1)
            pool.memset(ones[:], 1.0).then_inc(ones_set, 1)
            pool.wait_ge(consts_in, N_CONST)

            def build(i, g, n, first, slot):
                if not first:
                    pool.wait_ge(scores_ready, g - 1)
                q0 = i * QG
                for a in range(HALVES):
                    nc.gpsimd.tensor_tensor(
                        qdiag[n][:, a, :, :],
                        qT[:, a, bass.ds(q0, QG)].unsqueeze(2).to_broadcast([P, QG, H]),
                        head_mask[:, a, :].unsqueeze(1).to_broadcast([P, QG, H]), ALU.mult)
                nc.gpsimd.tensor_tensor(
                    qdiag[n][:, 2, :, :],
                    qrep[:, bass.ds(slot * H, H), bass.ds(q0, QG)].rearrange("p h j -> p j h"),
                    query_mask[:, :].unsqueeze(2).to_broadcast([P, QG, H]), ALU.mult).then_inc(qdiag_ready, 1)

            with pool.Fori(0, B) as b:
                slot = b % 2
                pool.wait_ge(q_in, b * 16 + 16)
                pool.wait_ge(qrep_in, (b + 1) * 16 * QG)
                pool.wait_ge(projected, (b + 1) * len(steps))
                build(0, None, 0, True, slot)
                build(1, None, 1, True, slot)
                with pool.Fori(1, NG // 2) as t:
                    build(t * 2, b * NG + t * 2, 0, False, slot)
                    build(t * 2 + 1, b * NG + t * 2 + 1, 1, False, slot)

        @block.tensor
        def _(pe):
            pe.wait_ge(consts_in, N_CONST)
            pe.wait_ge(ones_set, 2)

            def project(b):
                pe.wait_ge(x_in, b * 16 + 16)
                for n, (kind, m) in enumerate(steps):
                    if n >= 2:
                        pe.wait_ge(kept_act if n % 2 else kept_dve, b * HALF + n // 2)
                    dst = psP[n % 2]
                    for a in range(HALVES):
                        if kind == "v":
                            nc.tensor.matmul(dst[:, 0:E], xT[:, a, m * P:(m + 1) * P], wv[:, a, :],
                                             start=a == 0, stop=False)
                        else:
                            mm = nc.tensor.matmul(dst[:], wk[:, a, m * P:(m + 1) * P], xT[:, a, :], start=a == 0, stop=a == HALVES - 1)
                    if kind == "v":
                        mm = nc.tensor.matmul(dst[:, 0:E], ones[:], bvrow[:], start=False, stop=True)
                    mm.then_inc(projected, 1)

            def scores(i, g, n, first=False):
                pe.wait_ge(qdiag_ready, g + 1)
                if not first:
                    pe.wait_ge(probs_ready, g - 1)
                nc.tensor.matmul(psS[n][:], qdiag[n][:, 0, :, :].rearrange("p j h -> p (j h)"), kT[:, 0, :], start=True, stop=False)
                nc.tensor.matmul(psS[n][:], qdiag[n][:, 1, :, :].rearrange("p j h -> p (j h)"), kT[:, 1, :], start=False, stop=False)
                nc.tensor.matmul(psS[n][:], qdiag[n][:, 2, :, :].rearrange("p j h -> p (j h)"),
                                 relk[:, bass.ds(S - QG - i * QG, S)], start=False, stop=True).then_inc(scores_ready, 1)

            def transpose(g, n):
                pe.wait_ge(probs_ready, g + 1)
                for t in range(KT):
                    mm = nc.tensor.transpose(psT[n][:, t, :], probs[n][:, t * P:(t + 1) * P], ident[:])
                mm.then_inc(transposed, 1)

            def outputs(i, g, n, first=False):
                pe.wait_ge(probsT_ready, g + 1)
                if not first:
                    pe.wait_ge(out_read, g - 1)
                for t in range(KT):
                    nc.tensor.matmul(psO[n][:, P:OW], probsT[n][:, t, :], v1[:, t, :], start=t == 0, stop=t == KT - 1)
                for t in range(KT):
                    mm = nc.tensor.matmul(psO[n][:, 0:P], probsT[n][:, t, :],
                                          relv[:, bass.ds((i * QG + (KT - 1 - t) * P) * D, P)],
                                          start=t == 0, stop=t == KT - 1)
                mm.then_inc(out_ready, 1)

            with pe.Fori(0, B) as b:
                project(b)
                g = b * NG
                pe.wait_ge(kept_dve, b * HALF + HALF)
                pe.wait_ge(kept_act, b * HALF + HALF)
                scores(0, g, 0, first=True)
                scores(1, g + 1, 1, first=True)
                transpose(g, 0)
                scores(2, g + 2, 0)
                transpose(g + 1, 1)
                outputs(0, g, 0, first=True)
                scores(3, g + 3, 1)
                transpose(g + 2, 0)
                outputs(1, g + 1, 1, first=True)
                with pe.Fori(2, NG // 2) as t:
                    scores(t * 2, g + t * 2, 0)
                    transpose(g + t * 2 - 1, 1)
                    outputs(t * 2 - 2, g + t * 2 - 2, 0)
                    scores(t * 2 + 1, g + t * 2 + 1, 1)
                    transpose(g + t * 2, 0)
                    outputs(t * 2 - 1, g + t * 2 - 1, 1)
                transpose(g + NG - 1, 1)
                outputs(NG - 2, g + NG - 2, 0)
                outputs(NG - 1, g + NG - 1, 1)

        @block.scalar
        def _(act):
            act.wait_ge(consts_in, N_CONST)

            def exp(g, n):
                act.wait_ge(max_ready, g + 1)
                nc.scalar.activation(probs[n][:], psS[n][:], ACT.Exp, bias=negmax[n][:]).then_inc(probs_ready, 1)

            def keep(g, n, first=False):
                act.wait_ge(transposed, g + 1)
                if not first:
                    act.wait_ge(out_ready, g - 1)
                nc.scalar.activation(probsT[n][:], psT[n][:], ACT.Copy).then_inc(probsT_ready, 1)

            with act.Fori(0, B) as b:
                for n, (kind, m) in enumerate(steps):
                    if n % 2 == 0:
                        continue
                    act.wait_ge(projected, b * len(steps) + n + 1)
                    if kind == "v":
                        mm = nc.scalar.activation(window(kind, m), psP[1][:, 0:E], ACT.Copy)
                    else:
                        mm = nc.scalar.activation(window(kind, m), psP[1][:], ACT.Identity, bias=bk[:, m:m + 1])
                    mm.then_inc(kept_act, 1)
                g = b * NG
                exp(g, 0)
                exp(g + 1, 1)
                keep(g, 0, first=True)
                exp(g + 2, 0)
                keep(g + 1, 1, first=True)
                exp(g + 3, 1)
                keep(g + 2, 0)
                with act.Fori(2, NG // 2) as t:
                    exp(g + t * 2, 0)
                    keep(g + t * 2 - 1, 1)
                    exp(g + t * 2 + 1, 1)
                    keep(g + t * 2, 0)
                keep(g + NG - 1, 1)

        @block.vector
        def _(dve):
            dve.wait_ge(consts_in, N_CONST)

            def rowmax(g, n):
                dve.wait_ge(scores_ready, g + 1)
                nc.vector.tensor_reduce(negmax[n][:], psS[n][:], AX_X, ALU.max, negate=True).then_inc(max_ready, 1)

            def pick(i, g, n):
                dve.wait_ge(out_ready, g + 1)
                nc.vector.reciprocal(sum_inv[:, bass.ds(i, 1)], psO[n][:, P + E:OW])
                nc.vector.tensor_tensor(picked[n][:], psO[n][:, 0:P + E], out_mask[:], ALU.mult).then_inc(out_read, 1)
                dve.wait_ge(out_read, g + 1)
                for dst, c0, c1 in ((rel_out, 0, P), (value_out, P, P + E)):
                    mm = nc.vector.tensor_reduce(dst[:, bass.ds(i, 1), :].rearrange("p g e -> p (g e)"),
                                                 picked[n][:, c0:c1].rearrange("p (c e) -> p e c", e=D), AX_X, ALU.add)
                mm.then_inc(reduced, 1)

            with dve.Fori(0, B) as b:
                for n, (kind, m) in enumerate(steps):
                    if n % 2:
                        continue
                    dve.wait_ge(projected, b * len(steps) + n + 1)
                    if kind == "v":
                        mm = nc.vector.tensor_copy(window(kind, m), psP[0][:, 0:E])
                    else:
                        mm = nc.vector.tensor_scalar(window(kind, m), psP[0][:], bk[:, m:m + 1], None, ALU.add)
                    mm.then_inc(kept_dve, 1)
                g = b * NG
                dve.wait_ge(out_free, b + 1)
                rowmax(g, 0)
                rowmax(g + 1, 1)
                with dve.Fori(1, NG // 2) as t:
                    rowmax(g + t * 2, 0)
                    pick(t * 2 - 2, g + t * 2 - 2, 0)
                    rowmax(g + t * 2 + 1, 1)
                    pick(t * 2 - 1, g + t * 2 - 1, 1)
                pick(NG - 2, g + NG - 2, 0)
                pick(NG - 1, g + NG - 1, 1)
                dve.wait_ge(reduced, g + NG)
                for dst in (value_out, rel_out):
                    mm = nc.vector.tensor_tensor(dst[:], dst[:], sum_inv[:].unsqueeze(2).to_broadcast([P, NG, D]), ALU.mult)
                mm.then_inc(normed, 1)


def project_queries(nc, d, qs):
    with ExitStack() as ctx:
        wq = ctx.enter_context(nc.sbuf_tensor("wq", [P, HALVES, E], F32))
        bq = ctx.enter_context(nc.sbuf_tensor("bq", [P, HALVES], F32))
        xT = [ctx.enter_context(nc.sbuf_tensor(f"xTq{i}", [P, HALVES, S], F32)) for i in range(2)]
        q = [ctx.enter_context(nc.sbuf_tensor(f"q{i}", [P, HALVES, S], F32)) for i in range(2)]
        psQ = [ctx.enter_context(nc.psum_tensor(f"psQ{i}", [P, HALVES, S], F32)) for i in range(2)]
        w_in, projected, kept = (ctx.enter_context(nc.semaphore(n)) for n in ("wq_in", "q_projected", "q_kept"))
        x_in = [ctx.enter_context(nc.semaphore(f"xq_in{i}")) for i in range(2)]
        stored = [ctx.enter_context(nc.semaphore(f"q_stored{i}")) for i in range(2)]
        block = ctx.enter_context(nc.Block())

        @block.sync
        def _(sp):
            sp.dma_start(wq[:], d["a_wqT"].rearrange("(a p) o -> p a o", p=P)).then_inc(w_in, 16)
            sp.dma_start(bq[:], d["a_bq"]).then_inc(w_in, 16)
            for b in range(B):
                if b >= 2:
                    sp.wait_ge(projected, b - 1)
                sp.dma_start(xT[b % 2][:], d["a_xT"][b].rearrange("(a p) s -> p a s", p=P)).then_inc(x_in[b % 2], 16)

        @block.tensor
        def _(pe):
            pe.wait_ge(w_in, 32)
            for b in range(B):
                pe.wait_ge(x_in[b % 2], 16 * (b // 2 + 1))
                if b >= 2:
                    pe.wait_ge(kept, b - 1)
                for m in range(HALVES):
                    for a in range(HALVES):
                        mm = nc.tensor.matmul(psQ[b % 2][:, m, :], wq[:, a, m * P:(m + 1) * P], xT[b % 2][:, a, :],
                                              start=a == 0, stop=a == HALVES - 1)
                mm.then_inc(projected, 1)

        @block.vector
        def _(dve):
            dve.wait_ge(w_in, 32)
            for b in range(B):
                dve.wait_ge(projected, b + 1)
                if b >= 2:
                    dve.wait_ge(stored[b % 2], 16 * (b // 2))
                for m in range(HALVES):
                    mm = nc.vector.tensor_scalar(q[b % 2][:, m, :], psQ[b % 2][:, m, :], bq[:, m:m + 1], SC, ALU.add, ALU.mult)
                mm.then_inc(kept, 1)

        @block.scalar
        def _(act):
            for b in range(B):
                act.wait_ge(kept, b + 1)
                act.dma_start(qs[b].rearrange("(a p) s -> p a s", p=P), q[b % 2][:]).then_inc(stored[b % 2], 16)
            for i in range(2):
                act.wait_ge(stored[i], 16 * B // 2)


class Chain:

    def __init__(self, engine, sem, per_turn, turn):
        self.engine, self.sem, self.per_turn, self.turn, self.n = engine, sem, per_turn, turn, 0

    def link(self, instruction):
        self.n += 1
        instruction.then_inc(self.sem, 1)
        self.engine.wait_ge(self.sem, self.turn * self.per_turn + self.n)

    def link_alone(self, instruction):
        self.link(instruction)
        self.n += 1
        self.engine.sem_inc(self.sem, 1)

    def end(self):
        assert self.n == self.per_turn, (self.n, self.per_turn)


def layer_norm(nc, chain, turn, r, out, stats, moments, rstd, moments_ready, deviation_ready):
    for t in range(QT):
        last = nc.vector.bn_stats(stats[:, t, :], r[:, t, :])
    chain.link_alone(last)
    for t in range(QT):
        last = nc.vector.bn_aggr(moments[:, t, :], stats[:, t, :])
    last.then_inc(moments_ready, 1)
    chain.engine.wait_ge(deviation_ready, turn + 1)
    chain.link(nc.vector.reciprocal(rstd[:], rstd[:]))
    for t in range(QT):
        last = nc.vector.tensor_scalar(out[:, t, :], r[:, t, :], moments[:, t, 0:1], rstd[:, t:t + 1],
                                       ALU.subtract, ALU.mult)
    chain.link(last)


def deviation(nc, act, turn, moments, rstd, eps, moments_ready, deviation_ready):
    act.wait_ge(moments_ready, turn + 1)
    nc.scalar.activation(rstd[:], moments[:, :, 1], ACT.Sqrt, bias=eps[:]).then_inc(deviation_ready, 1)


def cross_attention(nc, d, attn, rel, x2_rows, acc_rows, gate_scores):
    with ExitStack() as ctx:
        def sb(name, shape, dt=F32):
            return ctx.enter_context(nc.sbuf_tensor("x_" + name, shape, dt))

        def ps(name, shape):
            return ctx.enter_context(nc.psum_tensor("x_" + name, shape, F32))

        def sem(name):
            return ctx.enter_context(nc.semaphore("x_" + name))

        PAIRS = H // 2
        HH = H // HALVES
        wo, wq, wk, wv, wo2 = (sb(n, [P, HALVES, E]) for n in ("wo", "wq", "wk", "wv", "wo2"))
        wg = sb("wg", [P, HALVES, NX])
        bo, bo2, bv, ones = (sb(n, [1, w]) for n, w in (("bo", E), ("bo2", E), ("bv", E), ("ones", P)))
        bq, bqs, bk = (sb(n, [P, HALVES]) for n in ("bq", "bqs", "bk"))
        ident = sb("ident", [P, P])
        half_mask = sb("half_mask", [P, HH])
        pair_mask = sb("pair_mask", [P, 2 * D])
        mask_in = sb("mask_in", [P, QT, SK], I32)
        keep = sb("keep", [P, QT, SK])
        fill = sb("fill", [P, QT, SK])
        ctxT = sb("ctxT", [P, HALVES, B, 2, SK])
        kT = sb("kT", [P, HALVES, B, SK])
        v = sb("v", [P, B, E])
        kdiag = sb("kdiag", [P, HALVES, HH, SK])
        vdiag = sb("vdiag", [P, PAIRS, 2 * D])
        x_sb, attn_sb, rel_sb = (sb(n, [P, QT, E]) for n in ("x_sb", "attn_sb", "rel_sb"))
        both = sb("both", [P, QT, E])
        r, x1, x2, o = (sb(n, [P, QT, E]) for n in ("r", "x1", "x2", "o"))
        aT, x1T, qT, oT, x2T = (sb(n, [P, HALVES, S]) for n in ("aT", "x1T", "qT", "oT", "x2T"))
        sc = [sb(f"sc{i}", [P, H, SK]) for i in range(2)]
        pr = [sb(f"pr{i}", [P, H, SK]) for i in range(2)]
        prT = [sb(f"prT{i}", [P, PAIRS, P]) for i in range(QT)]
        negmax, total, inv = (sb(n, [P, QT, H]) for n in ("negmax", "total", "inv"))
        stats = sb("stats", [P, QT, 6])
        moments = sb("moments", [P, QT, 2])
        rstd = sb("rstd", [P, QT])
        eneg = sb("eneg", [P, QT, NX])
        eps = sb("eps", [P, 1])
        zeros = sb("zeros", [P, QT, E])

        bankT = [ps(f"bankT{i}", [P, 4, P]) for i in range(2)]
        bankR = [ps(f"bankR{i}", [P, 2, E]) for i in range(2)]
        bankS = [ps(f"bankS{i}", [P, H, SK]) for i in range(2)]

        w_in = sem("w_in")
        ctx_in = sem("ctx_in")
        zeros_ready = sem("zeros_ready")
        ones_ready = sem("ones_ready")
        mask_ready = sem("mask_ready")
        eps_ready = sem("eps_ready")
        ctx_projected = sem("ctx_projected")
        ctx_kept = sem("ctx_kept")
        attn_in = sem("attn_in")
        x_in = sem("x_in")
        both_ready = sem("both_ready")
        bankT_full = sem("bankT_full")
        bankT_empty = [sem(f"bankT_empty{i}") for i in range(2)]
        bankR_full = sem("bankR_full")
        bankR_empty = [sem(f"bankR_empty{i}") for i in range(2)]
        bankS_full = sem("bankS_full")
        bankS_empty = sem("bankS_empty")
        diag_ready = sem("diag_ready")
        filled = sem("filled")
        max_ready = sem("max_ready")
        shifted = sem("shifted")
        exp_ready = sem("exp_ready")
        x1_ready = sem("x1_ready")
        x2_ready = sem("x2_ready")
        x2_free = sem("x2_free")
        o_ready = sem("o_ready")
        eneg_ready = sem("eneg_ready")
        stored = sem("stored")
        zero_stored = sem("zero_stored")
        dve_step = sem("dve_step")
        moments_ready = sem("moments_ready")
        deviation_ready = sem("deviation_ready")

        weights = [
            (ident, d["ident"]), (wo, d["a_woT"].rearrange("(a p) o -> p a o", p=P)), (bo, d["a_bo"]),
            (wk, d["x_wkT"].rearrange("(a p) o -> p a o", p=P)), (bk, d["x_bk"]),
            (wv, d["x_wvT"].rearrange("(a p) o -> p a o", p=P)), (bv, d["x_bv"]),
            (wq, d["x_wqT"].rearrange("(a p) o -> p a o", p=P)), (bq, d["x_bq"]),
            (wo2, d["x_woT"].rearrange("(a p) o -> p a o", p=P)), (bo2, d["x_bo"]),
            (wg, d["gate_wT"].rearrange("(a p) o -> p a o", p=P)),
            (half_mask, d["half_mask"]), (pair_mask, d["pair_mask"]),
            (mask_in, d["mask"].rearrange("(t p) k -> p t k", p=P)),
        ]
        N_W = 16 * len(weights)
        T_USES = 2 * (5 + QT)
        R_USES = 2 * 4
        KCOLS = B * SK // 512

        def rows(dram, b):
            return dram[bass.ds(b * S, S), :].rearrange("(t p) e -> p t e", p=P)

        block = ctx.enter_context(nc.Block())

        @block.sync
        def _(sp):
            for dst, src in weights:
                sp.dma_start(dst[:], src).then_inc(w_in, 16)
            for a in range(HALVES):
                sp.dma_start(ctxT[:, a], d["ctxT"][a * P:(a + 1) * P]).then_inc(ctx_in, 16)
            sp.sem_inc(x2_free, 1)
            sp.wait_ge(zeros_ready, 1)
            for dram in (x2_rows, *acc_rows):
                sp.dma_start(dram[TOK:TOK + CAP, :].rearrange("(t p) e -> p t e", p=P), zeros[:, 0:CAP // P, :])\
                    .then_inc(zero_stored, 16)

            def load_attn(b):
                sp.dma_start(attn_sb[:], rows(attn, b)).then_inc(attn_in, 16)
                sp.dma_start(rel_sb[:], rows(rel, b)).then_inc(attn_in, 16)

            def load_x(b):
                sp.dma_start(x_sb[:], rows(d["x"], b)).then_inc(x_in, 16)

            def store(b):
                sp.wait_ge(x2_ready, b + 1)
                for dram in (x2_rows, acc_rows[0]):
                    sp.dma_start(rows(dram, b), x2[:]).then_inc(stored, 16)
                sp.dma_start(rows(acc_rows[1], b), zeros[:]).then_inc(stored, 16)
                sp.wait_ge(stored, (b + 1) * 48)
                sp.sem_inc(x2_free, 1)

            load_attn(0)
            load_x(0)
            with sp.Fori(0, B - 1) as b:
                sp.wait_ge(both_ready, b + 1)
                load_attn(b + 1)
                sp.wait_ge(x1_ready, b + 1)
                load_x(b + 1)
                store(b)
            store(B - 1)
            sp.wait_ge(zero_stored, 48)

        @block.gpsimd
        def _(pool):
            pool.memset(zeros[:], 0.0).then_inc(zeros_ready, 1)
            pool.memset(ones[:], 1.0).then_inc(ones_ready, 1)
            pool.memset(eps[:], EPS).then_inc(eps_ready, 1)
            pool.wait_ge(w_in, N_W)
            pool.wait_ge(ctx_kept, HALVES * KCOLS + B // 2)
            pool.wait_ge(mask_ready, 1)

            def diag(b):
                for a in range(HALVES):
                    nc.gpsimd.tensor_tensor(
                        kdiag[:, a, :, :], kT[:, a, bass.ds(b, 1), :].to_broadcast([P, HH, SK]),
                        half_mask[:].unsqueeze(2).to_broadcast([P, HH, SK]), ALU.mult)
                nc.gpsimd.tensor_tensor(
                    vdiag[:], v[:, bass.ds(b, 1), :].rearrange("p b (g c) -> p (b g) c", c=2 * D),
                    pair_mask[:].unsqueeze(1).to_broadcast([P, PAIRS, 2 * D]), ALU.mult).then_inc(diag_ready, 1)

            def tiles(b):
                for t in range(QT):
                    pool.wait_ge(bankS_empty, b * QT + t + 3)
                    nc.gpsimd.tensor_tensor(sc[t % 2][:], sc[t % 2][:], fill[:, t, :].unsqueeze(1).to_broadcast([P, H, SK]),
                                            ALU.add).then_inc(filled, 1)
                    if t % 2:
                        for u in (t - 1, t):
                            pool.wait_ge(max_ready, b * QT + u + 1)
                            nc.gpsimd.tensor_tensor(sc[u % 2][:], sc[u % 2][:],
                                                    negmax[:, u, :].unsqueeze(2).to_broadcast([P, H, SK]),
                                                    ALU.add).then_inc(shifted, 1)

            diag(0)
            with pool.Fori(0, B - 1) as b:
                tiles(b)
                pool.wait_ge(bankR_full, b * R_USES + 4)
                diag(b + 1)
            tiles(B - 1)

        @block.tensor
        def _(pe):
            pe.wait_ge(w_in, N_W)
            pe.wait_ge(ones_ready, 1)
            pe.wait_ge(ctx_in, 16 * HALVES)
            n = 0
            for m in range(HALVES):
                for c in range(KCOLS):
                    if n >= 2:
                        pe.wait_ge(ctx_kept, n - 1)
                    for a in range(HALVES):
                        src = ctxT[:, a, c * (B // KCOLS):(c + 1) * (B // KCOLS), 0, :]
                        mm = nc.tensor.matmul(bankT[n % 2][:].rearrange("p a b -> p (a b)"), wk[:, a, m * P:(m + 1) * P], src,
                                              start=a == 0, stop=a == HALVES - 1)
                    mm.then_inc(ctx_projected, 1)
                    n += 1
            for c in range(B // 2):
                pe.wait_ge(ctx_kept, n - 1)
                for i in range(2):
                    dst = bankT[n % 2][:].rearrange("p a b -> p (a b)")[:, i * E:(i + 1) * E]
                    for a in range(HALVES):
                        nc.tensor.matmul(dst, ctxT[:, a, 2 * c + i].rearrange("p a b -> p (a b)"), wv[:, a, :], start=a == 0, stop=False)
                    mm = nc.tensor.matmul(dst, ones[:], bv[:], start=False, stop=True)
                mm.then_inc(ctx_projected, 1)
                n += 1
            pe.wait_ge(ctx_kept, n)

            with pe.Fori(0, B) as b:
                used = {"T": 0, "R": 0}

                def take(kind):
                    n = used[kind]
                    empty = {"T": bankT_empty, "R": bankR_empty}[kind][n % 2]
                    pe.wait_ge(empty, b * ({"T": T_USES, "R": R_USES}[kind] // 2) + n // 2 + 1)
                    used[kind] += 1
                    return {"T": bankT, "R": bankR}[kind][n % 2]

                def transpose_rows(src):
                    for a in range(HALVES):
                        bank = take("T")
                        for t in range(QT):
                            mm = nc.tensor.transpose(bank[:, t, :], src[:, t, a * P:(a + 1) * P], ident[:])
                        mm.then_inc(bankT_full, 1)

                def wait_bankT():
                    for i in range(2):
                        pe.wait_ge(bankT_empty[i], b * (T_USES // 2) + used["T"] // 2 + 1)

                def project(src, w, bias, cols):
                    for i in range(2):
                        bank = take("R")
                        for u in range(2):
                            t = 2 * i + u
                            for a in range(HALVES):
                                mm = nc.tensor.matmul(bank[:, u, 0:cols], src[:, a, t * P:(t + 1) * P], w[:, a, :],
                                                      start=a == 0, stop=a == HALVES - 1 and bias is None)
                            if bias is not None:
                                mm = nc.tensor.matmul(bank[:, u, 0:cols], ones[:], bias[:], start=False, stop=True)
                        mm.then_inc(bankR_full, 1)

                pe.wait_ge(both_ready, b + 1)
                transpose_rows(both)
                wait_bankT()
                project(aT, wo, bo, E)
                pe.wait_ge(x1_ready, b + 1)
                transpose_rows(x1)
                wait_bankT()
                for m in range(HALVES):
                    bank = take("T")
                    for a in range(HALVES):
                        mm = nc.tensor.matmul(bank[:].rearrange("p a b -> p (a b)"), wq[:, a, m * P:(m + 1) * P], x1T[:, a, :],
                                              start=a == 0, stop=a == HALVES - 1)
                    mm.then_inc(bankT_full, 1)
                wait_bankT()
                pe.wait_ge(diag_ready, b + 1)

                def scores(t):
                    pe.wait_ge(bankS_empty, b * QT + t + 1)
                    for a in range(HALVES):
                        mm = nc.tensor.matmul(bankS[t % 2][:, a * HH:(a + 1) * HH, :].rearrange("p h k -> p (h k)"),
                                              qT[:, a, t * P:(t + 1) * P], kdiag[:, a, :, :].rearrange("p h k -> p (h k)"),
                                              start=True, stop=True)
                    mm.then_inc(bankS_full, 1)

                def transpose_weights(t):
                    pe.wait_ge(exp_ready, b * QT + t + 1)
                    for c in range(2):
                        bank = take("T")
                        for g in range(4):
                            h = 2 * (4 * c + g)
                            mm = nc.tensor.transpose(bank[:, g, :], pr[t % 2][:, h:h + 2, :].rearrange("p h k -> p (h k)"), ident[:])
                        mm.then_inc(bankT_full, 1)

                for t in range(QT):
                    scores(t)
                for t in range(QT):
                    transpose_weights(t)
                wait_bankT()
                for i in range(2):
                    bank = take("R")
                    for u in range(2):
                        for g in range(PAIRS):
                            mm = nc.tensor.matmul(bank[:, u, g * 2 * D:(g + 1) * 2 * D], prT[2 * i + u][:, g, :], vdiag[:, g, :],
                                                  start=True, stop=True)
                    mm.then_inc(bankR_full, 1)
                pe.wait_ge(o_ready, b + 1)
                transpose_rows(o)
                wait_bankT()
                project(oT, wo2, bo2, E)
                pe.wait_ge(x2_ready, b + 1)
                transpose_rows(x2)
                wait_bankT()
                project(x2T, wg, None, NX)
                assert used == {"T": T_USES, "R": R_USES}

        @block.scalar
        def _(act):
            act.sem_inc(bankT_empty[0], 1)
            act.wait_ge(mask_ready, 1)
            act.wait_ge(eps_ready, 1)
            act.wait_ge(w_in, N_W)
            with act.Fori(0, B) as b:
                def full(n):
                    act.wait_ge(bankT_full, b * T_USES + n)

                def keep_half(n, dst):
                    full(n)
                    nc.scalar.activation(dst[:, 0, :], bankT[0][:].rearrange("p a b -> p (a b)"), ACT.Copy).then_inc(bankT_empty[0], 1)

                keep_half(1, aT)
                deviation(nc, act, b * 2, moments, rstd, eps, moments_ready, deviation_ready)
                keep_half(3, x1T)
                full(5)
                nc.scalar.activation(qT[:, 0, :], bankT[0][:].rearrange("p a b -> p (a b)"), ACT.Identity,
                                     bias=bqs[:, 0:1], scale=SC).then_inc(bankT_empty[0], 1)
                n = 6
                for t0 in range(0, QT, 2):
                    for t in (t0, t0 + 1):
                        act.wait_ge(shifted, b * QT + t + 1)
                        nc.scalar.activation(pr[t % 2][:], sc[t % 2][:], ACT.Exp).then_inc(exp_ready, 1)
                    for t in (t0, t0 + 1):
                        for c in range(2):
                            n += 1
                            full(n)
                            nc.scalar.activation(prT[t][:, 4 * c:4 * c + 4, :], bankT[c][:], ACT.Copy).then_inc(bankT_empty[c], 1)
                keep_half(n + 1, oT)
                deviation(nc, act, b * 2 + 1, moments, rstd, eps, moments_ready, deviation_ready)
                keep_half(n + 3, x2T)
                for i in range(2):
                    act.wait_ge(bankR_full, b * R_USES + 7 + i)
                    nc.scalar.activation(eneg[:, 2 * i:2 * i + 2, :], bankR[i][:, :, 0:NX], ACT.Exp, scale=-1.0).then_inc(bankR_empty[i], 1)

        @block.vector
        def _(dve):
            dve.sem_inc(bankT_empty[1], 1)
            dve.sem_inc(bankR_empty[0], 1)
            dve.sem_inc(bankR_empty[1], 1)
            dve.sem_inc(bankS_empty, 2)
            dve.wait_ge(w_in, N_W)
            nc.vector.tensor_scalar(bqs[:], bq[:], SC, None, ALU.mult)
            nc.vector.tensor_scalar(keep[:], mask_in[:], 0, None, ALU.not_equal)
            nc.vector.tensor_scalar(fill[:], mask_in[:], 0, NEG, ALU.is_equal, ALU.mult).then_inc(mask_ready, 1)
            n = 0
            for m in range(HALVES):
                for c in range(KCOLS):
                    n += 1
                    dve.wait_ge(ctx_projected, n)
                    nc.vector.tensor_scalar(
                        kT[:, m, c * (B // KCOLS):(c + 1) * (B // KCOLS), :].rearrange("p b k -> p (b k)"),
                        bankT[(n - 1) % 2][:].rearrange("p a b -> p (a b)"), bk[:, m:m + 1], None, ALU.add).then_inc(ctx_kept, 1)
            for c in range(B // 2):
                n += 1
                dve.wait_ge(ctx_projected, n)
                nc.vector.tensor_copy(v[:, 2 * c:2 * c + 2, :].rearrange("p b e -> p (b e)"),
                                      bankT[(n - 1) % 2][:].rearrange("p a b -> p (a b)")).then_inc(ctx_kept, 1)
            dve.wait_ge(mask_ready, 1)

            with dve.Fori(0, B) as b:
                chain = Chain(dve, dve_step, 12, b)

                def keep_half(n, dst):
                    dve.wait_ge(bankT_full, b * T_USES + n)
                    nc.vector.tensor_copy(dst[:, 1, :], bankT[1][:].rearrange("p a b -> p (a b)")).then_inc(bankT_empty[1], 1)

                def residual(n, x):
                    for i in range(2):
                        dve.wait_ge(bankR_full, b * R_USES + n + i)
                        nc.vector.tensor_tensor(r[:, 2 * i:2 * i + 2, :], bankR[i][:], x[:, 2 * i:2 * i + 2, :], ALU.add)\
                            .then_inc(bankR_empty[i], 1)
                    for i in range(2):
                        dve.wait_ge(bankR_empty[i], b * (R_USES // 2) + (n + 1) // 2 + 1)

                dve.wait_ge(attn_in, b * 32 + 32)
                nc.vector.tensor_tensor(both[:], attn_sb[:], rel_sb[:], ALU.add).then_inc(both_ready, 1)
                keep_half(2, aT)
                dve.wait_ge(x_in, b * 16 + 16)
                residual(1, x_sb)
                layer_norm(nc, chain, b * 2, r, x1, stats, moments, rstd, moments_ready, deviation_ready)
                dve.sem_inc(x1_ready, 1)
                keep_half(4, x1T)
                dve.wait_ge(bankT_full, b * T_USES + 6)
                nc.vector.tensor_scalar(qT[:, 1, :], bankT[1][:].rearrange("p a b -> p (a b)"), bq[:, 1:2], SC, ALU.add, ALU.mult)\
                    .then_inc(bankT_empty[1], 1)

                def take_scores(t):
                    dve.wait_ge(bankS_full, b * QT + t + 1)
                    nc.vector.tensor_tensor(sc[t % 2][:], bankS[t % 2][:], keep[:, t, :].unsqueeze(1).to_broadcast([P, H, SK]),
                                            ALU.mult).then_inc(bankS_empty, 1)

                def rowmax(t):
                    dve.wait_ge(filled, b * QT + t + 1)
                    nc.vector.tensor_reduce(negmax[:, t, :], sc[t % 2][:], AX_X, ALU.max, negate=True).then_inc(max_ready, 1)

                def rowsum(t):
                    dve.wait_ge(exp_ready, b * QT + t + 1)
                    return nc.vector.tensor_reduce(total[:, t, :], pr[t % 2][:], AX_X, ALU.add)

                take_scores(0)
                take_scores(1)
                rowmax(0)
                rowmax(1)
                rowsum(0)
                take_scores(2)
                rowsum(1)
                take_scores(3)
                rowmax(2)
                rowmax(3)
                rowsum(2)
                chain.link(rowsum(3))
                chain.link(nc.vector.reciprocal(inv[:], total[:]))
                for i in range(2):
                    dve.wait_ge(bankR_full, b * R_USES + 3 + i)
                    nc.vector.tensor_tensor(
                        o[:, 2 * i:2 * i + 2, :].rearrange("p t (h e) -> p (t h) e", e=D),
                        bankR[i][:].rearrange("p t (h e) -> p (t h) e", e=D),
                        inv[:, 2 * i:2 * i + 2, :].rearrange("p t h -> p (t h)").unsqueeze(2).to_broadcast([P, 2 * H, D]),
                        ALU.mult).then_inc(bankR_empty[i], 1)
                for i in range(2):
                    dve.wait_ge(bankR_empty[i], b * (R_USES // 2) + 3)
                dve.sem_inc(o_ready, 1)
                keep_half(T_USES - 2, oT)
                residual(5, x1)
                dve.wait_ge(x2_free, b + 1)
                layer_norm(nc, chain, b * 2 + 1, r, x2, stats, moments, rstd, moments_ready, deviation_ready)
                dve.sem_inc(x2_ready, 1)
                keep_half(T_USES, x2T)
                for i in range(2):
                    dve.wait_ge(bankR_empty[i], b * (R_USES // 2) + 5)
                chain.link(nc.vector.tensor_scalar(eneg[:], eneg[:], 1.0, None, ALU.add))
                chain.link(nc.vector.reciprocal(gate_scores[:, bass.ds(b * QT, QT), :], eneg[:]))
                chain.end()


def route(nc, d, gate_scores, slot_token, slot_weight, slot_index, slot_scale):
    with ExitStack() as ctx:
        def sb(name, shape, dt=F32):
            return ctx.enter_context(nc.sbuf_tensor("r_" + name, shape, dt))

        def sem(name):
            return ctx.enter_context(nc.semaphore("r_" + name))

        G = NX // GE
        CH = 512 // NX
        bias = sb("bias", [P, NX])
        before = sb("before", [P, P])
        ones = sb("ones", [P, P])
        ident = sb("ident", [P, P])
        lower = sb("lower", [P, G, G])
        iota = sb("iota", [P, SLOT_B])
        token1 = sb("token1", [P, NT])
        row_empty = sb("row_empty", [P, 2 * NX])
        own_expert = sb("own_expert", [P, GE])

        sfc = sb("sfc", [P, NT, NX])
        hi, lo = sb("hi", [P, NT * G, 4]), sb("lo", [P, NT * G, 4])
        hi2, lo2, lo2b = (sb(n, [P, NT * G, 2]) for n in ("hi2", "lo2", "lo2b"))
        lo3, lo3b = sb("lo3", [P, NT * G]), sb("lo3b", [P, NT * G])
        gscore = sb("gscore", [P, NT, G])
        rank = sb("rank", [P, NT, G])
        work = sb("work", [P, NT, NX])
        work2 = sb("work2", [P, NT, NX])
        top = sb("top", [P, NT, 8])
        mask = sb("mask", [P, NT, NX])
        wsum = sb("wsum", [P, NT])
        ai, bi = sb("ai", [P, NT, NX], I32), sb("bi", [P, NT, NX], I32)
        first = [sb(f"first{i}", [P, CH, GE, SLOT_A]) for i in range(2)]
        second = [sb(f"second{i}", [P, 3, CH, GE, SLOT_B]) for i in range(2)]
        picked = sb("picked", [P, 2, GE, SLOT_B])
        lists = sb("lists", [P, 2, G, SLOT_B])
        block_rows = sb("block_rows", [P, 2, P])

        banks = [ctx.enter_context(nc.psum_tensor(f"r_bank{i}", [P, 512], F32)) for i in range(8)]

        const_in = sem("const_in")
        ones_ready = sem("ones_ready")
        step = sem("step")
        mask_ready = sem("mask_ready")
        counted = sem("counted")
        kept = sem("kept")
        onehot_ready = sem("onehot_ready")
        second_ready = sem("second_ready")
        token_ready = sem("token_ready")
        chunk_done = sem("chunk_done")
        picked_out = sem("picked_out")
        lists_ready = sem("lists_ready")
        lists_stored = sem("lists_stored")
        rows_in = sem("rows_in")
        flipped = sem("flipped")

        consts = [(bias, d["gate_bias"]), (before, d["before"]), (ident, d["ident"]), (lower, d["lower"]),
                  (iota, d["iota"]), (token1, d["token1"]), (row_empty, d["row_empty"]),
                  (own_expert, d["own_expert"])]
        NCHUNK = NT // CH

        block = ctx.enter_context(nc.Block())

        @block.sync
        def _(sp):
            for dst, src in consts:
                sp.dma_start(dst[:], src).then_inc(const_in, 16)
            sp.wait_ge(lists_ready, 1)
            for i, dram in enumerate((slot_token, slot_weight)):
                sp.dma_start(dram.rearrange("(g p b) -> p g b", g=G, b=SLOT_B), lists[:, i]).then_inc(lists_stored, 16)
            sp.wait_ge(lists_stored, 32)
            for i, dram in enumerate((slot_token, slot_weight)):
                sp.dma_start(block_rows[:, i], dram.rearrange("(n q) -> n q", q=P)).then_inc(rows_in, 16)

        @block.tensor
        def _(pe):
            pe.wait_ge(const_in, 16 * len(consts))
            pe.wait_ge(ones_ready, 1)
            pe.wait_ge(mask_ready, 1)
            for c in range(NCHUNK):
                if c >= 4:
                    pe.wait_ge(kept, 2 * (c - 3))
                src = mask[:, c * CH:(c + 1) * CH, :].rearrange("p t e -> p (t e)")
                nc.tensor.matmul(banks[2 * c % 8][:], before[:], src, start=True, stop=True)
                nc.tensor.matmul(banks[(2 * c + 1) % 8][:], ones[:], src, start=True, stop=True).then_inc(counted, 1)
            pe.wait_ge(kept, 2 * NCHUNK)
            n = 0
            for g in range(G):
                if g >= 2:
                    pe.wait_ge(picked_out, g - 1)
                for c in range(NCHUNK):
                    pe.wait_ge(second_ready, n + 1)
                    pe.wait_ge(token_ready, n + 1)
                    for t in range(CH):
                        mm = nc.tensor.matmul(banks[g % 2][:, 0:2 * P], first[n % 2][:, t].rearrange("p e a -> p (e a)"),
                                              second[n % 2][:, 1:3, t].rearrange("p i e b -> p i (e b)"),
                                              start=c == 0 and t == 0, stop=c == NCHUNK - 1 and t == CH - 1)
                    mm.then_inc(chunk_done, 1)
                    n += 1
            pe.wait_ge(rows_in, 32)
            for i in range(2):
                mm = nc.tensor.transpose(banks[2][:, i * P:(i + 1) * P], block_rows[:, i], ident[:])
            mm.then_inc(flipped, 1)

        @block.gpsimd
        def _(pool):
            pool.memset(ones[:], 1.0).then_inc(ones_ready, 1)
            pool.wait_ge(const_in, 16 * len(consts))
            n = 0
            for g in range(G):
                for c in range(NCHUNK):
                    pool.wait_ge(onehot_ready, n + 1)
                    s = second[n % 2]
                    nc.gpsimd.tensor_tensor(
                        s[:, 1].rearrange("p t e b -> p t (e b)"), s[:, 0].rearrange("p t e b -> p t (e b)"),
                        token1[:, c * CH:(c + 1) * CH].unsqueeze(2).to_broadcast([P, CH, GE * SLOT_B]),
                        ALU.mult).then_inc(token_ready, 1)
                    n += 1

        @block.vector
        def _(dve):
            chain = Chain(dve, step, 0, 0)
            link = chain.link
            v = nc.vector
            dve.wait_ge(const_in, 16 * len(consts))
            link(v.tensor_tensor(sfc[:], gate_scores[:], bias[:].unsqueeze(1).to_broadcast([P, NT, NX]), ALU.add))
            x = sfc[:].rearrange("p t (g k) -> p (t g) k", k=GE)
            v.tensor_tensor(hi[:], x[:, :, 0:4], x[:, :, 4:8], ALU.max)
            link(v.tensor_tensor(lo[:], x[:, :, 0:4], x[:, :, 4:8], ALU.min))
            v.tensor_tensor(hi2[:], hi[:, :, 0:2], hi[:, :, 2:4], ALU.max)
            v.tensor_tensor(lo2[:], hi[:, :, 0:2], hi[:, :, 2:4], ALU.min)
            link(v.tensor_tensor(lo2b[:], lo[:, :, 0:2], lo[:, :, 2:4], ALU.max))
            link(v.tensor_tensor(lo2[:], lo2[:], lo2b[:], ALU.max))
            flat = gscore[:].rearrange("p t g -> p (t g)")
            v.tensor_tensor(flat, hi2[:, :, 0], hi2[:, :, 1], ALU.max)
            v.tensor_tensor(lo3[:], hi2[:, :, 0], hi2[:, :, 1], ALU.min)
            link(v.tensor_tensor(lo3b[:], lo2[:, :, 0], lo2[:, :, 1], ALU.max))
            link(v.tensor_tensor(lo3[:], lo3[:], lo3b[:], ALU.max))
            link(v.tensor_tensor(flat, flat, lo3[:], ALU.add))
            other = gscore[:].unsqueeze(2).to_broadcast([P, NT, G, G])
            own = gscore[:].unsqueeze(3).to_broadcast([P, NT, G, G])
            w4 = work[:].rearrange("p t (g k) -> p t g k", k=G)
            w4b = work2[:].rearrange("p t (g k) -> p t g k", k=G)
            v.tensor_tensor(w4, other, own, ALU.is_gt)
            link(v.tensor_tensor(w4b, other, own, ALU.is_equal))
            link(v.tensor_tensor(w4b, w4b, lower[:].unsqueeze(1).to_broadcast([P, NT, G, G]), ALU.mult))
            link(v.tensor_tensor(work[:], work[:], work2[:], ALU.add))
            link(v.tensor_reduce(rank[:], w4, AX_X, ALU.add))
            link(v.tensor_scalar(rank[:], rank[:], float(TOP_GROUPS), -FAR, ALU.is_ge, ALU.mult))
            link(v.tensor_tensor(work[:].rearrange("p t (g k) -> p (t g) k", k=GE), x,
                                 rank[:].rearrange("p t g -> p (t g)").unsqueeze(2).to_broadcast([P, NT * G, GE]), ALU.add))
            for t in range(NT):
                last = v.max(top[:, t, :], work[:, t, :])
            link(last)
            for t in range(NT):
                last = v.match_replace(work2[:, t, :], top[:, t, :], work[:, t, :], TAKEN)
            link(last)
            v.tensor_scalar(mask[:], work2[:], TAKEN, None, ALU.is_equal).then_inc(mask_ready, 1)
            dve.wait_ge(mask_ready, 1)
            link(v.tensor_tensor(gate_scores[:], gate_scores[:], mask[:], ALU.mult))
            link(v.tensor_reduce(wsum[:], gate_scores[:], AX_X, ALU.add))
            link(v.tensor_scalar(wsum[:], wsum[:], 1e-20, None, ALU.add))
            link(v.reciprocal(wsum[:], wsum[:]))
            link(v.tensor_scalar(wsum[:], wsum[:], ROUTE_SCALE, None, ALU.mult))
            v.tensor_tensor(gate_scores[:], gate_scores[:], wsum[:].unsqueeze(2).to_broadcast([P, NT, NX]), ALU.mult)
            pos = sfc
            total = work[:].rearrange("p t e -> p (t e)").rearrange("p (e t) -> p e t", t=NT)
            reset = work2[:].rearrange("p t e -> p (t e)").rearrange("p (e t) -> p e t", t=NT)
            for c in range(NCHUNK):
                dve.wait_ge(counted, c + 1)
                v.tensor_copy(pos[:, c * CH:(c + 1) * CH, :].rearrange("p t e -> p (t e)"), banks[2 * c % 8][:]).then_inc(kept, 1)
                v.tensor_copy(total[:, :, c * CH:(c + 1) * CH],
                              banks[(2 * c + 1) % 8][:].rearrange("p (t e) -> p e t", e=NX)).then_inc(kept, 1)
            dve.wait_ge(kept, 2 * NCHUNK)
            link(v.memset(reset, 1.0))
            link(v.memset(reset[:, :, 0:1], 0.0))
            running = ai[:].bitcast(F32)
            link(v.tensor_tensor_scan(running.rearrange("p t e -> p (t e)"), work2[:].rearrange("p t e -> p (t e)"),
                                      work[:].rearrange("p t e -> p (t e)"), 0.0, ALU.mult, ALU.add))
            link(v.tensor_tensor(work[:], running, work[:], ALU.subtract))
            link(v.tensor_tensor(pos[:], pos[:], total.rearrange("p e t -> p t e"), ALU.add))
            link(v.tensor_scalar(work2[:], mask[:], -UNCHOSEN, UNCHOSEN, ALU.mult, ALU.add))
            link(v.tensor_tensor(pos[:], pos[:], work2[:], ALU.add))
            link(v.tensor_copy(ai[:], pos[:]))
            v.tensor_scalar(bi[:], ai[:], SLOT_B - 1, None, ALU.bitwise_and)
            link(v.tensor_scalar(work2[:].bitcast(I32), ai[:], SLOT_BITS, None, ALU.arith_shift_right))
            high, low = work, pos
            v.tensor_copy(high[:], work2[:].bitcast(I32))
            link(v.tensor_copy(low[:], bi[:]))
            n = 0
            for g in range(G):
                e = slice(g * GE, (g + 1) * GE)
                for c in range(NCHUNK):
                    t = slice(c * CH, (c + 1) * CH)
                    if n >= 2:
                        dve.wait_ge(chunk_done, n - 1)
                    shape = [P, CH, GE, SLOT_B]
                    s = second[n % 2]
                    codes = iota[:].unsqueeze(1).unsqueeze(1).to_broadcast(shape)
                    v.tensor_tensor(s[:, 0], low[:, t, e].unsqueeze(3).to_broadcast(shape), codes, ALU.is_equal).then_inc(onehot_ready, 1)
                    v.tensor_tensor(first[n % 2][:], high[:, t, e].unsqueeze(3).to_broadcast(shape), codes, ALU.is_equal)
                    dve.wait_ge(onehot_ready, n + 1)
                    v.tensor_tensor(s[:, 2], s[:, 0], gate_scores[:, t, e].unsqueeze(3).to_broadcast(shape), ALU.mult).then_inc(second_ready, 1)
                    n += 1
                dve.wait_ge(chunk_done, n)
                v.tensor_tensor(picked[:], banks[g % 2][:, 0:2 * P].rearrange("p (i e b) -> p i e b", i=2, b=SLOT_B),
                                own_expert[:].unsqueeze(1).unsqueeze(3).to_broadcast([P, 2, GE, SLOT_B]), ALU.mult)\
                    .then_inc(picked_out, 1)
                dve.wait_ge(picked_out, g + 1)
                last = link(v.tensor_reduce(lists[:, :, g, :], picked[:].rearrange("p i e b -> p i b e"), AX_X, ALU.add))
            dve.sem_inc(lists_ready, 1)
            dve.wait_ge(flipped, 1)
            v.tensor_copy(slot_scale[:], banks[2][:, P:2 * P])
            link(v.tensor_scalar(hi[:, 0:NX // 2, :].rearrange("p a b -> p (a b)"), banks[2][:, 0:P], 0.0, None, ALU.is_equal))
            hole = hi[:, 0:NX // 2, :].rearrange("p a b -> p (a b)")
            link(v.tensor_tensor(hole, hole, row_empty[:], ALU.mult))
            link(v.tensor_tensor(hole, hole, banks[2][:, 0:P], ALU.add))
            link(v.tensor_scalar(slot_index[:], hole, -1.0, None, ALU.add))


def experts(nc, d, x2_rows, acc_rows, slot_index, slot_scale):
    with ExitStack() as ctx:
        def sb(name, shape, dt=F32):
            return ctx.enter_context(nc.sbuf_tensor("e_" + name, shape, dt))

        def sem(name):
            return ctx.enter_context(nc.semaphore("e_" + name))

        NS = 4
        ident = sb("ident", [P, P])
        wg, wu, wd = ([sb(f"{n}{i}", s) for i in range(NS)]
                      for n, s in (("wg", [P, HALVES, P]), ("wu", [P, HALVES, P]), ("wd", [P, E])))
        rows = [sb(f"rows{i}", [P, 2, E]) for i in range(NS)]
        rowsT = [sb(f"rowsT{i}", [P, HALVES, CAP]) for i in range(2)]
        silu = [sb(f"silu{i}", [P, CAP]) for i in range(2)]
        hidden = [sb(f"hidden{i}", [P, CAP]) for i in range(2)]
        y = [sb(f"y{i}", [P, 2, E]) for i in range(NS)]
        bankT, bankH, bankY = ([ctx.enter_context(nc.psum_tensor(f"e_{n}{i}", [P, 2, CAP], F32)) for i in range(2)]
                               for n in ("bankT", "bankH", "bankY"))
        ident_in = sem("ident_in")
        w_in = [sem(f"w_in{i}") for i in range(NS)]
        rows_in = [sem(f"rows_in{i}") for i in range(NS)]
        added = [sem(f"added{i}") for i in range(NS)]
        flipped, rowsT_ready, up_done, silu_ready, hidden_ready, down_done, y_ready = (
            sem(n) for n in ("flipped", "rowsT_ready", "up_done", "silu_ready", "hidden_ready", "down_done", "y_ready"))

        block = ctx.enter_context(nc.Block())

        @block.sync
        def _(sp):
            sp.dma_start(ident[:], d["ident"]).then_inc(ident_in, 16)

            def load(e, s):
                for dst, src in ((wg, "w_gate"), (wu, "w_up")):
                    sp.dma_start(dst[s][:], d[src][bass.ds(e, 1)].rearrange("e (a p) i -> p (e a) i", p=P)).then_inc(w_in[s], 16)
                sp.dma_start(wd[s][:], d["w_down"][bass.ds(e, 1)].rearrange("e i h -> (e i) h")).then_inc(w_in[s], 16)

            for s in range(NS):
                load(s, s)
            with sp.Fori(0, NX // NS - 1) as t:
                for s in range(NS):
                    sp.wait_ge(down_done, t * NS + s + 1)
                    load(t * NS + s + NS, s)

        @block.gpsimd
        def _(pool):
            def gather(e):
                s = e % NS
                if e >= NS:
                    pool.wait_ge(flipped, e - NS + 1)
                for i in range(2):
                    at = slot_index[:, 2 * e + i:2 * e + i + 1]
                    nc.gpsimd.indirect_dma_start(
                        out=rows[s][:, i, :], out_offset=None, in_=x2_rows,
                        in_offset=bass.IndirectOffsetOnAxis(ap=at, axis=0)).then_inc(rows_in[s], 16)

            def scatter(e):
                s = e % NS
                pool.wait_ge(y_ready, e + 1)
                if e >= 2:
                    pool.wait_ge(added[(e - 2) % NS], 32 * ((e - 2) // NS + 1))
                for i in range(2):
                    at = slot_index[:, 2 * e + i:2 * e + i + 1]
                    nc.gpsimd.indirect_dma_start(
                        out=acc_rows[e % 2], out_offset=bass.IndirectOffsetOnAxis(ap=at, axis=0),
                        in_=y[s][:, i, :], in_offset=None, compute_op=ALU.add).then_inc(added[s], 16)

            AHEAD = 3
            for e in range(AHEAD):
                gather(e)
            for e in range(NX):
                if e + AHEAD < NX:
                    gather(e + AHEAD)
                scatter(e)
            for s in range(NS):
                pool.wait_ge(added[s], 32 * NX // NS)

        @block.tensor
        def _(pe):
            pe.wait_ge(ident_in, 16)

            def flip(e, t, s, first=False):
                pe.wait_ge(rows_in[s], t * 32 + 32)
                for a in range(HALVES):
                    for i in range(2):
                        mm = nc.tensor.transpose(bankT[s % 2][:, a, i * P:(i + 1) * P], rows[s][:, i, a * P:(a + 1) * P], ident[:])
                mm.then_inc(flipped, 1)

            def up(e, t, s, first=False):
                pe.wait_ge(w_in[s], t * 48 + 48)
                pe.wait_ge(rowsT_ready, e + 1)
                for n, w in enumerate((wg, wu)):
                    for a in range(HALVES):
                        mm = nc.tensor.matmul(bankH[s % 2][:, n, :], w[s][:, a, :], rowsT[s % 2][:, a, :],
                                              start=a == 0, stop=a == HALVES - 1)
                mm.then_inc(up_done, 1)

            def down(e, t, s, first=False):
                pe.wait_ge(hidden_ready, e + 1)
                if not first:
                    pe.wait_ge(y_ready, e - 1)
                for i in range(2):
                    mm = nc.tensor.matmul(bankY[s % 2][:, i, :], hidden[s % 2][:, i * P:(i + 1) * P], wd[s][:], start=True, stop=True)
                mm.then_inc(down_done, 1)

            flip(0, 0, 0)
            flip(1, 0, 1)
            up(0, 0, 0)

            def turn(t, last=False, head=False):
                for s in range(NS):
                    e = t * NS + s
                    more = s + 2 >= NS
                    if not (last and more):
                        flip(e + 2, t + 1 if more else t, (s + 2) % NS)
                    if not (last and s == NS - 1):
                        up(e + 1, t + 1 if s == NS - 1 else t, (s + 1) % NS)
                    down(e, t, s, first=head and s < 2)

            turn(0, head=True)
            with pe.Fori(1, NX // NS - 1) as t:
                turn(t)
            turn(NX // NS - 1, last=True)

        @block.scalar
        def _(act):
            def keep(e, s, first=False):
                act.wait_ge(flipped, e + 1)
                if not first:
                    act.wait_ge(up_done, e - 1)
                nc.scalar.activation(rowsT[s % 2][:], bankT[s % 2][:], ACT.Copy).then_inc(rowsT_ready, 1)

            def gate(e, s, first=False):
                act.wait_ge(up_done, e + 1)
                if not first:
                    act.wait_ge(hidden_ready, e - 1)
                nc.scalar.activation(silu[s % 2][:], bankH[s % 2][:, 0, :], ACT.Silu).then_inc(silu_ready, 1)

            keep(0, 0, True)
            keep(1, 1, True)
            gate(0, 0, True)

            def turn(t, last=False, head=False):
                for s in range(NS):
                    e = t * NS + s
                    if not (last and s + 2 >= NS):
                        keep(e + 2, s)
                    if not (last and s == NS - 1):
                        gate(e + 1, s + 1, first=head and s == 0)

            turn(0, head=True)
            with act.Fori(1, NX // NS - 1) as t:
                turn(t)
            turn(NX // NS - 1, last=True)

        @block.vector
        def _(dve):
            def product(e, s, first=False):
                dve.wait_ge(silu_ready, e + 1)
                if not first:
                    dve.wait_ge(down_done, e - 1)
                nc.vector.tensor_tensor(hidden[s % 2][:], silu[s % 2][:], bankH[s % 2][:, 1, :], ALU.mult).then_inc(hidden_ready, 1)

            def scale(e, t, s, first=False):
                dve.wait_ge(down_done, e + 1)
                if not first:
                    dve.wait_ge(added[s], t * 32)
                for i in range(2):
                    mm = nc.vector.tensor_scalar(y[s][:, i, :], bankY[s % 2][:, i, :], slot_scale[:, bass.ds(e * 2 + i, 1)], None, ALU.mult)
                mm.then_inc(y_ready, 1)

            product(0, 0, True)

            def turn(t, last=False, head=False):
                for s in range(NS):
                    e = t * NS + s
                    if not (last and s == NS - 1):
                        product(e + 1, s + 1, first=head and s == 0)
                    scale(e, t, s, first=head)

            turn(0, head=True)
            with dve.Fori(1, NX // NS - 1) as t:
                turn(t)
            turn(NX // NS - 1, last=True)


def final_norm(nc, acc_rows, out):
    with ExitStack() as ctx:
        def sb(name, shape, dt=F32):
            return ctx.enter_context(nc.sbuf_tensor("f_" + name, shape, dt))

        def sem(name):
            return ctx.enter_context(nc.semaphore("f_" + name))

        parts = [[sb(f"part{i}{j}", [P, QT, E]) for j in range(2)] for i in range(2)]
        r = sb("r", [P, QT, E])
        normed = [sb(f"normed{i}", [P, QT, E]) for i in range(2)]
        stats, moments, rstd, eps = sb("stats", [P, QT, 6]), sb("moments", [P, QT, 2]), sb("rstd", [P, QT]), sb("eps", [P, 1])
        parts_in = [sem(f"parts_in{i}") for i in range(2)]
        stored = [sem(f"stored{i}") for i in range(2)]
        eps_ready, summed, moments_ready, deviation_ready, normed_ready, step = (
            sem(n) for n in ("eps_ready", "summed", "moments_ready", "deviation_ready", "normed_ready", "step"))

        def rows(dram, b):
            return dram[bass.ds(b * S, S), :].rearrange("(t p) e -> p t e", p=P)

        block = ctx.enter_context(nc.Block())

        @block.sync
        def _(sp):
            def load(b, i):
                for j in range(2):
                    sp.dma_start(parts[i][j][:], rows(acc_rows[j], b)).then_inc(parts_in[i], 16)

            load(0, 0)
            load(1, 1)
            with sp.Fori(0, B // 2 - 1) as t:
                for i in range(2):
                    sp.wait_ge(summed, t * 2 + i + 1)
                    load(t * 2 + i + 2, i)

        @block.gpsimd
        def _(pool):
            pool.memset(eps[:], EPS).then_inc(eps_ready, 1)
            with pool.Fori(0, B // 2) as t:
                for i in range(2):
                    pool.wait_ge(normed_ready, t * 2 + i + 1)
                    pool.dma_start(rows(out, t * 2 + i), normed[i][:]).then_inc(stored[i], 16)
            for i in range(2):
                pool.wait_ge(stored[i], 16 * B // 2)

        @block.scalar
        def _(act):
            act.wait_ge(eps_ready, 1)
            with act.Fori(0, B) as b:
                deviation(nc, act, b, moments, rstd, eps, moments_ready, deviation_ready)

        @block.vector
        def _(dve):
            def turn(t, i, first=False):
                b = t * 2 + i
                chain = Chain(dve, step, 4, b)
                dve.wait_ge(parts_in[i], t * 32 + 32)
                nc.vector.tensor_tensor(r[:], parts[i][0][:], parts[i][1][:], ALU.add).then_inc(summed, 1)
                dve.wait_ge(summed, b + 1)
                if not first:
                    dve.wait_ge(stored[i], t * 16)
                layer_norm(nc, chain, b, r, normed[i], stats, moments, rstd, moments_ready, deviation_ready)
                dve.sem_inc(normed_ready, 1)
                chain.end()

            turn(0, 0, True)
            turn(0, 1, True)
            with dve.Fori(1, B // 2) as t:
                turn(t, 0)
                turn(t, 1)


def layouts(x, ctx_1024, mask_1x1xSxS2_ik0, **w):
    def c(a):
        return np.ascontiguousarray(a)

    def columns(v):
        return c(v.reshape(HALVES, P).T)

    out = {}
    out["a_xT"] = c(np.transpose(x, (0, 2, 1)))
    wq, bq = w["L0_attn_Wq"], w["L0_attn_bq"]
    out["a_wqT"], out["a_wkT"], out["a_wvT"] = c(wq.T), c(w["L0_attn_Wk"].T), c(w["L0_attn_Wv"].T)
    out["a_bq"], out["a_bk"], out["a_bv"] = columns(bq), columns(w["L0_attn_bk"]), c(w["L0_attn_bv"].reshape(1, E))
    r, k = w["L0_attn_rel_k_emb"], w["L0_attn_rel_v_emb"]
    j = np.arange(QG)[:, None]
    at = np.clip(j + (S - QG) - np.arange(TKW)[None, :], -MAXREL, MAXREL) + MAXREL
    out["relk"] = c(np.transpose(r[at], (0, 2, 1)).reshape(P, TKW))
    at = np.clip(np.arange(TVZ)[None, :] - (KT - 1) * P - np.arange(P)[:, None], -MAXREL, MAXREL) + MAXREL
    out["relv"] = c(k[at].reshape(P, TVZ * D))
    p = np.arange(P)
    hm = np.zeros((P, HALVES, H), np.float32)
    for a in range(HALVES):
        hm[p, a, a * (P // D) + p // D] = 1
    out["head_mask"] = hm
    qm = np.zeros((P, QG), np.float32)
    qm[p, p // D] = 1
    out["query_mask"] = qm
    om = np.zeros((P, QG + H, D), np.float32)
    om[p, p // H, :] = 1
    om[p, QG + p % H, :] = 1
    out["out_mask"] = om.reshape(P, P + E)
    out["ident"] = np.eye(P, dtype=np.float32)
    out["x"] = c(x.reshape(TOK, E))
    out["a_woT"], out["a_bo"] = c(w["L0_attn_Wo"].T), c(w["L0_attn_bo"].reshape(1, E))
    for n in ("q", "k", "v", "o"):
        out[f"x_w{n}T"] = c(w[f"L0_xattn_W{n}"].T)
    out["x_bq"], out["x_bk"] = columns(w["L0_xattn_bq"]), columns(w["L0_xattn_bk"])
    out["x_bv"], out["x_bo"] = c(w["L0_xattn_bv"].reshape(1, E)), c(w["L0_xattn_bo"].reshape(1, E))
    out["ctxT"] = c(np.repeat(np.transpose(ctx_1024, (2, 0, 1))[:, :, None, :], 2, axis=2))
    out["mask"] = c(mask_1x1xSxS2_ik0.reshape(S, SK))
    out["gate_wT"] = c(w["L0_ffn_gate_w"].T)
    half = np.zeros((P, H // HALVES), np.float32)
    half[p, p // D] = 1
    out["half_mask"] = half
    pair = np.zeros((P, 2, D), np.float32)
    pair[p, p // SK, :] = 1
    out["pair_mask"] = pair.reshape(P, 2 * D)
    out["gate_bias"] = c(np.broadcast_to(w["L0_ffn_gate_bias"], (P, NX)))
    out["before"] = np.triu(np.ones((P, P), np.float32), 1)
    out["lower"] = c(np.broadcast_to(np.tril(np.ones((NX // GE, NX // GE), np.float32), -1), (P, NX // GE, NX // GE)))
    out["iota"] = c(np.broadcast_to(np.arange(SLOT_B, dtype=np.float32), (P, SLOT_B)))
    out["token1"] = (p[:, None] + P * np.arange(NT)[None, :] + 1).astype(np.float32)
    out["row_empty"] = (TOK + 1 + p[:, None] + P * (np.arange(2 * NX)[None, :] % 2)).astype(np.float32)
    own = np.zeros((P, GE), np.float32)
    own[p, p // SLOT_A] = 1
    out["own_expert"] = own
    for n in ("w_gate", "w_up", "w_down"):
        out[n] = w[f"L0_ffn_{n}"]
    return out


def program(nc, d, out):
    qs = nc.dram_tensor("q_scratch", [B, E, S], F32).ap()
    attn = nc.dram_tensor("attn_scratch", [B, S, E], F32).ap()
    rel = nc.dram_tensor("rel_scratch", [B, S, E], F32).ap()
    x2_rows = nc.dram_tensor("x2_scratch", [TOK + CAP, E], F32).ap()
    acc_rows = [nc.dram_tensor(f"acc_scratch{i}", [TOK + CAP, E], F32).ap() for i in range(2)]
    slot_token = nc.dram_tensor("slot_token_scratch", [NX * CAP], F32).ap()
    slot_weight = nc.dram_tensor("slot_weight_scratch", [NX * CAP], F32).ap()
    project_queries(nc, d, qs)
    self_attention(nc, d, qs, attn, rel)
    with (nc.sbuf_tensor("gate_scores", [P, NT, NX], F32) as gate_scores,
          nc.sbuf_tensor("slot_index", [P, 2 * NX], U32) as slot_index,
          nc.sbuf_tensor("slot_scale", [P, 2 * NX], F32) as slot_scale):
        cross_attention(nc, d, attn.rearrange("b s e -> (b s) e"), rel.rearrange("b s e -> (b s) e"), x2_rows, acc_rows,
                        gate_scores)
        route(nc, d, gate_scores, slot_token, slot_weight, slot_index, slot_scale)
        experts(nc, d, x2_rows, acc_rows, slot_index, slot_scale)
    final_norm(nc, acc_rows, out.rearrange("b s e -> (b s) e"))


def kernel(**inputs):
    import concourse.bacc as bacc
    from concourse.bass_utils import run_bass_kernel_spmd

    arrays = layouts(**{k: np.asarray(v) for k, v in inputs.items()})
    nc = bacc.Bacc("TRN2", target_bir_lowering=False, num_devices=1)
    named = {f"in_{k}": v for k, v in arrays.items()}
    d = {k: nc.dram_tensor(f"in_{k}", v.shape, mybir.dt.from_np(v.dtype), kind="ExternalInput").ap()
         for k, v in arrays.items()}
    out = nc.dram_tensor("out", [B, S, E], F32, kind="ExternalOutput").ap()
    program(nc, d, out)
    r = run_bass_kernel_spmd(nc, [named], core_ids=[0])
    return r.results[0]["out"]
```

```python
from contextlib import ExitStack

import numpy as np

import concourse.bass as bass
from concourse import mybir
from concourse.alu_op_type import AluOpType as ALU

ACT = mybir.ActivationFunctionType
F32 = mybir.dt.float32
I32 = mybir.dt.int32
U32 = mybir.dt.uint32
AX_X = mybir.AxisListType.X

P = 128
B, S, E = 16, 512, 256
H, D = 16, 16
MAXREL = 128
HALVES = E // P
QG = P // H
NG = S // QG
KT = S // P
TKW = 2 * S - QG
TVZ = 2 * S - P
SC = D ** -0.5
QT = S // P
SK = 64
TOK = B * S
NT = TOK // P
NX = 64
GE = 8
TOP_GROUPS = 4
CAP = 256
SLOT_A = SLOT_B = 16
SLOT_BITS = 4
ROUTE_SCALE = 2.5
NEG = -1e9
FAR = 1e30
TAKEN = -3e38
UNCHOSEN = 65536.0
EPS = 1e-5
HH = H // HALVES
NORM_STEPS = 3
CTX_STEPS = HALVES + B // 4
OW = 2 * P + KT


def project_queries(nc, d, qs):
    with ExitStack() as ctx:
        wq = ctx.enter_context(nc.sbuf_tensor("wq", [P, HALVES, E], F32))
        bq = ctx.enter_context(nc.sbuf_tensor("bq", [P, HALVES], F32))
        xT = [ctx.enter_context(nc.sbuf_tensor(f"xTq{i}", [P, HALVES, S], F32)) for i in range(2)]
        q = [ctx.enter_context(nc.sbuf_tensor(f"q{i}", [P, HALVES, S], F32)) for i in range(2)]
        psQ = [ctx.enter_context(nc.psum_tensor(f"psQ{i}", [P, HALVES, S], F32)) for i in range(2)]
        w_in, projected, kept = (ctx.enter_context(nc.semaphore(n)) for n in ("wq_in", "q_projected", "q_kept"))
        x_in = [ctx.enter_context(nc.semaphore(f"xq_in{i}")) for i in range(2)]
        stored = [ctx.enter_context(nc.semaphore(f"q_stored{i}")) for i in range(2)]
        block = ctx.enter_context(nc.Block())

        @block.sync
        def _(sp):
            sp.dma_start(wq[:], d["a_wqT"].rearrange("(a p) o -> p a o", p=P)).then_inc(w_in, 16)
            sp.dma_start(bq[:], d["a_bq"]).then_inc(w_in, 16)
            for b in range(B):
                if b >= 2:
                    sp.wait_ge(projected, b - 1)
                sp.dma_start(xT[b % 2][:], d["a_xT"][b].rearrange("(a p) s -> p a s", p=P)).then_inc(x_in[b % 2], 16)

        @block.tensor
        def _(pe):
            pe.wait_ge(w_in, 32)
            for b in range(B):
                pe.wait_ge(x_in[b % 2], 16 * (b // 2 + 1))
                if b >= 2:
                    pe.wait_ge(kept, b - 1)
                for m in range(HALVES):
                    for a in range(HALVES):
                        mm = nc.tensor.matmul(psQ[b % 2][:, m, :], wq[:, a, m * P:(m + 1) * P], xT[b % 2][:, a, :],
                                              start=a == 0, stop=a == HALVES - 1)
                mm.then_inc(projected, 1)

        @block.vector
        def _(dve):
            dve.wait_ge(w_in, 32)
            for b in range(B):
                dve.wait_ge(projected, b + 1)
                if b >= 2:
                    dve.wait_ge(stored[b % 2], 16 * (b // 2))
                for m in range(HALVES):
                    mm = nc.vector.tensor_scalar(q[b % 2][:, m, :], psQ[b % 2][:, m, :], bq[:, m:m + 1], SC, ALU.add, ALU.mult)
                mm.then_inc(kept, 1)

        @block.scalar
        def _(act):
            for b in range(B):
                act.wait_ge(kept, b + 1)
                act.dma_start(qs[b].rearrange("(a p) s -> p a s", p=P), q[b % 2][:]).then_inc(stored[b % 2], 16)
            for i in range(2):
                act.wait_ge(stored[i], 16 * B // 2)


class Chain:

    def __init__(self, engine, sem, per_turn, turn):
        self.engine, self.sem, self.per_turn, self.turn, self.n = engine, sem, per_turn, turn, 0

    def link(self, instruction):
        self.n += 1
        instruction.then_inc(self.sem, 1)
        self.engine.wait_ge(self.sem, self.turn * self.per_turn + self.n)

    def link_alone(self, instruction):
        self.link(instruction)
        self.n += 1
        self.engine.sem_inc(self.sem, 1)

    def end(self):
        assert self.n == self.per_turn, (self.n, self.per_turn)


def self_attention(nc, d, qs, attn, rel):
    with ExitStack() as ctx:
        def sb(name, shape, dt=F32):
            return ctx.enter_context(nc.sbuf_tensor(name, shape, dt))

        def ps(name, shape):
            return ctx.enter_context(nc.psum_tensor(name, shape, F32))

        def sem(name):
            return ctx.enter_context(nc.semaphore(name))

        wk = sb("wk", [P, HALVES, E])
        wv = sb("wv", [P, HALVES, E])
        bk = sb("bk", [P, HALVES])
        bvrow = sb("bvrow", [1, E])
        ones = sb("ones", [1, P])
        head_mask = sb("head_mask", [P, HH])
        query_mask = sb("query_mask", [P, QG])
        out_mask = sb("out_mask", [P, 2 * P])
        relv_far = sb("relv_far", [P, 2, D])
        ident = sb("ident", [P, P])
        relk = sb("relk", [P, TKW])
        relv = sb("relv", [P, TVZ * D])

        xT = sb("xT", [P, HALVES, S])
        kT = sb("kT", [P, HALVES, S])
        qT = sb("qT", [P, HALVES, S])
        qrep = sb("qrep", [P, 2 * H, S])
        v1 = sb("v1", [P, KT, HALVES, P + KT])
        qdiag = [sb(f"qdiag{i}", [P, 2 * HALVES, QG, HH]) for i in range(2)]
        negmax = [sb(f"negmax{i}", [P, 1]) for i in range(2)]
        probs = [sb(f"probs{i}", [P, S]) for i in range(2)]
        probsT = [sb(f"probsT{i}", [P, KT, P]) for i in range(2)]
        picked = [sb(f"picked{i}", [P, 2 * P]) for i in range(2)]
        tile_sums = sb("tile_sums", [P, NG, KT])
        far = sb("far", [P, NG])
        far_out = sb("far_out", [P, NG, D])
        sum_inv = sb("sum_inv", [P, NG])
        heads_out = sb("heads_out", [P, NG, 2, D])

        psP = [ps(f"psP{i}", [P, S]) for i in range(2)]
        psS = [ps(f"psS{i}", [P, S]) for i in range(2)]
        psT = [ps(f"psT{i}", [P, KT, P]) for i in range(2)]
        psO = [ps(f"psO{i}", [P, S]) for i in range(2)]

        consts_in = sem("consts_in")
        q_in = sem("q_in")
        qrep_in = sem("qrep_in")
        x_in = sem("x_in")
        projected = sem("projected")
        kept_dve = sem("kept_dve")
        kept_act = sem("kept_act")
        ones_set = sem("ones_set")
        qdiag_ready = sem("qdiag_ready")
        scores_ready = sem("scores_ready")
        max_ready = sem("max_ready")
        probs_ready = sem("probs_ready")
        transposed = sem("transposed")
        probsT_ready = sem("probsT_ready")
        out_ready = sem("out_ready")
        out_read = sem("out_read")
        picked_ready = sem("picked_ready")
        reduced = sem("reduced")
        finish_step = sem("finish_step")
        normed = sem("normed")
        out_free = sem("out_free")
        stored = sem("stored")

        loads = [
            (wk, d["a_wkT"].rearrange("(a p) o -> p a o", p=P)),
            (bk, d["a_bk"]), (bvrow, d["a_bv"]),
            (wv, d["a_wvT"].rearrange("(a p) o -> p a o", p=P)),
            (head_mask, d["head_mask"]), (query_mask, d["query_mask"]),
            (out_mask, d["out_mask"]), (relv_far, d["relv_far"]), (ident, d["ident"]),
            (relk, d["relk"]), (relv, d["relv"]),
        ]
        N_CONST = 16 * len(loads)
        steps = [("k", 0), ("k", 1)] + [("v", t) for t in range(KT)]
        HALF = len(steps) // 2

        HP = P // HALVES
        GT = P // QG

        def near_tiles(tile):
            return [t for t in range(KT) if abs(t - tile) <= 1]

        def window(kind, n):
            return kT[:, n, :] if kind == "k" else v1[:, n, :, 0:P]

        block = ctx.enter_context(nc.Block())

        @block.sync
        def _(sp):
            for dst, src in loads:
                sp.dma_start(dst[:], src).then_inc(consts_in, 16)
            x_in_dram = d["a_xT"].rearrange("b (a p) s -> p (b a) s", p=P)
            q_dram = qs.rearrange("b (a p) s -> p (b a) s", p=P)
            sp.sem_inc(out_free, 1)

            def load_x(b):
                sp.dma_start(xT[:], x_in_dram[:, bass.ds(b * HALVES, HALVES), :]).then_inc(x_in, 16)

            def load_q(b):
                sp.dma_start(qT[:], q_dram[:, bass.ds(b * HALVES, HALVES), :]).then_inc(q_in, 16)

            def load_qrep(b, slot):
                head = qs[:, bass.ds(b * D, D), :].rearrange("h e s -> e h s")
                for j in range(QG):
                    sp.dma_start(qrep[j * D:(j + 1) * D, bass.ds(slot * H, H), :], head).then_inc(qrep_in, 16)

            def store(b):
                sp.wait_ge(normed, b + 1)
                for a in range(HALVES):
                    for j in range(QG):
                        rows = slice((a * QG + j) * HH, (a * QG + j + 1) * HH)
                        out = attn[bass.ds(b, 1), j::QG, a * P:(a + 1) * P].rearrange("b g (h e) -> (b h) g e", e=D)
                        sp.dma_start(out, heads_out[rows, :, 1, :]).then_inc(stored, 16)
                        out = rel[a * HH:(a + 1) * HH, j::QG, bass.ds(b * D, D)]
                        sp.dma_start(out, heads_out[rows, :, 0, :]).then_inc(stored, 16)
                sp.wait_ge(stored, 2 * HALVES * QG * 16 * (b + 1))
                sp.sem_inc(out_free, 1)

            load_x(0)
            load_q(0)
            load_qrep(0, 0)
            with sp.Fori(0, B - 1) as b:
                sp.wait_ge(qdiag_ready, b * NG + 1)
                load_qrep(b + 1, (b + 1) % 2)
                sp.wait_ge(projected, (b + 1) * len(steps))
                load_x(b + 1)
                sp.wait_ge(qdiag_ready, (b + 1) * NG)
                load_q(b + 1)
                store(b)
            store(B - 1)

        @block.gpsimd
        def _(pool):
            pool.memset(v1[:, :, :, P:], 0.0).then_inc(ones_set, 1)
            pool.wait_ge(ones_set, 1)
            for t in range(KT):
                pool.memset(v1[:, t, :, P + t:P + t + 1], 1.0).then_inc(ones_set, 1)
            pool.memset(ones[:], 1.0).then_inc(ones_set, 1)
            pool.wait_ge(consts_in, N_CONST)

            def build(i, g, n, first, slot):
                if not first:
                    pool.wait_ge(scores_ready, g - 1)
                q0 = i * QG
                for a in range(HALVES):
                    nc.gpsimd.tensor_tensor(
                        qdiag[n][:, a, :, :],
                        qT[:, a, bass.ds(q0, QG)].unsqueeze(2).to_broadcast([P, QG, HH]),
                        head_mask[:].unsqueeze(1).to_broadcast([P, QG, HH]), ALU.mult)
                nc.gpsimd.tensor_tensor(
                    qdiag[n][:, HALVES:, :, :],
                    qrep[:, bass.ds(slot * H, H), bass.ds(q0, QG)].rearrange("p (a h) j -> p a j h", a=HALVES),
                    query_mask[:].unsqueeze(1).unsqueeze(3).to_broadcast([P, HALVES, QG, HH]), ALU.mult)\
                    .then_inc(qdiag_ready, 1)

            with pool.Fori(0, B) as b:
                slot = b % 2
                pool.wait_ge(q_in, b * 16 + 16)
                pool.wait_ge(qrep_in, (b + 1) * 16 * QG)
                pool.wait_ge(projected, (b + 1) * len(steps))
                build(0, None, 0, True, slot)
                build(1, None, 1, True, slot)
                with pool.Fori(1, NG // 2) as t:
                    build(t * 2, b * NG + t * 2, 0, False, slot)
                    build(t * 2 + 1, b * NG + t * 2 + 1, 1, False, slot)

        @block.tensor
        def _(pe):
            pe.wait_ge(consts_in, N_CONST)
            pe.wait_ge(ones_set, KT + 2)

            def project(b):
                pe.wait_ge(x_in, b * 16 + 16)
                for n, (kind, m) in enumerate(steps):
                    if n >= 2:
                        pe.wait_ge(kept_act if n % 2 else kept_dve, b * HALF + n // 2)
                    dst = psP[n % 2]
                    for a in range(HALVES):
                        if kind == "v":
                            nc.tensor.matmul(dst[:, 0:E], xT[:, a, m * P:(m + 1) * P], wv[:, a, :],
                                             start=a == 0, stop=False)
                        else:
                            mm = nc.tensor.matmul(dst[:], wk[:, a, m * P:(m + 1) * P], xT[:, a, :], start=a == 0, stop=a == HALVES - 1)
                    if kind == "v":
                        mm = nc.tensor.matmul(dst[:, 0:E], ones[:], bvrow[:], start=False, stop=True)
                    mm.then_inc(projected, 1)

            def scores(i, g, n, first=False):
                pe.wait_ge(qdiag_ready, g + 1)
                if not first:
                    pe.wait_ge(probs_ready, g - 1)
                for a in range(HALVES):
                    nc.tensor.matmul(psS[n][a * HP:(a + 1) * HP, :], qdiag[n][:, a, :, :].rearrange("p j h -> p (j h)"),
                                     kT[:, a, :], start=True, stop=False)
                nc.tensor.matmul(psS[n][:], qdiag[n][:, HALVES:, :, :].rearrange("p a j h -> p (a j h)"),
                                 relk[:, bass.ds(S - QG - i * QG, S)], start=False, stop=True).then_inc(scores_ready, 1)

            def transpose(g, n):
                pe.wait_ge(probs_ready, g + 1)
                for t in range(KT):
                    mm = nc.tensor.transpose(psT[n][:, t, :], probs[n][:, t * P:(t + 1) * P], ident[:])
                mm.then_inc(transposed, 1)

            def outputs(i, g, n, near, first=False):
                pe.wait_ge(probsT_ready, g + 1)
                if not first:
                    pe.wait_ge(out_read, g - 1)
                for t in range(KT):
                    for a in range(HALVES):
                        rows = slice(a * HP, (a + 1) * HP)
                        nc.tensor.matmul(psO[n][rows, P:OW], probsT[n][:, t, rows], v1[:, t, a, :], start=t == 0, stop=t == KT - 1)
                for t in near:
                    mm = nc.tensor.matmul(psO[n][:, 0:P], probsT[n][:, t, :],
                                          relv[:, bass.ds((i * QG + (KT - 1 - t) * P) * D, P)],
                                          start=t == near[0], stop=t == near[-1])
                mm.then_inc(out_ready, 1)

            with pe.Fori(0, B) as b:
                project(b)
                g = b * NG
                pe.wait_ge(kept_dve, b * HALF + HALF)
                pe.wait_ge(kept_act, b * HALF + HALF)
                scores(0, g, 0, first=True)
                scores(1, g + 1, 1, first=True)
                transpose(g, 0)
                scores(2, g + 2, 0)
                transpose(g + 1, 1)
                outputs(0, g, 0, near_tiles(0), first=True)
                scores(3, g + 3, 1)
                transpose(g + 2, 0)
                outputs(1, g + 1, 1, near_tiles(0), first=True)
                for tile in range(KT):
                    near = near_tiles(tile)
                    with pe.Fori(max(2, tile * GT // 2 + 1), min((tile + 1) * GT // 2 + 1, NG // 2)) as t:
                        scores(t * 2, g + t * 2, 0)
                        transpose(g + t * 2 - 1, 1)
                        outputs(t * 2 - 2, g + t * 2 - 2, 0, near)
                        scores(t * 2 + 1, g + t * 2 + 1, 1)
                        transpose(g + t * 2, 0)
                        outputs(t * 2 - 1, g + t * 2 - 1, 1, near)
                transpose(g + NG - 1, 1)
                outputs(NG - 2, g + NG - 2, 0, near)
                outputs(NG - 1, g + NG - 1, 1, near)

        @block.scalar
        def _(act):
            act.wait_ge(consts_in, N_CONST)

            def exp(g, n):
                act.wait_ge(max_ready, g + 1)
                nc.scalar.activation(probs[n][:], psS[n][:], ACT.Exp, bias=negmax[n][:]).then_inc(probs_ready, 1)

            def keep(g, n, first=False):
                act.wait_ge(transposed, g + 1)
                if not first:
                    act.wait_ge(out_ready, g - 1)
                nc.scalar.activation(probsT[n][:], psT[n][:], ACT.Copy).then_inc(probsT_ready, 1)

            with act.Fori(0, B) as b:
                for n, (kind, m) in enumerate(steps):
                    if n % 2 == 0:
                        continue
                    act.wait_ge(projected, b * len(steps) + n + 1)
                    if kind == "v":
                        mm = nc.scalar.activation(window(kind, m), psP[1][:, 0:E].rearrange("p (a c) -> p a c", a=HALVES), ACT.Copy)
                    else:
                        mm = nc.scalar.activation(window(kind, m), psP[1][:], ACT.Identity, bias=bk[:, m:m + 1])
                    mm.then_inc(kept_act, 1)
                g = b * NG
                exp(g, 0)
                exp(g + 1, 1)
                keep(g, 0, first=True)
                exp(g + 2, 0)
                keep(g + 1, 1, first=True)
                exp(g + 3, 1)
                keep(g + 2, 0)
                with act.Fori(2, NG // 2) as t:
                    exp(g + t * 2, 0)
                    keep(g + t * 2 - 1, 1)
                    exp(g + t * 2 + 1, 1)
                    keep(g + t * 2, 0)
                keep(g + NG - 1, 1)

        @block.vector
        def _(dve):
            dve.wait_ge(consts_in, N_CONST)

            def rowmax(g, n):
                dve.wait_ge(scores_ready, g + 1)
                nc.vector.tensor_reduce(negmax[n][:], psS[n][:], AX_X, ALU.max, negate=True).then_inc(max_ready, 1)

            def pick(i, g, n):
                dve.wait_ge(out_ready, g + 1)
                nc.vector.tensor_copy(tile_sums[:, bass.ds(i, 1), :].rearrange("p g t -> p (g t)"), psO[n][:, 2 * P:OW])
                nc.vector.tensor_tensor(picked[n][:], psO[n][:, 0:2 * P], out_mask[:], ALU.mult).then_inc(out_read, 1)
                dve.wait_ge(out_read, g + 1)
                nc.vector.tensor_reduce(heads_out[:, bass.ds(i, 1), :, :].rearrange("p g i e -> p (g i) e"),
                                        picked[n][:].rearrange("p (i c e) -> p i e c", i=2, e=D), AX_X, ALU.add).then_inc(reduced, 1)

            def finish(b):
                chain = Chain(dve, finish_step, 4, b)
                dve.wait_ge(reduced, b * NG + NG)
                half = NG // 2
                nc.vector.tensor_tensor(far[:, 0:GT], tile_sums[:, 0:GT, 2], tile_sums[:, 0:GT, 3], ALU.add)
                nc.vector.tensor_copy(far[:, GT:2 * GT], tile_sums[:, GT:2 * GT, 3])
                nc.vector.tensor_copy(far[:, 2 * GT:3 * GT], tile_sums[:, 2 * GT:3 * GT, 0])
                nc.vector.tensor_tensor(far[:, 3 * GT:], tile_sums[:, 3 * GT:, 0], tile_sums[:, 3 * GT:, 1], ALU.add)
                chain.link(nc.vector.tensor_reduce(sum_inv[:], tile_sums[:], AX_X, ALU.add))
                nc.vector.reciprocal(sum_inv[:], sum_inv[:])
                for i in range(2):
                    last = nc.vector.tensor_tensor(
                        far_out[:, i * half:(i + 1) * half, :], far[:, i * half:(i + 1) * half].unsqueeze(2).to_broadcast([P, half, D]),
                        relv_far[:, i, :].unsqueeze(1).to_broadcast([P, half, D]), ALU.mult)
                chain.link(last)
                chain.link(nc.vector.tensor_tensor(heads_out[:, :, 0, :], heads_out[:, :, 0, :], far_out[:], ALU.add))
                chain.link(nc.vector.tensor_tensor(
                    heads_out[:].rearrange("p g i e -> p g (i e)"), heads_out[:].rearrange("p g i e -> p g (i e)"),
                    sum_inv[:].unsqueeze(2).to_broadcast([P, NG, 2 * D]), ALU.mult))
                dve.sem_inc(normed, 1)
                chain.end()

            with dve.Fori(0, B) as b:
                for n, (kind, m) in enumerate(steps):
                    if n % 2:
                        continue
                    dve.wait_ge(projected, b * len(steps) + n + 1)
                    if kind == "v":
                        mm = nc.vector.tensor_copy(window(kind, m), psP[0][:, 0:E].rearrange("p (a c) -> p a c", a=HALVES))
                    else:
                        mm = nc.vector.tensor_scalar(window(kind, m), psP[0][:], bk[:, m:m + 1], None, ALU.add)
                    mm.then_inc(kept_dve, 1)
                g = b * NG
                dve.wait_ge(out_free, b + 1)
                rowmax(g, 0)
                rowmax(g + 1, 1)
                with dve.Fori(1, NG // 2) as t:
                    rowmax(g + t * 2, 0)
                    pick(t * 2 - 2, g + t * 2 - 2, 0)
                    rowmax(g + t * 2 + 1, 1)
                    pick(t * 2 - 1, g + t * 2 - 1, 1)
                pick(NG - 2, g + NG - 2, 0)
                pick(NG - 1, g + NG - 1, 1)
                finish(b)


def take_moments(nc, r, stats, moments, engine, step, base, moments_ready):
    for t in range(QT):
        last = nc.vector.bn_stats(stats[:, t, :], r[:, t, :])
    last.then_inc(step, 1)
    engine.wait_ge(step, base + 1)
    engine.sem_inc(step, 1)
    for t in range(QT):
        last = nc.vector.bn_aggr(moments[:, t, :], stats[:, t, :])
    last.then_inc(moments_ready, 1)


def deviation(nc, act, turn, moments, rstd, eps, moments_ready, deviation_ready):
    act.wait_ge(moments_ready, turn + 1)
    nc.scalar.activation(rstd[:], moments[:, :, 1], ACT.Sqrt, bias=eps[:]).then_inc(deviation_ready, 1)


def apply_norm(nc, r, out, moments, rstd, engine, step, base, turn, deviation_ready):
    engine.wait_ge(deviation_ready, turn + 1)
    nc.vector.reciprocal(rstd[:], rstd[:]).then_inc(step, 1)
    engine.wait_ge(step, base + 3)
    for t in range(QT):
        last = nc.vector.tensor_scalar(out[:, t, :], r[:, t, :], moments[:, t, 0:1], rstd[:, t:t + 1],
                                       ALU.subtract, ALU.mult)
    return last


def cross_attention(nc, d, attn, rel, x2_rows, acc_rows, gate_scores):
    with ExitStack() as ctx:
        def sb(name, shape, dt=F32):
            return ctx.enter_context(nc.sbuf_tensor("x_" + name, shape, dt))

        def ps(name, shape):
            return ctx.enter_context(nc.psum_tensor("x_" + name, shape, F32))

        def sem(name):
            return ctx.enter_context(nc.semaphore("x_" + name))

        PAIRS = H // 2
        wo, wq, wk, wv, wo2 = (sb(n, [P, HALVES, E]) for n in ("wo", "wq", "wk", "wv", "wo2"))
        wg = sb("wg", [P, HALVES, NX])
        bo, bo2 = sb("bo", [P, E]), sb("bo2", [P, E])
        bv, ones = sb("bv", [1, E]), sb("ones", [1, P])
        bq, bqs, bk = (sb(n, [P, HALVES]) for n in ("bq", "bqs", "bk"))
        ident = sb("ident", [P, P])
        half_mask = sb("half_mask", [P, HH])
        pair_mask = sb("pair_mask", [P, 2 * D])
        mask_in = sb("mask_in", [P, QT, SK], I32)
        keep = sb("keep", [P, QT, SK])
        fill = sb("fill", [P, QT, SK])
        ctxT = sb("ctxT", [P, HALVES, B // 2, 2, SK])
        kT = sb("kT", [P, HALVES, B, SK])
        v = sb("v", [P, B, E])
        kdiag = sb("kdiag", [P, HALVES, HH, SK])
        vdiag = sb("vdiag", [P, PAIRS, 2 * D])
        x_sb, attn_sb, rel_sb, xb, both = (sb(n, [P, QT, E]) for n in ("x_sb", "attn_sb", "rel_sb", "xb", "both"))
        r1, r2, x1, x2 = (sb(n, [P, QT, E]) for n in ("r1", "r2", "x1", "x2"))
        x1b = sb("x1b", [P, 2, QT, E])
        aT, x1T, qT, oT, x2T = (sb(n, [P, HALVES, S]) for n in ("aT", "x1T", "qT", "oT", "x2T"))
        sc = [sb(f"sc{i}", [P, H, SK]) for i in range(2)]
        pr = [sb(f"pr{i}", [P, H, SK]) for i in range(2)]
        prT = sb("prT", [P, PAIRS, QT, P])
        negmax, inv = (sb(n, [P, QT, H]) for n in ("negmax", "inv"))
        stats1, stats2 = sb("stats1", [P, QT, 6]), sb("stats2", [P, QT, 6])
        moments1, moments2 = sb("moments1", [P, QT, 2]), sb("moments2", [P, QT, 2])
        rstd1, rstd2 = sb("rstd1", [P, QT]), sb("rstd2", [P, QT])
        eneg = sb("eneg", [P, QT, NX])
        eps = sb("eps", [P, 1])
        zeros = sb("zeros", [P, QT, E])

        bankT = [ps(f"bankT{i}", [P, 4, P]) for i in range(2)]
        bankR = [ps(f"bankR{i}", [P, 2, E]) for i in range(2)]
        bankS = [ps(f"bankS{i}", [P, H, SK]) for i in range(2)]

        w_in = sem("w_in")
        ctx_in = sem("ctx_in")
        zeros_ready = sem("zeros_ready")
        ones_ready = sem("ones_ready")
        eps_ready = sem("eps_ready")
        mask_ready = sem("mask_ready")
        ctx_projected = sem("ctx_projected")
        ctx_kept = sem("ctx_kept")
        attn_in = sem("attn_in")
        x_in = sem("x_in")
        both_ready = sem("both_ready")
        xb_ready = sem("xb_ready")
        x1b_ready = sem("x1b_ready")
        bankT_full = sem("bankT_full")
        bankT_empty = [sem(f"bankT_empty{i}") for i in range(2)]
        bankR_full = sem("bankR_full")
        bankR_empty = [sem(f"bankR_empty{i}") for i in range(2)]
        bankS_full = sem("bankS_full")
        bankS_empty = sem("bankS_empty")
        kdiag_ready = sem("kdiag_ready")
        vdiag_ready = sem("vdiag_ready")
        filled = sem("filled")
        max_ready = sem("max_ready")
        shifted = sem("shifted")
        exp_ready = sem("exp_ready")
        weights_ready = sem("weights_ready")
        x1_ready = sem("x1_ready")
        x2_ready = sem("x2_ready")
        x2_free = sem("x2_free")
        stored = sem("stored")
        zero_stored = sem("zero_stored")
        soft_step = sem("soft_step")
        gate_step = sem("gate_step")
        norm1_step, norm2_step = sem("norm1_step"), sem("norm2_step")
        moments1_ready, moments2_ready = sem("moments1_ready"), sem("moments2_ready")
        deviation1_ready, deviation2_ready = sem("deviation1_ready"), sem("deviation2_ready")

        weights = [
            (ident, d["ident"]), (wk, d["x_wkT"].rearrange("(a p) o -> p a o", p=P)), (bk, d["x_bk"]),
            (wv, d["x_wvT"].rearrange("(a p) o -> p a o", p=P)), (bv, d["x_bv"]),
            (wo, d["a_woT"].rearrange("(a p) o -> p a o", p=P)), (bo, d["a_bo"]),
            (wq, d["x_wqT"].rearrange("(a p) o -> p a o", p=P)), (bq, d["x_bq"]),
            (wo2, d["x_woT"].rearrange("(a p) o -> p a o", p=P)), (bo2, d["x_bo"]),
            (wg, d["gate_wT"].rearrange("(a p) o -> p a o", p=P)),
            (half_mask, d["half_mask"]), (pair_mask, d["pair_mask"]),
            (mask_in, d["mask"].rearrange("(t p) k -> p t k", p=P)),
        ]
        N_W = 16 * len(weights)

        class Uses:

            def __init__(self, first, turn):
                self.first, self.turn = first, turn

            def at(self, b, name, x, z):
                if b is None:
                    return self.first.index(name)
                names = [n for n in self.turn if (x or n[0] != "x") and (z or n[0] != "z")]
                n = names.index(name) + len(self.first)
                if isinstance(b, int) and b == 0:
                    return n
                return b * len(self.turn) + n - sum(m[0] == "z" for m in self.turn)

        usesT = Uses(["x_a", "x_x1", "x_q"], ["x_a", "w0", "w1", "z_x2", "w2", "w3", "x_x1", "out", "x_q"])
        usesR = Uses(["x_proj"], ["x_proj", "z_gate", "proj"])

        def flat(bank):
            return bank[:].rearrange("p a b -> p (a b)")

        def rows(dram, b):
            return dram[bass.ds(b * S, S), :].rearrange("(t p) e -> p t e", p=P)

        block = ctx.enter_context(nc.Block())

        @block.sync
        def _(sp):
            for dst, src in weights:
                sp.dma_start(dst[:], src).then_inc(w_in, 16)

            def load_ctx(half):
                for a in range(HALVES):
                    sp.dma_start(ctxT[:, a], d["ctxT"][a * P:(a + 1) * P, half * (B // 2):(half + 1) * (B // 2)]).then_inc(ctx_in, 16)

            def load_attn(b):
                sp.dma_start(attn_sb[:], rows(attn, b)).then_inc(attn_in, 16)
                sp.dma_start(rel_sb[:], rows(rel, b)).then_inc(attn_in, 16)

            def load_x(b):
                sp.dma_start(x_sb[:], rows(d["x"], b)).then_inc(x_in, 16)

            def store(b):
                sp.wait_ge(x2_ready, b + 1)
                for dram in (x2_rows, acc_rows[0]):
                    sp.dma_start(rows(dram, b), x2[:]).then_inc(stored, 16)
                sp.dma_start(rows(acc_rows[1], b), zeros[:]).then_inc(stored, 16)
                sp.wait_ge(stored, (b + 1) * 48)
                sp.sem_inc(x2_free, 1)

            load_ctx(0)
            load_attn(0)
            load_x(0)
            sp.sem_inc(x2_free, 1)
            sp.wait_ge(ctx_projected, CTX_STEPS)
            load_ctx(1)
            sp.wait_ge(zeros_ready, 1)
            for dram in (x2_rows, *acc_rows):
                sp.dma_start(dram[TOK:TOK + CAP, :].rearrange("(t p) e -> p t e", p=P), zeros[:, 0:CAP // P, :])\
                    .then_inc(zero_stored, 16)

            def load(b):
                sp.wait_ge(both_ready, b)
                load_attn(b)
                sp.wait_ge(xb_ready, b)
                load_x(b)

            load(1)
            with sp.Fori(2, B) as b:
                load(b)
                store(b - 2)
            for b in (B - 2, B - 1):
                store(b)
            sp.wait_ge(zero_stored, 48)

        @block.gpsimd
        def _(pool):
            pool.memset(zeros[:], 0.0).then_inc(zeros_ready, 1)
            pool.memset(ones[:], 1.0).then_inc(ones_ready, 1)
            pool.memset(eps[:], EPS).then_inc(eps_ready, 1)
            pool.wait_ge(w_in, N_W)
            pool.wait_ge(mask_ready, 1)

            def inputs(b):
                pool.wait_ge(attn_in, b * 32 + 32)
                nc.gpsimd.tensor_tensor(both[:], attn_sb[:], rel_sb[:], ALU.add).then_inc(both_ready, 1)
                pool.wait_ge(x_in, b * 16 + 16)
                nc.gpsimd.tensor_tensor(xb[:], x_sb[:], bo[:].unsqueeze(1).to_broadcast([P, QT, E]), ALU.add).then_inc(xb_ready, 1)

            def residual(b):
                pool.wait_ge(x1_ready, b + 1)
                nc.gpsimd.tensor_tensor(x1b[:, bass.ds(b % 2, 1)].rearrange("p i t e -> p (i t) e"), x1[:],
                                        bo2[:].unsqueeze(1).to_broadcast([P, QT, E]), ALU.add).then_inc(x1b_ready, 1)

            def diag_k(b):
                for a in range(HALVES):
                    mm = nc.gpsimd.tensor_tensor(
                        kdiag[:, a, :, :], kT[:, a, bass.ds(b, 1), :].to_broadcast([P, HH, SK]),
                        half_mask[:].unsqueeze(2).to_broadcast([P, HH, SK]), ALU.mult)
                mm.then_inc(kdiag_ready, 1)

            def diag_v(b):
                nc.gpsimd.tensor_tensor(
                    vdiag[:], v[:, bass.ds(b, 1), :].rearrange("p b (g c) -> p (b g) c", c=2 * D),
                    pair_mask[:].unsqueeze(1).to_broadcast([P, PAIRS, 2 * D]), ALU.mult).then_inc(vdiag_ready, 1)

            def tiles(b, t0):
                for t in (t0, t0 + 1):
                    pool.wait_ge(bankS_empty, b * QT + t + 3)
                    nc.gpsimd.tensor_tensor(sc[t % 2][:], sc[t % 2][:], fill[:, t, :].unsqueeze(1).to_broadcast([P, H, SK]),
                                            ALU.add).then_inc(filled, 1)
                for t in (t0, t0 + 1):
                    pool.wait_ge(max_ready, b * QT + t + 1)
                    nc.gpsimd.tensor_tensor(sc[t % 2][:], sc[t % 2][:], negmax[:, t, :].unsqueeze(2).to_broadcast([P, H, SK]),
                                            ALU.add).then_inc(shifted, 1)

            def turn(b, x=True, z=True):
                tiles(b, 0)
                tiles(b, 2)
                if x:
                    residual(b + 1)
                    diag_k(b + 1)
                    pool.wait_ge(bankT_full, 2 * usesT.at(b, "out", x, z) + 2)
                    diag_v(b + 1)

            def before(b):
                inputs(b)

            before(0)
            pool.wait_ge(ctx_kept, 2 * CTX_STEPS)
            diag_k(0)
            diag_v(0)
            residual(0)
            before(1)
            turn(0, z=False)
            with pool.Fori(1, B - 1) as b:
                before(b + 1)
                turn(b)
            turn(B - 1, x=False)

        @block.tensor
        def _(pe):
            pe.wait_ge(w_in, N_W)
            pe.wait_ge(ones_ready, 1)
            n = 0
            for half in range(2):
                pe.wait_ge(ctx_in, 32 * (half + 1))
                for m in range(HALVES):
                    if n >= 2:
                        pe.wait_ge(ctx_kept, n - 1)
                    for a in range(HALVES):
                        mm = nc.tensor.matmul(flat(bankT[n % 2]), wk[:, a, m * P:(m + 1) * P], ctxT[:, a, :, 0, :],
                                              start=a == 0, stop=a == HALVES - 1)
                    mm.then_inc(ctx_projected, 1)
                    n += 1
                for c in range(B // 4):
                    pe.wait_ge(ctx_kept, n - 1)
                    for i in range(2):
                        dst = flat(bankT[n % 2])[:, i * E:(i + 1) * E]
                        for a in range(HALVES):
                            nc.tensor.matmul(dst, ctxT[:, a, 2 * c + i].rearrange("p a b -> p (a b)"), wv[:, a, :], start=a == 0, stop=False)
                        mm = nc.tensor.matmul(dst, ones[:], bv[:], start=False, stop=True)
                    mm.then_inc(ctx_projected, 1)
                    n += 1
            pe.wait_ge(ctx_kept, n)

            def take(kind, at, i):
                banks, empty = {"T": (bankT, bankT_empty), "R": (bankR, bankR_empty)}[kind]
                pe.wait_ge(empty[i], at + 1)
                return banks[i]

            def transpose_rows(src, at):
                for a in range(HALVES):
                    bank = take("T", at, a)
                    for t in range(QT):
                        mm = nc.tensor.transpose(bank[:, t, :], src[:, t, a * P:(a + 1) * P], ident[:])
                    mm.then_inc(bankT_full, 1)

            def in_sbuf(at):
                for i in range(2):
                    pe.wait_ge(bankT_empty[i], at + 2)

            def project(src, w, cols, at):
                for i in range(2):
                    bank = take("R", at, i)
                    for u in range(2):
                        t = 2 * i + u
                        for a in range(HALVES):
                            mm = nc.tensor.matmul(bank[:, u, 0:cols], src[:, a, t * P:(t + 1) * P], w[:, a, :],
                                                  start=a == 0, stop=a == HALVES - 1)
                    mm.then_inc(bankR_full, 1)

            def sum_transposed(b, at):
                pe.wait_ge(both_ready, b + 1)
                transpose_rows(both, at)

            def projected(atT, atR):
                in_sbuf(atT)
                project(aT, wo, E, atR)

            def x1_transposed(b, at):
                pe.wait_ge(x1_ready, b + 1)
                transpose_rows(x1, at)

            def queries(at1, at):
                in_sbuf(at1)
                for m in range(HALVES):
                    bank = take("T", at, m)
                    for a in range(HALVES):
                        mm = nc.tensor.matmul(flat(bank), wq[:, a, m * P:(m + 1) * P], x1T[:, a, :],
                                              start=a == 0, stop=a == HALVES - 1)
                    mm.then_inc(bankT_full, 1)

            def scores(b, t):
                pe.wait_ge(bankS_empty, b * QT + t + 1)
                for a in range(HALVES):
                    mm = nc.tensor.matmul(bankS[t % 2][:, a * HH:(a + 1) * HH, :].rearrange("p h k -> p (h k)"),
                                          qT[:, a, t * P:(t + 1) * P], kdiag[:, a, :, :].rearrange("p h k -> p (h k)"),
                                          start=True, stop=True)
                mm.then_inc(bankS_full, 1)

            def transpose_weights(b, t, at):
                pe.wait_ge(weights_ready, b * QT + t + 1)
                for c in range(2):
                    bank = take("T", at, c)
                    for g in range(4):
                        h = 2 * (4 * c + g)
                        mm = nc.tensor.transpose(bank[:, g, :], pr[t % 2][:, h:h + 2, :].rearrange("p h k -> p (h k)"), ident[:])
                    mm.then_inc(bankT_full, 1)

            def outputs(b, at3, at):
                pe.wait_ge(vdiag_ready, b + 1)
                in_sbuf(at3)
                for c in range(2):
                    bank = take("T", at, c)
                    for g in range(4):
                        mm = nc.tensor.matmul(flat(bank)[g * 2 * D:(g + 1) * 2 * D, :], vdiag[:, 4 * c + g, :],
                                              prT[:, 4 * c + g, :, :].rearrange("p t q -> p (t q)"), start=True, stop=True)
                    mm.then_inc(bankT_full, 1)

            def turn(b, x=True, z=True):
                def atT(name):
                    return usesT.at(b, name, x, z)

                def atR(name):
                    return usesR.at(b, name, x, z)

                pe.wait_ge(kdiag_ready, b + 1)
                in_sbuf(usesT.at(None, "x_q", True, True) if isinstance(b, int) and b == 0
                        else atT("x_a" if x else "w0") - 1)
                scores(b, 0)
                scores(b, 1)
                if x:
                    sum_transposed(b + 1, atT("x_a"))
                transpose_weights(b, 0, atT("w0"))
                transpose_weights(b, 1, atT("w1"))
                scores(b, 2)
                scores(b, 3)
                if z:
                    pe.wait_ge(x2_ready, b)
                    transpose_rows(x2, atT("z_x2"))
                if x:
                    projected(atT("x_a"), atR("x_proj"))
                transpose_weights(b, 2, atT("w2"))
                transpose_weights(b, 3, atT("w3"))
                if z:
                    in_sbuf(atT("z_x2"))
                    project(x2T, wg, NX, atR("z_gate"))
                if x:
                    x1_transposed(b + 1, atT("x_x1"))
                outputs(b, atT("w3"), atT("out"))
                if x:
                    queries(atT("x_x1"), atT("x_q"))
                in_sbuf(atT("out"))
                project(oT, wo2, E, atR("proj"))

            def at0(name):
                return usesT.at(None, name, True, True)

            sum_transposed(0, at0("x_a"))
            projected(at0("x_a"), 0)
            x1_transposed(0, at0("x_x1"))
            queries(at0("x_x1"), at0("x_q"))
            turn(0, z=False)
            with pe.Fori(1, B - 1) as b:
                turn(b)
            turn(B - 1, x=False)
            pe.wait_ge(x2_ready, B)
            end = usesT.at(B - 1, "out", False, True) + 1
            transpose_rows(x2, end)
            in_sbuf(end)
            project(x2T, wg, NX, usesR.at(B - 1, "proj", False, True) + 1)

        @block.scalar
        def _(act):
            act.sem_inc(bankT_empty[0], 1)
            act.wait_ge(mask_ready, 1)
            act.wait_ge(eps_ready, 1)
            act.wait_ge(w_in, N_W)

            def keep_half(at, dst):
                act.wait_ge(bankT_full, 2 * at + 1)
                nc.scalar.activation(dst[:, 0, :], flat(bankT[0]), ACT.Copy).then_inc(bankT_empty[0], 1)

            def queries(at):
                act.wait_ge(bankT_full, 2 * at + 1)
                nc.scalar.activation(qT[:, 0, :], flat(bankT[0]), ACT.Identity, bias=bqs[:, 0:1], scale=SC).then_inc(bankT_empty[0], 1)

            def exp(b, t):
                act.wait_ge(shifted, b * QT + t + 1)
                nc.scalar.activation(pr[t % 2][:], sc[t % 2][:], ACT.Exp).then_inc(exp_ready, 1)

            def keep_weights(t, at):
                for c in range(2):
                    act.wait_ge(bankT_full, 2 * at + c + 1)
                    nc.scalar.activation(prT[:, 4 * c:4 * c + 4, t, :], bankT[c][:], ACT.Copy).then_inc(bankT_empty[c], 1)

            def gate(at):
                for i in range(2):
                    act.wait_ge(bankR_full, 2 * at + i + 1)
                    nc.scalar.activation(eneg[:, 2 * i:2 * i + 2, :], bankR[i][:, :, 0:NX], ACT.Exp, scale=-1.0).then_inc(bankR_empty[i], 1)

            def turn(b, x=True, z=True):
                def atT(name):
                    return usesT.at(b, name, x, z)

                if z:
                    deviation(nc, act, b - 1, moments2, rstd2, eps, moments2_ready, deviation2_ready)
                if x:
                    keep_half(atT("x_a"), aT)
                exp(b, 0)
                exp(b, 1)
                keep_weights(0, atT("w0"))
                keep_weights(1, atT("w1"))
                if z:
                    keep_half(atT("z_x2"), x2T)
                if x:
                    deviation(nc, act, b + 1, moments1, rstd1, eps, moments1_ready, deviation1_ready)
                exp(b, 2)
                exp(b, 3)
                keep_weights(2, atT("w2"))
                keep_weights(3, atT("w3"))
                if z:
                    gate(usesR.at(b, "z_gate", x, z))
                if x:
                    keep_half(atT("x_x1"), x1T)
                keep_half(atT("out"), oT)
                if x:
                    queries(atT("x_q"))

            keep_half(0, aT)
            deviation(nc, act, 0, moments1, rstd1, eps, moments1_ready, deviation1_ready)
            keep_half(1, x1T)
            queries(2)
            turn(0, z=False)
            with act.Fori(1, B - 1) as b:
                turn(b)
            turn(B - 1, x=False)
            deviation(nc, act, B - 1, moments2, rstd2, eps, moments2_ready, deviation2_ready)
            keep_half(usesT.at(B - 1, "out", False, True) + 1, x2T)
            gate(usesR.at(B - 1, "proj", False, True) + 1)

        @block.vector
        def _(dve):
            dve.sem_inc(bankT_empty[1], 1)
            dve.sem_inc(bankR_empty[0], 1)
            dve.sem_inc(bankR_empty[1], 1)
            dve.sem_inc(bankS_empty, 2)
            dve.wait_ge(w_in, N_W)
            nc.vector.tensor_scalar(bqs[:], bq[:], SC, None, ALU.mult)
            nc.vector.tensor_scalar(keep[:], mask_in[:], 0, None, ALU.not_equal)
            nc.vector.tensor_scalar(fill[:], mask_in[:], 0, NEG, ALU.is_equal, ALU.mult).then_inc(mask_ready, 1)
            n = 0
            for half in range(2):
                for m in range(HALVES):
                    n += 1
                    dve.wait_ge(ctx_projected, n)
                    nc.vector.tensor_scalar(
                        kT[:, m, half * (B // 2):(half + 1) * (B // 2), :].rearrange("p b k -> p (b k)"),
                        flat(bankT[(n - 1) % 2]), bk[:, m:m + 1], None, ALU.add).then_inc(ctx_kept, 1)
                for c in range(B // 4):
                    n += 1
                    dve.wait_ge(ctx_projected, n)
                    at = half * (B // 2) + 2 * c
                    nc.vector.tensor_copy(v[:, at:at + 2, :].rearrange("p b e -> p (b e)"), flat(bankT[(n - 1) % 2])).then_inc(ctx_kept, 1)
            dve.wait_ge(mask_ready, 1)

            def keep_half(at, dst):
                dve.wait_ge(bankT_full, 2 * at + 2)
                nc.vector.tensor_copy(dst[:, 1, :], flat(bankT[1])).then_inc(bankT_empty[1], 1)

            def queries(at):
                dve.wait_ge(bankT_full, 2 * at + 2)
                nc.vector.tensor_scalar(qT[:, 1, :], flat(bankT[1]), bq[:, 1:2], SC, ALU.add, ALU.mult).then_inc(bankT_empty[1], 1)

            def residual(at, x, r):
                for i in range(2):
                    dve.wait_ge(bankR_full, 2 * at + i + 1)
                    nc.vector.tensor_tensor(r[:, 2 * i:2 * i + 2, :], bankR[i][:], x(i), ALU.add).then_inc(bankR_empty[i], 1)
                for i in range(2):
                    dve.wait_ge(bankR_empty[i], at + 2)

            def first_moments(b, at):
                dve.wait_ge(xb_ready, b + 1)
                residual(at, lambda i: xb[:, 2 * i:2 * i + 2, :], r1)
                take_moments(nc, r1, stats1, moments1, dve, norm1_step, b * NORM_STEPS, moments1_ready)

            def first_norm(b):
                apply_norm(nc, r1, x1, moments1, rstd1, dve, norm1_step, b * NORM_STEPS, b, deviation1_ready).then_inc(x1_ready, 1)

            def second_moments(b, at):
                dve.wait_ge(x1b_ready, b + 1)
                residual(at, lambda i: x1b[:, bass.ds(b % 2, 1), 2 * i:2 * i + 2, :].rearrange("p o t e -> p (o t) e"), r2)
                take_moments(nc, r2, stats2, moments2, dve, norm2_step, b * NORM_STEPS, moments2_ready)

            def second_norm(b):
                dve.wait_ge(x2_free, b + 1)
                apply_norm(nc, r2, x2, moments2, rstd2, dve, norm2_step, b * NORM_STEPS, b, deviation2_ready).then_inc(x2_ready, 1)

            def take_scores(b, t):
                dve.wait_ge(bankS_full, b * QT + t + 1)
                nc.vector.tensor_tensor(sc[t % 2][:], bankS[t % 2][:], keep[:, t, :].unsqueeze(1).to_broadcast([P, H, SK]),
                                        ALU.mult).then_inc(bankS_empty, 1)

            def rowmax(b, t):
                dve.wait_ge(filled, b * QT + t + 1)
                nc.vector.tensor_reduce(negmax[:, t, :], sc[t % 2][:], AX_X, ALU.max, negate=True).then_inc(max_ready, 1)

            def divide(b, t):
                step = b * 2 * QT + 2 * t
                dve.wait_ge(exp_ready, b * QT + t + 1)
                nc.vector.tensor_reduce(inv[:, t, :], pr[t % 2][:], AX_X, ALU.add).then_inc(soft_step, 1)
                dve.wait_ge(soft_step, step + 1)
                nc.vector.reciprocal(inv[:, t, :], inv[:, t, :]).then_inc(soft_step, 1)
                dve.wait_ge(soft_step, step + 2)
                nc.vector.tensor_tensor(pr[t % 2][:], pr[t % 2][:], inv[:, t, :].unsqueeze(2).to_broadcast([P, H, SK]),
                                        ALU.mult).then_inc(weights_ready, 1)

            def gate(b, at):
                for i in range(2):
                    dve.wait_ge(bankR_empty[i], at + 2)
                nc.vector.tensor_scalar(eneg[:], eneg[:], 1.0, None, ALU.add).then_inc(gate_step, 1)
                dve.wait_ge(gate_step, 2 * b + 1)
                nc.vector.reciprocal(gate_scores[:, bass.ds(b * QT, QT), :], eneg[:]).then_inc(gate_step, 1)

            def turn(b, x=True, z=True):
                def atT(name):
                    return usesT.at(b, name, x, z)

                def atR(name):
                    return usesR.at(b, name, x, z)

                take_scores(b, 0)
                take_scores(b, 1)
                if z:
                    second_norm(b - 1)
                if x:
                    keep_half(atT("x_a"), aT)
                rowmax(b, 0)
                rowmax(b, 1)
                divide(b, 0)
                divide(b, 1)
                take_scores(b, 2)
                take_scores(b, 3)
                if z:
                    keep_half(atT("z_x2"), x2T)
                rowmax(b, 2)
                rowmax(b, 3)
                if x:
                    first_moments(b + 1, atR("x_proj"))
                    first_norm(b + 1)
                divide(b, 2)
                divide(b, 3)
                if z:
                    gate(b - 1, atR("z_gate"))
                if x:
                    keep_half(atT("x_x1"), x1T)
                keep_half(atT("out"), oT)
                if x:
                    queries(atT("x_q"))
                second_moments(b, atR("proj"))

            keep_half(0, aT)
            first_moments(0, 0)
            first_norm(0)
            keep_half(1, x1T)
            queries(2)
            turn(0, z=False)
            with dve.Fori(1, B - 1) as b:
                turn(b)
            turn(B - 1, x=False)
            second_norm(B - 1)
            keep_half(usesT.at(B - 1, "out", False, True) + 1, x2T)
            gate(B - 1, usesR.at(B - 1, "proj", False, True) + 1)


def route(nc, d, gate_scores, slot_token, slot_weight, slot_index, slot_scale):
    with ExitStack() as ctx:
        def sb(name, shape, dt=F32):
            return ctx.enter_context(nc.sbuf_tensor("r_" + name, shape, dt))

        def sem(name):
            return ctx.enter_context(nc.semaphore("r_" + name))

        G = NX // GE
        CH = 512 // NX
        bias = sb("bias", [P, NX])
        before = sb("before", [P, P])
        ones = sb("ones", [P, P])
        ident = sb("ident", [P, P])
        lower = sb("lower", [P, G, G])
        iota = sb("iota", [P, SLOT_B])
        token1 = sb("token1", [P, NT])
        row_empty = sb("row_empty", [P, 2 * NX])
        own_expert = sb("own_expert", [P, GE])

        sfc = sb("sfc", [P, NT, NX])
        hi, lo = sb("hi", [P, NT * G, 4]), sb("lo", [P, NT * G, 4])
        hi2, lo2, lo2b = (sb(n, [P, NT * G, 2]) for n in ("hi2", "lo2", "lo2b"))
        lo3, lo3b = sb("lo3", [P, NT * G]), sb("lo3b", [P, NT * G])
        gscore = sb("gscore", [P, NT, G])
        rank = sb("rank", [P, NT, G])
        work = sb("work", [P, NT, NX])
        work2 = sb("work2", [P, NT, NX])
        top = sb("top", [P, NT, 8])
        mask = sb("mask", [P, NT, NX])
        wsum = sb("wsum", [P, NT])
        ai, bi = sb("ai", [P, NT, NX], I32), sb("bi", [P, NT, NX], I32)
        first = [sb(f"first{i}", [P, CH, GE, SLOT_A]) for i in range(2)]
        second = [sb(f"second{i}", [P, 3, CH, GE, SLOT_B]) for i in range(2)]
        picked = sb("picked", [P, 2, GE, SLOT_B])
        lists = sb("lists", [P, 2, G, SLOT_B])
        block_rows = sb("block_rows", [P, 2, P])

        banks = [ctx.enter_context(nc.psum_tensor(f"r_bank{i}", [P, 512], F32)) for i in range(8)]

        const_in = sem("const_in")
        ones_ready = sem("ones_ready")
        step = sem("step")
        mask_ready = sem("mask_ready")
        counted = sem("counted")
        kept = sem("kept")
        onehot_ready = sem("onehot_ready")
        second_ready = sem("second_ready")
        token_ready = sem("token_ready")
        chunk_done = sem("chunk_done")
        picked_out = sem("picked_out")
        lists_ready = sem("lists_ready")
        lists_stored = sem("lists_stored")
        rows_in = sem("rows_in")
        flipped = sem("flipped")

        consts = [(bias, d["gate_bias"]), (before, d["before"]), (ident, d["ident"]), (lower, d["lower"]),
                  (iota, d["iota"]), (token1, d["token1"]), (row_empty, d["row_empty"]),
                  (own_expert, d["own_expert"])]
        NCHUNK = NT // CH

        block = ctx.enter_context(nc.Block())

        @block.sync
        def _(sp):
            for dst, src in consts:
                sp.dma_start(dst[:], src).then_inc(const_in, 16)
            sp.wait_ge(lists_ready, 1)
            for i, dram in enumerate((slot_token, slot_weight)):
                sp.dma_start(dram.rearrange("(g p b) -> p g b", g=G, b=SLOT_B), lists[:, i]).then_inc(lists_stored, 16)
            sp.wait_ge(lists_stored, 32)
            for i, dram in enumerate((slot_token, slot_weight)):
                sp.dma_start(block_rows[:, i], dram.rearrange("(n q) -> n q", q=P)).then_inc(rows_in, 16)

        @block.tensor
        def _(pe):
            pe.wait_ge(const_in, 16 * len(consts))
            pe.wait_ge(ones_ready, 1)
            pe.wait_ge(mask_ready, 1)
            for c in range(NCHUNK):
                if c >= 4:
                    pe.wait_ge(kept, 2 * (c - 3))
                src = mask[:, c * CH:(c + 1) * CH, :].rearrange("p t e -> p (t e)")
                nc.tensor.matmul(banks[2 * c % 8][:], before[:], src, start=True, stop=True)
                nc.tensor.matmul(banks[(2 * c + 1) % 8][:], ones[:], src, start=True, stop=True).then_inc(counted, 1)
            pe.wait_ge(kept, 2 * NCHUNK)
            n = 0
            for g in range(G):
                if g >= 2:
                    pe.wait_ge(picked_out, g - 1)
                for c in range(NCHUNK):
                    pe.wait_ge(second_ready, n + 1)
                    pe.wait_ge(token_ready, n + 1)
                    for t in range(CH):
                        mm = nc.tensor.matmul(banks[g % 2][:, 0:2 * P], first[n % 2][:, t].rearrange("p e a -> p (e a)"),
                                              second[n % 2][:, 1:3, t].rearrange("p i e b -> p i (e b)"),
                                              start=c == 0 and t == 0, stop=c == NCHUNK - 1 and t == CH - 1)
                    mm.then_inc(chunk_done, 1)
                    n += 1
            pe.wait_ge(rows_in, 32)
            for i in range(2):
                mm = nc.tensor.transpose(banks[2][:, i * P:(i + 1) * P], block_rows[:, i], ident[:])
            mm.then_inc(flipped, 1)

        @block.gpsimd
        def _(pool):
            pool.memset(ones[:], 1.0).then_inc(ones_ready, 1)
            pool.wait_ge(const_in, 16 * len(consts))
            n = 0
            for g in range(G):
                for c in range(NCHUNK):
                    pool.wait_ge(onehot_ready, n + 1)
                    s = second[n % 2]
                    nc.gpsimd.tensor_tensor(
                        s[:, 1].rearrange("p t e b -> p t (e b)"), s[:, 0].rearrange("p t e b -> p t (e b)"),
                        token1[:, c * CH:(c + 1) * CH].unsqueeze(2).to_broadcast([P, CH, GE * SLOT_B]),
                        ALU.mult).then_inc(token_ready, 1)
                    n += 1

        @block.vector
        def _(dve):
            chain = Chain(dve, step, 0, 0)
            link = chain.link
            v = nc.vector
            dve.wait_ge(const_in, 16 * len(consts))
            link(v.tensor_tensor(sfc[:], gate_scores[:], bias[:].unsqueeze(1).to_broadcast([P, NT, NX]), ALU.add))
            x = sfc[:].rearrange("p t (g k) -> p (t g) k", k=GE)
            v.tensor_tensor(hi[:], x[:, :, 0:4], x[:, :, 4:8], ALU.max)
            link(v.tensor_tensor(lo[:], x[:, :, 0:4], x[:, :, 4:8], ALU.min))
            v.tensor_tensor(hi2[:], hi[:, :, 0:2], hi[:, :, 2:4], ALU.max)
            v.tensor_tensor(lo2[:], hi[:, :, 0:2], hi[:, :, 2:4], ALU.min)
            link(v.tensor_tensor(lo2b[:], lo[:, :, 0:2], lo[:, :, 2:4], ALU.max))
            link(v.tensor_tensor(lo2[:], lo2[:], lo2b[:], ALU.max))
            flat = gscore[:].rearrange("p t g -> p (t g)")
            v.tensor_tensor(flat, hi2[:, :, 0], hi2[:, :, 1], ALU.max)
            v.tensor_tensor(lo3[:], hi2[:, :, 0], hi2[:, :, 1], ALU.min)
            link(v.tensor_tensor(lo3b[:], lo2[:, :, 0], lo2[:, :, 1], ALU.max))
            link(v.tensor_tensor(lo3[:], lo3[:], lo3b[:], ALU.max))
            link(v.tensor_tensor(flat, flat, lo3[:], ALU.add))
            other = gscore[:].unsqueeze(2).to_broadcast([P, NT, G, G])
            own = gscore[:].unsqueeze(3).to_broadcast([P, NT, G, G])
            w4 = work[:].rearrange("p t (g k) -> p t g k", k=G)
            w4b = work2[:].rearrange("p t (g k) -> p t g k", k=G)
            v.tensor_tensor(w4, other, own, ALU.is_gt)
            link(v.tensor_tensor(w4b, other, own, ALU.is_equal))
            link(v.tensor_tensor(w4b, w4b, lower[:].unsqueeze(1).to_broadcast([P, NT, G, G]), ALU.mult))
            link(v.tensor_tensor(work[:], work[:], work2[:], ALU.add))
            link(v.tensor_reduce(rank[:], w4, AX_X, ALU.add))
            link(v.tensor_scalar(rank[:], rank[:], float(TOP_GROUPS), -FAR, ALU.is_ge, ALU.mult))
            link(v.tensor_tensor(work[:].rearrange("p t (g k) -> p (t g) k", k=GE), x,
                                 rank[:].rearrange("p t g -> p (t g)").unsqueeze(2).to_broadcast([P, NT * G, GE]), ALU.add))
            for t in range(NT):
                last = v.max(top[:, t, :], work[:, t, :])
            link(last)
            for t in range(NT):
                last = v.match_replace(work2[:, t, :], top[:, t, :], work[:, t, :], TAKEN)
            link(last)
            v.tensor_scalar(mask[:], work2[:], TAKEN, None, ALU.is_equal).then_inc(mask_ready, 1)
            dve.wait_ge(mask_ready, 1)
            link(v.tensor_tensor(gate_scores[:], gate_scores[:], mask[:], ALU.mult))
            link(v.tensor_reduce(wsum[:], gate_scores[:], AX_X, ALU.add))
            link(v.tensor_scalar(wsum[:], wsum[:], 1e-20, None, ALU.add))
            link(v.reciprocal(wsum[:], wsum[:]))
            link(v.tensor_scalar(wsum[:], wsum[:], ROUTE_SCALE, None, ALU.mult))
            v.tensor_tensor(gate_scores[:], gate_scores[:], wsum[:].unsqueeze(2).to_broadcast([P, NT, NX]), ALU.mult)
            pos = sfc
            total = work[:].rearrange("p t e -> p (t e)").rearrange("p (e t) -> p e t", t=NT)
            reset = work2[:].rearrange("p t e -> p (t e)").rearrange("p (e t) -> p e t", t=NT)
            for c in range(NCHUNK):
                dve.wait_ge(counted, c + 1)
                v.tensor_copy(pos[:, c * CH:(c + 1) * CH, :].rearrange("p t e -> p (t e)"), banks[2 * c % 8][:]).then_inc(kept, 1)
                v.tensor_copy(total[:, :, c * CH:(c + 1) * CH],
                              banks[(2 * c + 1) % 8][:].rearrange("p (t e) -> p e t", e=NX)).then_inc(kept, 1)
            dve.wait_ge(kept, 2 * NCHUNK)
            link(v.memset(reset, 1.0))
            link(v.memset(reset[:, :, 0:1], 0.0))
            running = ai[:].bitcast(F32)
            link(v.tensor_tensor_scan(running.rearrange("p t e -> p (t e)"), work2[:].rearrange("p t e -> p (t e)"),
                                      work[:].rearrange("p t e -> p (t e)"), 0.0, ALU.mult, ALU.add))
            link(v.tensor_tensor(work[:], running, work[:], ALU.subtract))
            link(v.tensor_tensor(pos[:], pos[:], total.rearrange("p e t -> p t e"), ALU.add))
            link(v.tensor_scalar(work2[:], mask[:], -UNCHOSEN, UNCHOSEN, ALU.mult, ALU.add))
            link(v.tensor_tensor(pos[:], pos[:], work2[:], ALU.add))
            link(v.tensor_copy(ai[:], pos[:]))
            v.tensor_scalar(bi[:], ai[:], SLOT_B - 1, None, ALU.bitwise_and)
            link(v.tensor_scalar(work2[:].bitcast(I32), ai[:], SLOT_BITS, None, ALU.arith_shift_right))
            high, low = work, pos
            v.tensor_copy(high[:], work2[:].bitcast(I32))
            link(v.tensor_copy(low[:], bi[:]))
            n = 0
            for g in range(G):
                e = slice(g * GE, (g + 1) * GE)
                for c in range(NCHUNK):
                    t = slice(c * CH, (c + 1) * CH)
                    if n >= 2:
                        dve.wait_ge(chunk_done, n - 1)
                    shape = [P, CH, GE, SLOT_B]
                    s = second[n % 2]
                    codes = iota[:].unsqueeze(1).unsqueeze(1).to_broadcast(shape)
                    v.tensor_tensor(s[:, 0], low[:, t, e].unsqueeze(3).to_broadcast(shape), codes, ALU.is_equal).then_inc(onehot_ready, 1)
                    v.tensor_tensor(first[n % 2][:], high[:, t, e].unsqueeze(3).to_broadcast(shape), codes, ALU.is_equal)
                    dve.wait_ge(onehot_ready, n + 1)
                    v.tensor_tensor(s[:, 2], s[:, 0], gate_scores[:, t, e].unsqueeze(3).to_broadcast(shape), ALU.mult).then_inc(second_ready, 1)
                    n += 1
                dve.wait_ge(chunk_done, n)
                v.tensor_tensor(picked[:], banks[g % 2][:, 0:2 * P].rearrange("p (i e b) -> p i e b", i=2, b=SLOT_B),
                                own_expert[:].unsqueeze(1).unsqueeze(3).to_broadcast([P, 2, GE, SLOT_B]), ALU.mult)\
                    .then_inc(picked_out, 1)
                dve.wait_ge(picked_out, g + 1)
                last = link(v.tensor_reduce(lists[:, :, g, :], picked[:].rearrange("p i e b -> p i b e"), AX_X, ALU.add))
            dve.sem_inc(lists_ready, 1)
            dve.wait_ge(flipped, 1)
            v.tensor_copy(slot_scale[:], banks[2][:, P:2 * P])
            link(v.tensor_scalar(hi[:, 0:NX // 2, :].rearrange("p a b -> p (a b)"), banks[2][:, 0:P], 0.0, None, ALU.is_equal))
            hole = hi[:, 0:NX // 2, :].rearrange("p a b -> p (a b)")
            link(v.tensor_tensor(hole, hole, row_empty[:], ALU.mult))
            link(v.tensor_tensor(hole, hole, banks[2][:, 0:P], ALU.add))
            link(v.tensor_scalar(slot_index[:], hole, -1.0, None, ALU.add))


def experts(nc, d, x2_rows, acc_rows, slot_index, slot_scale):
    with ExitStack() as ctx:
        def sb(name, shape, dt=F32):
            return ctx.enter_context(nc.sbuf_tensor("e_" + name, shape, dt))

        def sem(name):
            return ctx.enter_context(nc.semaphore("e_" + name))

        NS = 4
        ident = sb("ident", [P, P])
        wg, wu, wd = ([sb(f"{n}{i}", s) for i in range(NS)]
                      for n, s in (("wg", [P, HALVES, P]), ("wu", [P, HALVES, P]), ("wd", [P, E])))
        rows = [sb(f"rows{i}", [P, 2, E]) for i in range(NS)]
        rowsT = [sb(f"rowsT{i}", [P, HALVES, CAP]) for i in range(2)]
        silu = [sb(f"silu{i}", [P, CAP]) for i in range(2)]
        hidden = [sb(f"hidden{i}", [P, CAP]) for i in range(2)]
        y = [sb(f"y{i}", [P, 2, E]) for i in range(NS)]
        bankT, bankH, bankY = ([ctx.enter_context(nc.psum_tensor(f"e_{n}{i}", [P, 2, CAP], F32)) for i in range(2)]
                               for n in ("bankT", "bankH", "bankY"))
        ident_in = sem("ident_in")
        w_in = [sem(f"w_in{i}") for i in range(NS)]
        rows_in = [sem(f"rows_in{i}") for i in range(NS)]
        added = [sem(f"added{i}") for i in range(NS)]
        flipped, rowsT_ready, up_done, silu_ready, hidden_ready, down_done, y_ready = (
            sem(n) for n in ("flipped", "rowsT_ready", "up_done", "silu_ready", "hidden_ready", "down_done", "y_ready"))

        block = ctx.enter_context(nc.Block())

        @block.sync
        def _(sp):
            sp.dma_start(ident[:], d["ident"]).then_inc(ident_in, 16)

            def load(e, s):
                for dst, src in ((wg, "w_gate"), (wu, "w_up")):
                    sp.dma_start(dst[s][:], d[src][bass.ds(e, 1)].rearrange("e (a p) i -> p (e a) i", p=P)).then_inc(w_in[s], 16)
                sp.dma_start(wd[s][:], d["w_down"][bass.ds(e, 1)].rearrange("e i h -> (e i) h")).then_inc(w_in[s], 16)

            for s in range(NS):
                load(s, s)
            with sp.Fori(0, NX // NS - 1) as t:
                for s in range(NS):
                    sp.wait_ge(down_done, t * NS + s + 1)
                    load(t * NS + s + NS, s)

        @block.gpsimd
        def _(pool):
            def gather(e):
                s = e % NS
                if e >= NS:
                    pool.wait_ge(flipped, e - NS + 1)
                for i in range(2):
                    at = slot_index[:, 2 * e + i:2 * e + i + 1]
                    nc.gpsimd.indirect_dma_start(
                        out=rows[s][:, i, :], out_offset=None, in_=x2_rows,
                        in_offset=bass.IndirectOffsetOnAxis(ap=at, axis=0)).then_inc(rows_in[s], 16)

            def scatter(e):
                s = e % NS
                pool.wait_ge(y_ready, e + 1)
                if e >= 2:
                    pool.wait_ge(added[(e - 2) % NS], 32 * ((e - 2) // NS + 1))
                for i in range(2):
                    at = slot_index[:, 2 * e + i:2 * e + i + 1]
                    nc.gpsimd.indirect_dma_start(
                        out=acc_rows[e % 2], out_offset=bass.IndirectOffsetOnAxis(ap=at, axis=0),
                        in_=y[s][:, i, :], in_offset=None, compute_op=ALU.add).then_inc(added[s], 16)

            AHEAD = 3
            for e in range(AHEAD):
                gather(e)
            for e in range(NX):
                if e + AHEAD < NX:
                    gather(e + AHEAD)
                scatter(e)
            for s in range(NS):
                pool.wait_ge(added[s], 32 * NX // NS)

        @block.tensor
        def _(pe):
            pe.wait_ge(ident_in, 16)

            def flip(e, t, s, first=False):
                pe.wait_ge(rows_in[s], t * 32 + 32)
                for a in range(HALVES):
                    for i in range(2):
                        mm = nc.tensor.transpose(bankT[s % 2][:, a, i * P:(i + 1) * P], rows[s][:, i, a * P:(a + 1) * P], ident[:])
                mm.then_inc(flipped, 1)

            def up(e, t, s, first=False):
                pe.wait_ge(w_in[s], t * 48 + 48)
                pe.wait_ge(rowsT_ready, e + 1)
                for n, w in enumerate((wg, wu)):
                    for a in range(HALVES):
                        mm = nc.tensor.matmul(bankH[s % 2][:, n, :], w[s][:, a, :], rowsT[s % 2][:, a, :],
                                              start=a == 0, stop=a == HALVES - 1)
                mm.then_inc(up_done, 1)

            def down(e, t, s, first=False):
                pe.wait_ge(hidden_ready, e + 1)
                if not first:
                    pe.wait_ge(y_ready, e - 1)
                for i in range(2):
                    mm = nc.tensor.matmul(bankY[s % 2][:, i, :], hidden[s % 2][:, i * P:(i + 1) * P], wd[s][:], start=True, stop=True)
                mm.then_inc(down_done, 1)

            flip(0, 0, 0)
            flip(1, 0, 1)
            up(0, 0, 0)

            def turn(t, last=False, head=False):
                for s in range(NS):
                    e = t * NS + s
                    more = s + 2 >= NS
                    if not (last and more):
                        flip(e + 2, t + 1 if more else t, (s + 2) % NS)
                    if not (last and s == NS - 1):
                        up(e + 1, t + 1 if s == NS - 1 else t, (s + 1) % NS)
                    down(e, t, s, first=head and s < 2)

            turn(0, head=True)
            with pe.Fori(1, NX // NS - 1) as t:
                turn(t)
            turn(NX // NS - 1, last=True)

        @block.scalar
        def _(act):
            def keep(e, s, first=False):
                act.wait_ge(flipped, e + 1)
                if not first:
                    act.wait_ge(up_done, e - 1)
                nc.scalar.activation(rowsT[s % 2][:], bankT[s % 2][:], ACT.Copy).then_inc(rowsT_ready, 1)

            def gate(e, s, first=False):
                act.wait_ge(up_done, e + 1)
                if not first:
                    act.wait_ge(hidden_ready, e - 1)
                nc.scalar.activation(silu[s % 2][:], bankH[s % 2][:, 0, :], ACT.Silu).then_inc(silu_ready, 1)

            keep(0, 0, True)
            keep(1, 1, True)
            gate(0, 0, True)

            def turn(t, last=False, head=False):
                for s in range(NS):
                    e = t * NS + s
                    if not (last and s + 2 >= NS):
                        keep(e + 2, s)
                    if not (last and s == NS - 1):
                        gate(e + 1, s + 1, first=head and s == 0)

            turn(0, head=True)
            with act.Fori(1, NX // NS - 1) as t:
                turn(t)
            turn(NX // NS - 1, last=True)

        @block.vector
        def _(dve):
            def product(e, s, first=False):
                dve.wait_ge(silu_ready, e + 1)
                if not first:
                    dve.wait_ge(down_done, e - 1)
                nc.vector.tensor_tensor(hidden[s % 2][:], silu[s % 2][:], bankH[s % 2][:, 1, :], ALU.mult).then_inc(hidden_ready, 1)

            def scale(e, t, s, first=False):
                dve.wait_ge(down_done, e + 1)
                if not first:
                    dve.wait_ge(added[s], t * 32)
                for i in range(2):
                    mm = nc.vector.tensor_scalar(y[s][:, i, :], bankY[s % 2][:, i, :], slot_scale[:, bass.ds(e * 2 + i, 1)], None, ALU.mult)
                mm.then_inc(y_ready, 1)

            product(0, 0, True)

            def turn(t, last=False, head=False):
                for s in range(NS):
                    e = t * NS + s
                    if not (last and s == NS - 1):
                        product(e + 1, s + 1, first=head and s == 0)
                    scale(e, t, s, first=head)

            turn(0, head=True)
            with dve.Fori(1, NX // NS - 1) as t:
                turn(t)
            turn(NX // NS - 1, last=True)


def final_norm(nc, acc_rows, out):
    with ExitStack() as ctx:
        def sb(name, shape, dt=F32):
            return ctx.enter_context(nc.sbuf_tensor("f_" + name, shape, dt))

        def sem(name):
            return ctx.enter_context(nc.semaphore("f_" + name))

        parts = [[sb(f"part{i}{j}", [P, QT, E]) for j in range(2)] for i in range(2)]
        r = [sb(f"r{i}", [P, QT, E]) for i in range(2)]
        normed = [sb(f"normed{i}", [P, QT, E]) for i in range(2)]
        stats, moments, rstd = ([sb(f"{n}{i}", [P, QT, w]) for i in range(2)] for n, w in (("stats", 6), ("moments", 2), ("rstd", 1)))
        eps = sb("eps", [P, 1])
        parts_in = [sem(f"parts_in{i}") for i in range(2)]
        stored = [sem(f"stored{i}") for i in range(2)]
        eps_ready, summed, moments_ready, deviation_ready, normed_ready, step = (
            sem(n) for n in ("eps_ready", "summed", "moments_ready", "deviation_ready", "normed_ready", "step"))

        def rows(dram, b):
            return dram[bass.ds(b * S, S), :].rearrange("(t p) e -> p t e", p=P)

        block = ctx.enter_context(nc.Block())

        @block.sync
        def _(sp):
            def load(b, i):
                for j in range(2):
                    sp.dma_start(parts[i][j][:], rows(acc_rows[j], b)).then_inc(parts_in[i], 16)

            load(0, 0)
            load(1, 1)
            with sp.Fori(0, B // 2 - 1) as t:
                for i in range(2):
                    sp.wait_ge(summed, t * 2 + i + 1)
                    load(t * 2 + i + 2, i)

        @block.gpsimd
        def _(pool):
            pool.memset(eps[:], EPS).then_inc(eps_ready, 1)
            with pool.Fori(0, B // 2) as t:
                for i in range(2):
                    pool.wait_ge(normed_ready, t * 2 + i + 1)
                    pool.dma_start(rows(out, t * 2 + i), normed[i][:]).then_inc(stored[i], 16)
            for i in range(2):
                pool.wait_ge(stored[i], 16 * B // 2)

        @block.scalar
        def _(act):
            act.wait_ge(eps_ready, 1)
            with act.Fori(0, B // 2) as t:
                for i in range(2):
                    deviation(nc, act, t * 2 + i, moments[i], rstd[i][:, :, 0], eps, moments_ready, deviation_ready)

        @block.vector
        def _(dve):
            def turn(t, i, first=False):
                b = t * 2 + i
                if not first:
                    dve.wait_ge(stored[i], t * 16)
                dve.wait_ge(parts_in[i], t * 32 + 32)
                nc.vector.tensor_tensor(r[i][:], parts[i][0][:], parts[i][1][:], ALU.add).then_inc(summed, 1)
                dve.wait_ge(summed, b + 1)
                take_moments(nc, r[i], stats[i], moments[i], dve, step, b * NORM_STEPS, moments_ready)
                apply_norm(nc, r[i], normed[i], moments[i], rstd[i][:, :, 0], dve, step, b * NORM_STEPS, b, deviation_ready).then_inc(normed_ready, 1)

            turn(0, 0, True)
            turn(0, 1, True)
            with dve.Fori(1, B // 2) as t:
                turn(t, 0)
                turn(t, 1)


def layouts(x, ctx_1024, mask_1x1xSxS2_ik0, **w):
    def c(a):
        return np.ascontiguousarray(a)

    def columns(v):
        return c(v.reshape(HALVES, P).T)

    out = {}
    out["a_xT"] = c(np.transpose(x, (0, 2, 1)))
    wq, bq = w["L0_attn_Wq"], w["L0_attn_bq"]
    out["a_wqT"], out["a_wkT"], out["a_wvT"] = c(wq.T), c(w["L0_attn_Wk"].T), c(w["L0_attn_Wv"].T)
    out["a_bq"], out["a_bk"], out["a_bv"] = columns(bq), columns(w["L0_attn_bk"]), c(w["L0_attn_bv"].reshape(1, E))
    r, k = w["L0_attn_rel_k_emb"], w["L0_attn_rel_v_emb"]
    j = np.arange(QG)[:, None]
    at = np.clip(j + (S - QG) - np.arange(TKW)[None, :], -MAXREL, MAXREL) + MAXREL
    out["relk"] = c(np.transpose(r[at], (0, 2, 1)).reshape(P, TKW))
    at = np.clip(np.arange(TVZ)[None, :] - (KT - 1) * P - np.arange(P)[:, None], -MAXREL, MAXREL) + MAXREL
    out["relv"] = c(k[at].reshape(P, TVZ * D))
    p = np.arange(P)
    hm = np.zeros((P, HH), np.float32)
    hm[p, p // D] = 1
    out["head_mask"] = hm
    qm = np.zeros((P, QG), np.float32)
    qm[p, p // D] = 1
    out["query_mask"] = qm
    om = np.zeros((P, QG + HH, D), np.float32)
    om[p, p // HH % QG, :] = 1
    om[p, QG + p % HH, :] = 1
    out["out_mask"] = om.reshape(P, 2 * P)
    out["relv_far"] = c(np.broadcast_to(k[[0, 2 * MAXREL]], (P, 2, D)))
    out["ident"] = np.eye(P, dtype=np.float32)
    out["x"] = c(x.reshape(TOK, E))
    out["a_woT"], out["a_bo"] = c(w["L0_attn_Wo"].T), c(np.broadcast_to(w["L0_attn_bo"], (P, E)))
    for n in ("q", "k", "v", "o"):
        out[f"x_w{n}T"] = c(w[f"L0_xattn_W{n}"].T)
    out["x_bq"], out["x_bk"] = columns(w["L0_xattn_bq"]), columns(w["L0_xattn_bk"])
    out["x_bv"], out["x_bo"] = c(w["L0_xattn_bv"].reshape(1, E)), c(np.broadcast_to(w["L0_xattn_bo"], (P, E)))
    out["ctxT"] = c(np.repeat(np.transpose(ctx_1024, (2, 0, 1))[:, :, None, :], 2, axis=2))
    out["mask"] = c(mask_1x1xSxS2_ik0.reshape(S, SK))
    out["gate_wT"] = c(w["L0_ffn_gate_w"].T)
    half = np.zeros((P, H // HALVES), np.float32)
    half[p, p // D] = 1
    out["half_mask"] = half
    pair = np.zeros((P, 2, D), np.float32)
    pair[p, p // SK, :] = 1
    out["pair_mask"] = pair.reshape(P, 2 * D)
    out["gate_bias"] = c(np.broadcast_to(w["L0_ffn_gate_bias"], (P, NX)))
    out["before"] = np.triu(np.ones((P, P), np.float32), 1)
    out["lower"] = c(np.broadcast_to(np.tril(np.ones((NX // GE, NX // GE), np.float32), -1), (P, NX // GE, NX // GE)))
    out["iota"] = c(np.broadcast_to(np.arange(SLOT_B, dtype=np.float32), (P, SLOT_B)))
    out["token1"] = (p[:, None] + P * np.arange(NT)[None, :] + 1).astype(np.float32)
    out["row_empty"] = (TOK + 1 + p[:, None] + P * (np.arange(2 * NX)[None, :] % 2)).astype(np.float32)
    own = np.zeros((P, GE), np.float32)
    own[p, p // SLOT_A] = 1
    out["own_expert"] = own
    for n in ("w_gate", "w_up", "w_down"):
        out[n] = w[f"L0_ffn_{n}"]
    return out


def program(nc, d, out):
    qs = nc.dram_tensor("q_scratch", [B, E, S], F32).ap()
    attn = nc.dram_tensor("attn_scratch", [B, S, E], F32).ap()
    rel = nc.dram_tensor("rel_scratch", [B, S, E], F32).ap()
    x2_rows = nc.dram_tensor("x2_scratch", [TOK + CAP, E], F32).ap()
    acc_rows = [nc.dram_tensor(f"acc_scratch{i}", [TOK + CAP, E], F32).ap() for i in range(2)]
    slot_token = nc.dram_tensor("slot_token_scratch", [NX * CAP], F32).ap()
    slot_weight = nc.dram_tensor("slot_weight_scratch", [NX * CAP], F32).ap()
    project_queries(nc, d, qs)
    self_attention(nc, d, qs, attn, rel)
    with (nc.sbuf_tensor("gate_scores", [P, NT, NX], F32) as gate_scores,
          nc.sbuf_tensor("slot_index", [P, 2 * NX], U32) as slot_index,
          nc.sbuf_tensor("slot_scale", [P, 2 * NX], F32) as slot_scale):
        cross_attention(nc, d, attn.rearrange("b s e -> (b s) e"), rel.rearrange("b s e -> (b s) e"), x2_rows, acc_rows,
                        gate_scores)
        route(nc, d, gate_scores, slot_token, slot_weight, slot_index, slot_scale)
        experts(nc, d, x2_rows, acc_rows, slot_index, slot_scale)
    final_norm(nc, acc_rows, out.rearrange("b s e -> (b s) e"))


def kernel(**inputs):
    import concourse.bacc as bacc
    from concourse.bass_utils import run_bass_kernel_spmd

    arrays = layouts(**{k: np.asarray(v) for k, v in inputs.items()})
    nc = bacc.Bacc("TRN2", target_bir_lowering=False, num_devices=1)
    named = {f"in_{k}": v for k, v in arrays.items()}
    d = {k: nc.dram_tensor(f"in_{k}", v.shape, mybir.dt.from_np(v.dtype), kind="ExternalInput").ap()
         for k, v in arrays.items()}
    out = nc.dram_tensor("out", [B, S, E], F32, kind="ExternalOutput").ap()
    program(nc, d, out)
    r = run_bass_kernel_spmd(nc, [named], core_ids=[0])
    return r.results[0]["out"]
```

```python
from contextlib import ExitStack

import numpy as np

import concourse.bass as bass
from concourse import mybir
from concourse.alu_op_type import AluOpType as ALU

ACT = mybir.ActivationFunctionType
F32 = mybir.dt.float32
I32 = mybir.dt.int32
U32 = mybir.dt.uint32
AX_X = mybir.AxisListType.X

P = 128
B, S, E = 16, 512, 256
H, D = 16, 16
MAXREL = 128
HALVES = E // P
QG = P // H
NG = S // QG
GT = P // QG
KT = S // P
TKW = 2 * S - QG
TVZ = 3 * P
SC = D ** -0.5
QT = S // P
SK = 64
TOK = B * S
NT = TOK // P
NX = 64
GE = 8
TOP_GROUPS = 4
CAP = 256
SLOT_A = SLOT_B = 16
SLOT_BITS = 4
ROUTE_SCALE = 2.5
NEG = -1e9
FAR = 1e30
TAKEN = -3e38
UNCHOSEN = 65536.0
EPS = 1e-5
HH = H // HALVES
NORM_STEPS = 3
CTX_STEPS = HALVES + B // 4


class Chain:

    def __init__(self, engine, sem, per_turn, turn):
        self.engine, self.sem, self.per_turn, self.turn, self.n = engine, sem, per_turn, turn, 0

    def link(self, instruction):
        self.n += 1
        instruction.then_inc(self.sem, 1)
        self.engine.wait_ge(self.sem, self.turn * self.per_turn + self.n)

    def end(self):
        assert self.n == self.per_turn, (self.n, self.per_turn)


def project_queries(nc, d, qs, far_scores):
    with ExitStack() as ctx:
        def sb(name, shape):
            return ctx.enter_context(nc.sbuf_tensor(name, shape, F32))

        wq, bq = sb("wq", [P, HALVES, E]), sb("bq", [P, HALVES])
        relk_far = sb("relk_far", [P, HALVES, 2, H])
        xT = [sb(f"xTq{i}", [P, HALVES, S]) for i in range(2)]
        q = [sb(f"q{i}", [P, HALVES, S]) for i in range(2)]
        far = [sb(f"farq{i}", [H, QG, NG]) for i in range(2)]
        psQ = [ctx.enter_context(nc.psum_tensor(f"psQ{i}", [P, HALVES, S], F32)) for i in range(2)]
        psF = [ctx.enter_context(nc.psum_tensor(f"psF{i}", [H, S], F32)) for i in range(2)]
        w_in, projected, kept, far_ready, far_kept = (
            ctx.enter_context(nc.semaphore(n)) for n in ("wq_in", "q_projected", "q_kept", "far_ready", "far_kept"))
        x_in = [ctx.enter_context(nc.semaphore(f"xq_in{i}")) for i in range(2)]
        stored = [ctx.enter_context(nc.semaphore(f"q_stored{i}")) for i in range(2)]
        far_stored = [ctx.enter_context(nc.semaphore(f"far_stored{i}")) for i in range(2)]
        block = ctx.enter_context(nc.Block())

        @block.sync
        def _(sp):
            sp.dma_start(wq[:], d["a_wqT"].rearrange("(a p) o -> p a o", p=P)).then_inc(w_in, 16)
            sp.dma_start(bq[:], d["a_bq"]).then_inc(w_in, 16)
            sp.dma_start(relk_far[:], d["relk_far"].rearrange("p (a i h) -> p a i h", a=HALVES, i=2)).then_inc(w_in, 16)
            for b in range(B):
                if b >= 2:
                    sp.wait_ge(projected, b - 1)
                sp.dma_start(xT[b % 2][:], d["a_xT"][b].rearrange("(a p) s -> p a s", p=P)).then_inc(x_in[b % 2], 16)

        @block.tensor
        def _(pe):
            pe.wait_ge(w_in, 48)

            def far_products(b):
                pe.wait_ge(kept, b + 1)
                if b >= 2:
                    pe.wait_ge(far_kept, b - 1)
                for side in range(2):
                    keys = slice(side * S // 2, (side + 1) * S // 2)
                    for a in range(HALVES):
                        mm = nc.tensor.matmul(psF[b % 2][:, keys], relk_far[:, a, side, :], q[b % 2][:, a, keys],
                                              start=a == 0, stop=a == HALVES - 1)
                mm.then_inc(far_ready, 1)

            for b in range(B):
                pe.wait_ge(x_in[b % 2], 16 * (b // 2 + 1))
                if b >= 2:
                    pe.wait_ge(kept, b - 1)
                for m in range(HALVES):
                    for a in range(HALVES):
                        mm = nc.tensor.matmul(psQ[b % 2][:, m, :], wq[:, a, m * P:(m + 1) * P], xT[b % 2][:, a, :],
                                              start=a == 0, stop=a == HALVES - 1)
                mm.then_inc(projected, 1)
                if b >= 1:
                    far_products(b - 1)
            far_products(B - 1)

        @block.vector
        def _(dve):
            dve.wait_ge(w_in, 48)
            for b in range(B):
                dve.wait_ge(projected, b + 1)
                if b >= 2:
                    dve.wait_ge(stored[b % 2], 16 * (b // 2))
                    dve.wait_ge(far_ready, b - 1)
                for m in range(HALVES):
                    mm = nc.vector.tensor_scalar(q[b % 2][:, m, :], psQ[b % 2][:, m, :], bq[:, m:m + 1], SC, ALU.add, ALU.mult)
                mm.then_inc(kept, 1)

        @block.scalar
        def _(act):
            for b in range(B):
                act.wait_ge(kept, b + 1)
                act.dma_start(qs[b].rearrange("(a p) s -> p a s", p=P), q[b % 2][:]).then_inc(stored[b % 2], 16)
                act.wait_ge(far_ready, b + 1)
                if b >= 2:
                    act.wait_ge(far_stored[b % 2], 16 * (b // 2))
                nc.scalar.activation(far[b % 2][:], psF[b % 2][:].rearrange("h (g j) -> h j g", j=QG), ACT.Copy).then_inc(far_kept, 1)
                act.wait_ge(far_kept, b + 1)
                act.dma_start(far_scores[b], far[b % 2][:]).then_inc(far_stored[b % 2], 16)
            for i in range(2):
                act.wait_ge(stored[i], 16 * B // 2)
                act.wait_ge(far_stored[i], 16 * B // 2)


def self_attention(nc, d, qs, far_scores, attnT, rel):
    with ExitStack() as ctx:
        def sb(name, shape, dt=F32):
            return ctx.enter_context(nc.sbuf_tensor(name, shape, dt))

        def ps(name, shape):
            return ctx.enter_context(nc.psum_tensor(name, shape, F32))

        def sem(name):
            return ctx.enter_context(nc.semaphore(name))

        HP = P // HALVES
        wk = sb("wk", [P, HALVES, E])
        wv = sb("wv", [P, HALVES, E])
        bk = sb("bk", [P, HALVES])
        bvrow = sb("bvrow", [1, E])
        ones = sb("ones", [1, P])
        head_mask = sb("head_mask", [P, HH])
        query_mask = sb("query_mask", [P, QG])
        out_mask = sb("out_mask", [P, P])
        relv_far = sb("relv_far", [P, 2, D])
        ident = sb("ident", [P, P])
        relk = sb("relk", [P, TKW])
        relv = sb("relv", [P, TVZ * D])

        xT = sb("xT", [P, HALVES, S])
        v = sb("v", [P, KT, E + D])
        kT = sb("kT", [P, HALVES, S])
        qT = sb("qT", [P, 2 * HALVES, S])
        qrep = [sb(f"qrep{i}", [P, H, S // 2]) for i in range(2)]
        far_in = sb("far_in", [P, 2 * NG])
        qdiag = [sb(f"qdiag{i}", [P, 2 * HALVES, QG, HH]) for i in range(2)]
        part_max = [sb(f"part_max{i}", [P, 2]) for i in range(2)]
        negmax = [sb(f"negmax{i}", [P, 2]) for i in range(2)]
        probs = [sb(f"probs{i}", [P, S]) for i in range(2)]
        total = [sb(f"total{i}", [P, 1]) for i in range(2)]
        sums = sb("sums", [P, 2 * NG, 2])
        inv = sb("inv", [P, 2 * NG])
        probsT = [sb(f"probsT{i}", [P, KT, GT, P]) for i in range(2)]
        values_out = [sb(f"values_out{i}", [P, H // 4, P]) for i in range(2)]
        picked = [sb(f"picked{i}", [P, P]) for i in range(2)]
        far = sb("far", [P, NG])
        far_out = sb("far_out", [P, NG, D])
        rel_out = sb("rel_out", [P, 2 * NG, D])

        psP = [ps(f"psP{i}", [P, S]) for i in range(2)]
        psS = [ps(f"psS{i}", [P, S]) for i in range(2)]
        psT = [ps(f"psT{i}", [P, KT, P]) for i in range(2)]
        psR = [ps(f"psR{i}", [P, S]) for i in range(2)]
        psV = psP[1][:].rearrange("p (c q) -> p c q", q=P)

        consts_in = sem("consts_in")
        q_in = sem("q_in")
        far_scores_in = sem("far_scores_in")
        qrep_in = [sem(f"qrep_in{i}") for i in range(2)]
        x_in = sem("x_in")
        projected = sem("projected")
        kept_dve = sem("kept_dve")
        kept_act = sem("kept_act")
        ones_set = sem("ones_set")
        qdiag_ready = sem("qdiag_ready")
        scores_ready = sem("scores_ready")
        part_max_ready = sem("part_max_ready")
        max_ready = sem("max_ready")
        exp_ready = sem("exp_ready")
        norm_step = sem("norm_step")
        weights_ready = sem("weights_ready")
        transposed = sem("transposed")
        probsT_ready = sem("probsT_ready")
        rel_ready = sem("rel_ready")
        rel_read = sem("rel_read")
        reduced = sem("reduced")
        values_ready = sem("values_ready")
        values_kept = sem("values_kept")
        values_stored = [sem(f"values_stored{i}") for i in range(2)]
        finish_step = sem("finish_step")
        finished = sem("finished")
        rel_stored = sem("rel_stored")
        rel_free = sem("rel_free")

        loads = [
            (wk, d["a_wkT"].rearrange("(a p) o -> p a o", p=P)),
            (bk, d["a_bk"]), (bvrow, d["a_bv"]),
            (wv, d["a_wvT"].rearrange("(a p) o -> p a o", p=P)),
            (head_mask, d["head_mask"]), (query_mask, d["query_mask"]),
            (out_mask, d["out_mask"]), (relv_far, d["relv_far"]), (ident, d["ident"]),
            (relk, d["relk"]), (relv, d["relv"]),
        ]
        N_CONST = 16 * len(loads)
        projections = [("k", 0), ("k", 1)] + [("v", t) for t in range(KT)]
        KEYS, VALUES = slice(0, HALVES), slice(HALVES, None)
        HALF = len(projections) // 2
        REL_STORES = HALVES * QG * 16

        def near_tiles(tile):
            return [t for t in range(KT) if abs(t - tile) <= 1]

        def near_far(tile):
            near = near_tiles(tile)
            first, end = near[0] * P, (near[-1] + 1) * P
            return slice(first, end), (slice(end, S) if first == 0 else slice(0, first))

        def is_first(b):
            return isinstance(b, int) and b == 0

        block = ctx.enter_context(nc.Block())

        @block.sync
        def _(sp):
            for dst, src in loads:
                sp.dma_start(dst[:], src).then_inc(consts_in, 16)
            x_in_dram = d["a_xT"].rearrange("b (a p) s -> p (b a) s", p=P)
            q_dram = qs.rearrange("b (a p) s -> p (b a) s", p=P)

            sp.sem_inc(rel_stored, 1)

            def load_x(b):
                sp.dma_start(xT[:], x_in_dram[:, bass.ds(b * HALVES, HALVES), :]).then_inc(x_in, 16)

            def load_q(b):
                sp.dma_start(qT[:, bass.ds(b % 2 * HALVES, HALVES), :], q_dram[:, bass.ds(b * HALVES, HALVES), :]).then_inc(q_in, 16)

            def load_qrep(b, half):
                head = qs[:, bass.ds(b * D, D), half * (S // 2):(half + 1) * (S // 2)].rearrange("h e s -> e h s")
                for j in range(QG):
                    sp.dma_start(qrep[half][j * D:(j + 1) * D, :, :], head).then_inc(qrep_in[half], 16)

            def load_far_scores(b):
                for a in range(HALVES):
                    for j in range(QG):
                        rows = slice((a * QG + j) * HH, (a * QG + j + 1) * HH)
                        sp.dma_start(far_in[rows, bass.ds(b % 2 * NG, NG)],
                                     far_scores[a * HH:(a + 1) * HH, bass.ds(b, 1), j, :].rearrange("h b g -> (h b) g"))\
                            .then_inc(far_scores_in, 16)

            def store_values(b, tile):
                sp.wait_ge(values_kept, b * KT + tile + 1)
                for i in range(4):
                    dst = attnT[bass.ds(b, 1), :, tile * P:(tile + 1) * P].rearrange("b (c i e) q -> i (b e) c q", i=4, e=D)
                    sp.dma_start(dst[i], values_out[tile % 2][32 * i:32 * i + D, :, :]).then_inc(values_stored[tile % 2], 16)

            def store_rel(b):
                sp.wait_ge(finished, b + 1)
                sp.wait_ge(rel_stored, b * REL_STORES + 1)
                sp.sem_inc(rel_free, 1)
                for a in range(HALVES):
                    for j in range(QG):
                        rows = slice((a * QG + j) * HH, (a * QG + j + 1) * HH)
                        dst = rel[a * HH:(a + 1) * HH, j::QG, bass.ds(b * D, D)]
                        sp.dma_start(dst, rel_out[rows, bass.ds(b % 2 * NG, NG), :]).then_inc(rel_stored, 16)

            def batch(b, more=True):
                if not is_first(b):
                    store_rel(b - 1)
                if more:
                    sp.wait_ge(projected, (b + 1) * len(projections))
                    load_x(b + 1)
                if not is_first(b):
                    sp.wait_ge(qdiag_ready, b * NG)
                    sp.wait_ge(max_ready, b * NG)
                if more:
                    load_q(b + 1)
                    load_far_scores(b + 1)
                if not is_first(b):
                    load_qrep(b, 1)
                    store_values(b - 1, KT - 1)
                store_values(b, 0)
                if more:
                    sp.wait_ge(qdiag_ready, b * NG + NG // 2)
                    load_qrep(b + 1, 0)
                store_values(b, 1)
                store_values(b, 2)

            load_x(0)
            load_q(0)
            load_far_scores(0)
            load_qrep(0, 0)
            load_qrep(0, 1)
            batch(0)
            with sp.Fori(1, B - 1) as b:
                batch(b)
            batch(B - 1, more=False)
            store_values(B - 1, KT - 1)
            store_rel(B - 1)
            for i in range(2):
                sp.wait_ge(values_stored[i], B * KT // 2 * 4 * 16)
            sp.wait_ge(rel_stored, B * REL_STORES + 1)

        @block.gpsimd
        def _(pool):
            pool.memset(v[:, :, E:], 0.0).then_inc(ones_set, 1)
            pool.memset(ones[:], 1.0).then_inc(ones_set, 1)
            pool.wait_ge(consts_in, N_CONST)

            def build(b, i, n, half, first=False):
                if not first:
                    pool.wait_ge(scores_ready, b * NG + i - 1)
                for a in range(HALVES):
                    nc.gpsimd.tensor_tensor(
                        qdiag[n][:, a, :, :],
                        qT[:, bass.ds(b % 2 * HALVES + a, 1), bass.ds(i * QG, QG)].rearrange("p a q -> p (a q)").unsqueeze(2).to_broadcast([P, QG, HH]),
                        head_mask[:].unsqueeze(1).to_broadcast([P, QG, HH]), ALU.mult)
                nc.gpsimd.tensor_tensor(
                    qdiag[n][:, HALVES:, :, :],
                    qrep[half][:, :, bass.ds((i - half * (NG // 2)) * QG, QG)].rearrange("p (a h) j -> p a j h", a=HALVES),
                    query_mask[:].unsqueeze(1).unsqueeze(3).to_broadcast([P, HALVES, QG, HH]), ALU.mult)\
                    .then_inc(qdiag_ready, 1)

            def batch(b):
                pool.wait_ge(q_in, b * 16 + 16)
                for half in range(2):
                    pool.wait_ge(qrep_in[half], (b + 1) * 16 * QG)
                    i = half * (NG // 2)
                    build(b, i, 0, half, first=is_first(b) and half == 0)
                    build(b, i + 1, 1, half, first=is_first(b) and half == 0)
                    with pool.Fori(half * (NG // 4) + 1, (half + 1) * (NG // 4)) as t:
                        build(b, t * 2, 0, half)
                        build(b, t * 2 + 1, 1, half)

            batch(0)
            with pool.Fori(1, B) as b:
                batch(b)

        @block.tensor
        def _(pe):
            pe.wait_ge(consts_in, N_CONST)
            pe.wait_ge(ones_set, 2)

            def project(b, part):
                pe.wait_ge(x_in, b * 16 + 16)
                for n, (kind, m) in list(enumerate(projections))[part]:
                    if n >= 2:
                        pe.wait_ge(kept_act if n % 2 else kept_dve, b * HALF + n // 2)
                    if n % 2 and not is_first(b):
                        pe.wait_ge(values_kept, b * KT - (kind == "k"))
                    dst = psP[n % 2]
                    for a in range(HALVES):
                        if kind == "v":
                            nc.tensor.matmul(dst[:, 0:E], xT[:, a, m * P:(m + 1) * P], wv[:, a, :],
                                             start=a == 0, stop=False)
                        else:
                            mm = nc.tensor.matmul(dst[:], wk[:, a, m * P:(m + 1) * P], xT[:, a, :], start=a == 0, stop=a == HALVES - 1)
                    if kind == "v":
                        mm = nc.tensor.matmul(dst[:, 0:E], ones[:], bvrow[:], start=False, stop=True)
                    mm.then_inc(projected, 1)

            def keys_kept(b):
                pe.wait_ge(kept_dve, b * HALF + 1)
                pe.wait_ge(kept_act, b * HALF + 1)

            def scores(b, i, n, tile, first=False):
                pe.wait_ge(qdiag_ready, b * NG + i + 1)
                if not first:
                    pe.wait_ge(exp_ready, b * NG + i - 1)
                for a in range(HALVES):
                    nc.tensor.matmul(psS[n][a * HP:(a + 1) * HP, :], qdiag[n][:, a, :, :].rearrange("p j h -> p (j h)"),
                                     kT[:, a, :], start=True, stop=False)
                near, _ = near_far(tile)
                nc.tensor.matmul(psS[n][:, near], qdiag[n][:, HALVES:, :, :].rearrange("p a j h -> p (a j h)"),
                                 relk[:, bass.ds(S - QG - i * QG + near.start, near.stop - near.start)],
                                 start=False, stop=True).then_inc(scores_ready, 1)

            def transpose(b, i, n):
                pe.wait_ge(weights_ready, b * NG + i + 1)
                for t in range(KT):
                    mm = nc.tensor.transpose(psT[n][:, t, :], probs[n][:, t * P:(t + 1) * P], ident[:])
                mm.then_inc(transposed, 1)

            def rel_part(b, i, n, tile):
                pe.wait_ge(probsT_ready, b * NG + i + 1)
                if not (is_first(b) and isinstance(i, int) and i < 2):
                    pe.wait_ge(rel_read, b * NG + i - 1)
                near = near_tiles(tile)
                for t in near:
                    weights = probsT[tile % 2][:, t, i % GT, :]
                    mm = nc.tensor.matmul(psR[n][:, 0:P], weights, relv[:, bass.ds((i * QG + (1 - t) * P) * D, P)],
                                          start=t == near[0], stop=t == near[-1])
                mm.then_inc(rel_ready, 1)

            def values(b, tile):
                if tile == 0:
                    pe.wait_ge(kept_dve, b * HALF + HALF)
                    pe.wait_ge(kept_act, b * HALF + HALF)
                if not (is_first(b) and tile == 0):
                    pe.wait_ge(values_kept, b * KT + tile)
                for c in range(H // 4):
                    for t in range(KT):
                        for i in range(4):
                            h = 4 * c + i
                            a, hh = divmod(h, HH)
                            mm = nc.tensor.matmul(
                                psV[32 * i:32 * i + 2 * D, c, :],
                                v[:, t, h * D:(h + 2) * D],
                                probsT[tile % 2][:, t, :, a * HP + hh:(a + 1) * HP:HH],
                                start=t == 0, stop=t == KT - 1)
                mm.then_inc(values_ready, 1)

            def batch(b, more=True):
                for i in range(3, NG):
                    scores(b, i, i % 2, i // GT)
                    transpose(b, i - 2, i % 2)
                    rel_part(b, i - 3, (i - 3) % 2, (i - 3) // GT)
                    if i == 3:
                        project(b, VALUES)
                    if i > GT and i % GT == 2:
                        values(b, i // GT - 1)
                    if more and i == NG - GT + 5:
                        project(b + 1, KEYS)
                transpose(b, NG - 2, 0)
                rel_part(b, NG - 3, 1, KT - 1)
                if more:
                    keys_kept(b + 1)
                    scores(b + 1, 0, 0, 0)
                if more:
                    scores(b + 1, 1, 1, 0)
                transpose(b, NG - 1, 1)
                rel_part(b, NG - 2, 0, KT - 1)
                if more:
                    scores(b + 1, 2, 0, 0)
                    transpose(b + 1, 0, 0)
                rel_part(b, NG - 1, 1, KT - 1)
                values(b, KT - 1)

            project(0, KEYS)
            keys_kept(0)
            scores(0, 0, 0, 0, first=True)
            scores(0, 1, 1, 0, first=True)
            scores(0, 2, 0, 0)
            transpose(0, 0, 0)
            batch(0)
            with pe.Fori(1, B - 1) as b:
                batch(b)
            batch(B - 1, more=False)

        @block.scalar
        def _(act):
            act.wait_ge(consts_in, N_CONST)

            def project(b, part):
                for n, (kind, m) in list(enumerate(projections))[part]:
                    if n % 2 == 0:
                        continue
                    act.wait_ge(projected, b * len(projections) + n + 1)
                    if kind == "v":
                        mm = nc.scalar.activation(v[:, m, 0:E], psP[1][:, 0:E], ACT.Copy)
                    else:
                        mm = nc.scalar.activation(kT[:, m, :], psP[1][:],
                                                  ACT.Identity, bias=bk[:, m:m + 1])
                    mm.then_inc(kept_act, 1)

            def exp(b, i, n, tile):
                act.wait_ge(max_ready, b * NG + i + 1)
                for side, keys in enumerate(near_far(tile)):
                    mm = nc.scalar.activation(
                        probs[n][:, keys], psS[n][:, keys], ACT.Exp, bias=negmax[n][:, side:side + 1],
                        accum_out=sums[:, bass.ds(b % 2 * NG + i, 1), side:side + 1].rearrange("p g i -> p (g i)"))
                mm.then_inc(exp_ready, 1)

            def keep(b, i, n, tile):
                act.wait_ge(transposed, b * NG + i + 1)
                if isinstance(i, int) and i % GT == 0 and not (is_first(b) and tile < 2):
                    act.wait_ge(values_ready, b * KT + tile - 1)
                nc.scalar.activation(probsT[tile % 2][:, :, bass.ds(i - tile * GT, 1), :].rearrange("p t g r -> p t (g r)"),
                                     psT[n][:], ACT.Copy).then_inc(probsT_ready, 1)

            def keep_values(b, tile):
                act.wait_ge(values_ready, b * KT + tile + 1)
                if not (is_first(b) and tile < 2):
                    act.wait_ge(values_stored[tile % 2], (b * KT // 2 + tile // 2) * 4 * 16)
                nc.scalar.activation(values_out[tile % 2][:], psV, ACT.Copy).then_inc(values_kept, 1)

            def step(b, i, n, tile=None):
                keep(b, i - 2, n, (i - 2) // GT if tile is None else tile)
                exp(b, i, n, i // GT if tile is None else tile)

            def batch(b, more=True):
                step(b, 3, 1)
                if not is_first(b):
                    keep_values(b - 1, KT - 1)
                project(b, VALUES)
                for tile in range(KT):
                    if tile:
                        for i in range(tile * GT, tile * GT + 4):
                            step(b, i, i % 2)
                        keep_values(b, tile - 1)
                    with act.Fori(tile * GT // 2 + 2, (tile + 1) * GT // 2) as t:
                        step(b, t * 2, 0, tile)
                        step(b, t * 2 + 1, 1, tile)
                if more:
                    act.wait_ge(scores_ready, (b + 1) * NG)
                    project(b + 1, KEYS)
                keep(b, NG - 2, 0, KT - 1)
                if more:
                    exp(b + 1, 0, 0, 0)
                keep(b, NG - 1, 1, KT - 1)
                if more:
                    exp(b + 1, 1, 1, 0)
                    keep(b + 1, 0, 0, 0)
                    exp(b + 1, 2, 0, 0)

            project(0, KEYS)
            exp(0, 0, 0, 0)
            exp(0, 1, 1, 0)
            keep(0, 0, 0, 0)
            exp(0, 2, 0, 0)
            batch(0)
            with act.Fori(1, B - 1) as b:
                batch(b)
            batch(B - 1, more=False)
            keep_values(B - 1, KT - 1)

        @block.vector
        def _(dve):
            dve.wait_ge(consts_in, N_CONST)

            def project(b, part):
                for n, (kind, m) in list(enumerate(projections))[part]:
                    if n % 2:
                        continue
                    dve.wait_ge(projected, b * len(projections) + n + 1)
                    if kind == "v":
                        mm = nc.vector.tensor_copy(v[:, m, 0:E], psP[0][:, 0:E])
                    else:
                        mm = nc.vector.tensor_scalar(kT[:, m, :], psP[0][:],
                                                     bk[:, m:m + 1], None, ALU.add)
                    mm.then_inc(kept_dve, 1)

            def maxima(b, i, n, tile):
                dve.wait_ge(scores_ready, b * NG + i + 1)
                for side, keys in enumerate(near_far(tile)):
                    last = nc.vector.tensor_reduce(part_max[n][:, side:side + 1], psS[n][:, keys], AX_X, ALU.max, negate=True)
                last.then_inc(part_max_ready, 1)

            def exponents_bias(b, i, n):
                dve.wait_ge(part_max_ready, b * NG + i + 1)
                near, beyond = part_max[n][:, 0:1], part_max[n][:, 1:2]
                far_score = far_in[:, bass.ds(b % 2 * NG + i, 1)]
                nc.vector.tensor_scalar(negmax[n][:, 0:1], beyond, far_score, near, ALU.subtract, ALU.min)
                nc.vector.tensor_scalar(negmax[n][:, 1:2], near, far_score, beyond, ALU.add, ALU.min).then_inc(max_ready, 1)

            def add_sums(b, i, n):
                dve.wait_ge(exp_ready, b * NG + i + 1)
                nc.vector.tensor_reduce(total[n][:], sums[:, bass.ds(b % 2 * NG + i, 1), :].rearrange("p g i -> p (g i)"), AX_X, ALU.add)\
                    .then_inc(norm_step, 1)

            def invert(b, i, n):
                dve.wait_ge(norm_step, 2 * (b * NG + i) + 1)
                nc.vector.reciprocal(inv[:, bass.ds(b % 2 * NG + i, 1)], total[n][:]).then_inc(norm_step, 1)

            def scale(b, i, n):
                dve.wait_ge(norm_step, 2 * (b * NG + i) + 2)
                nc.vector.tensor_scalar(probs[n][:], probs[n][:], inv[:, bass.ds(b % 2 * NG + i, 1)], None, ALU.mult).then_inc(weights_ready, 1)

            def pick(b, i, n):
                dve.wait_ge(rel_ready, b * NG + i + 1)
                nc.vector.tensor_tensor(picked[n][:], psR[n][:, 0:P], out_mask[:], ALU.mult).then_inc(rel_read, 1)

            def collect(b, i, n):
                dve.wait_ge(rel_read, b * NG + i + 1)
                nc.vector.tensor_reduce(rel_out[:, bass.ds(b % 2 * NG + i, 1), :].rearrange("p g e -> p (g e)"),
                                        picked[n][:].rearrange("p (j e) -> p e j", e=D), AX_X, ALU.add).then_inc(reduced, 1)

            def work(n, tile, maxima_of, scale_of, pick_of):
                if maxima_of:
                    maxima(*maxima_of, n, tile)
                if scale_of:
                    add_sums(*scale_of, 1 - n)
                if pick_of:
                    pick(*pick_of, n)
                if maxima_of:
                    exponents_bias(*maxima_of, n)
                if scale_of:
                    invert(*scale_of, 1 - n)
                if pick_of:
                    collect(*pick_of, n)
                if scale_of:
                    scale(*scale_of, 1 - n)

            def finish(b):
                chain = Chain(dve, finish_step, 2, b)
                groups = bass.ds(b % 2 * NG, NG)
                dve.wait_ge(reduced, b * NG + NG)
                half = NG // 2
                chain.link(nc.vector.tensor_tensor(far[:], sums[:, groups, 1], inv[:, groups], ALU.mult))
                for side in range(2):
                    last = nc.vector.tensor_tensor(
                        far_out[:, side * half:(side + 1) * half, :], far[:, side * half:(side + 1) * half].unsqueeze(2).to_broadcast([P, half, D]),
                        relv_far[:, side, :].unsqueeze(1).to_broadcast([P, half, D]), ALU.mult)
                chain.link(last)
                nc.vector.tensor_tensor(rel_out[:, groups, :], rel_out[:, groups, :], far_out[:], ALU.add).then_inc(finished, 1)
                chain.end()

            def step(b, i, n, tile=None):
                work(n, i // GT if tile is None else tile, (b, i), (b, i - 1),
                     None if isinstance(i, int) and i < 4 else (b, i - 4))

            def batch(b, more=True):
                if not is_first(b):
                    dve.wait_ge(rel_free, b)
                step(b, 3, 1)
                project(b, VALUES)
                for tile in range(KT):
                    if tile:
                        for i in range(tile * GT, tile * GT + 4):
                            step(b, i, i % 2)
                    with dve.Fori(tile * GT // 2 + 2, (tile + 1) * GT // 2) as t:
                        step(b, t * 2, 0, tile)
                        step(b, t * 2 + 1, 1, tile)
                if more:
                    dve.wait_ge(scores_ready, (b + 1) * NG)
                    project(b + 1, KEYS)
                    dve.wait_ge(far_scores_in, (b + 2) * 16 * HALVES * QG)
                following = [(b + 1, i) if more else None for i in range(3)]
                work(0, 0, following[0], (b, NG - 1), (b, NG - 4))
                work(1, 0, following[1], following[0], (b, NG - 3))
                work(0, 0, following[2], following[1], (b, NG - 2))
                work(1, 0, None, None, (b, NG - 1))
                finish(b)

            project(0, KEYS)
            dve.wait_ge(far_scores_in, 16 * HALVES * QG)
            work(0, 0, (0, 0), None, None)
            work(1, 0, (0, 1), (0, 0), None)
            work(0, 0, (0, 2), (0, 1), None)
            batch(0)
            with dve.Fori(1, B - 1) as b:
                batch(b)
            batch(B - 1, more=False)


def take_moments(nc, r, stats, moments, engine, step, base, moments_ready):
    for t in range(QT):
        last = nc.vector.bn_stats(stats[:, t, :], r[:, t, :])
    last.then_inc(step, 1)
    engine.wait_ge(step, base + 1)
    engine.sem_inc(step, 1)
    for t in range(QT):
        last = nc.vector.bn_aggr(moments[:, t, :], stats[:, t, :])
    last.then_inc(moments_ready, 1)


def deviation(nc, act, turn, moments, rstd, eps, moments_ready, deviation_ready):
    act.wait_ge(moments_ready, turn + 1)
    nc.scalar.activation(rstd[:], moments[:, :, 1], ACT.Sqrt, bias=eps[:]).then_inc(deviation_ready, 1)


def apply_norm(nc, r, out, moments, rstd, engine, step, base, turn, deviation_ready):
    engine.wait_ge(deviation_ready, turn + 1)
    nc.vector.reciprocal(rstd[:], rstd[:]).then_inc(step, 1)
    engine.wait_ge(step, base + 3)
    for t in range(QT):
        last = nc.vector.tensor_scalar(out[:, t, :], r[:, t, :], moments[:, t, 0:1], rstd[:, t:t + 1],
                                       ALU.subtract, ALU.mult)
    return last


def cross_attention(nc, d, attnT, rel, x2_rows, acc_rows, gate_scores):
    with ExitStack() as ctx:
        def sb(name, shape, dt=F32):
            return ctx.enter_context(nc.sbuf_tensor("x_" + name, shape, dt))

        def ps(name, shape):
            return ctx.enter_context(nc.psum_tensor("x_" + name, shape, F32))

        def sem(name):
            return ctx.enter_context(nc.semaphore("x_" + name))

        PAIRS = H // 2
        wo, wq, wk, wv, wo2 = (sb(n, [P, HALVES, E]) for n in ("wo", "wq", "wk", "wv", "wo2"))
        wg = sb("wg", [P, HALVES, NX])
        bo, bo2 = sb("bo", [P, E]), sb("bo2", [P, E])
        bv, ones = sb("bv", [1, E]), sb("ones", [1, P])
        bq, bqs, bk = (sb(n, [P, HALVES]) for n in ("bq", "bqs", "bk"))
        ident = sb("ident", [P, P])
        half_mask = sb("half_mask", [P, HH])
        pair_mask = sb("pair_mask", [P, 2 * D])
        mask_in = sb("mask_in", [P, QT, SK], I32)
        keep = sb("keep", [P, QT, SK])
        fill = sb("fill", [P, QT, SK])
        ctxT = sb("ctxT", [P, HALVES, B // 2, 2, SK])
        kT = sb("kT", [P, HALVES, B, SK])
        v = sb("v", [P, B, E])
        kdiag = sb("kdiag", [P, HALVES, HH, SK])
        vdiag = sb("vdiag", [P, PAIRS, 2 * D])
        x_sb, rel_sb, xb = (sb(n, [P, QT, E]) for n in ("x_sb", "rel_sb", "xb"))
        attnT_sb = sb("attnT_sb", [P, 2 * HALVES, S])
        r1, r2, x1, x2 = (sb(n, [P, QT, E]) for n in ("r1", "r2", "x1", "x2"))
        x1b = sb("x1b", [P, 2, QT, E])
        aT, x1T, qT, oT, x2T = (sb(n, [P, HALVES, S]) for n in ("aT", "x1T", "qT", "oT", "x2T"))
        sc = [sb(f"sc{i}", [P, H, SK]) for i in range(QT)]
        pr = [sb(f"pr{i}", [P, H, SK]) for i in range(QT)]
        prT = sb("prT", [P, PAIRS, QT, P])
        negmax, inv = (sb(n, [P, QT, H]) for n in ("negmax", "inv"))
        stats1, stats2 = sb("stats1", [P, QT, 6]), sb("stats2", [P, QT, 6])
        moments1, moments2 = sb("moments1", [P, QT, 2]), sb("moments2", [P, QT, 2])
        rstd1, rstd2 = sb("rstd1", [P, QT]), sb("rstd2", [P, QT])
        eneg = sb("eneg", [P, QT, NX])
        eps = sb("eps", [P, 1])
        zeros = sb("zeros", [P, QT, E])

        bankT = [ps(f"bankT{i}", [P, 4, P]) for i in range(2)]
        bankR = [ps(f"bankR{i}", [P, 2, E]) for i in range(2)]
        bankS = [ps(f"bankS{i}", [P, H, SK]) for i in range(2)]

        w_in = sem("w_in")
        ctx_in = sem("ctx_in")
        zeros_ready = sem("zeros_ready")
        ones_ready = sem("ones_ready")
        eps_ready = sem("eps_ready")
        mask_ready = sem("mask_ready")
        ctx_projected = sem("ctx_projected")
        ctx_kept = sem("ctx_kept")
        attn_in = sem("attn_in")
        x_in = sem("x_in")
        rel_in = sem("rel_in")
        xb_ready = sem("xb_ready")
        x1b_ready = sem("x1b_ready")
        bankT_full = sem("bankT_full")
        bankT_empty = [sem(f"bankT_empty{i}") for i in range(2)]
        bankR_full = sem("bankR_full")
        bankR_empty = [sem(f"bankR_empty{i}") for i in range(2)]
        bankS_full = sem("bankS_full")
        bankS_empty = sem("bankS_empty")
        kdiag_ready = sem("kdiag_ready")
        vdiag_ready = sem("vdiag_ready")
        filled = sem("filled")
        max_ready = sem("max_ready")
        shifted = sem("shifted")
        exp_ready = sem("exp_ready")
        weights_ready = sem("weights_ready")
        x1_ready = sem("x1_ready")
        x2_ready = sem("x2_ready")
        x2_free = sem("x2_free")
        stored = sem("stored")
        zero_stored = sem("zero_stored")
        soft_step = sem("soft_step")
        gate_step = sem("gate_step")
        norm1_step, norm2_step = sem("norm1_step"), sem("norm2_step")
        moments1_ready, moments2_ready = sem("moments1_ready"), sem("moments2_ready")
        deviation1_ready, deviation2_ready = sem("deviation1_ready"), sem("deviation2_ready")

        weights = [
            (ident, d["ident"]), (wk, d["x_wkT"].rearrange("(a p) o -> p a o", p=P)), (bk, d["x_bk"]),
            (wv, d["x_wvT"].rearrange("(a p) o -> p a o", p=P)), (bv, d["x_bv"]),
            (wo, d["a_woT"].rearrange("(a p) o -> p a o", p=P)), (bo, d["a_bo"]),
            (wq, d["x_wqT"].rearrange("(a p) o -> p a o", p=P)), (bq, d["x_bq"]),
            (wo2, d["x_woT"].rearrange("(a p) o -> p a o", p=P)), (bo2, d["x_bo"]),
            (wg, d["gate_wT"].rearrange("(a p) o -> p a o", p=P)),
            (half_mask, d["half_mask"]), (pair_mask, d["pair_mask"]),
            (mask_in, d["mask"].rearrange("(t p) k -> p t k", p=P)),
        ]
        N_W = 16 * len(weights)

        class Uses:

            def __init__(self, first, turn):
                self.first, self.turn = first, turn

            def at(self, b, name, kinds="qxz"):
                if b is None:
                    return self.first.index(name)
                names = [n for n in self.turn if n[0] not in "qxz" or n[0] in kinds]
                n = names.index(name) + len(self.first)
                if isinstance(b, int) and b == 0:
                    return n
                missing = "zx" if isinstance(b, int) and b == B - 1 else "z"
                return b * len(self.turn) + n - sum(m[0] in missing for m in self.turn)

        usesT = Uses(["x_a of 0", "q_x1 of 0", "q_q of 0", "x_a of 1"],
                     ["q_x1", "q_q", "z_x2", "w0", "w1", "x_a", "w2", "w3", "out"])
        usesR = Uses(["x_proj of 0", "x_proj of 1"], ["z_gate", "x_proj", "proj"])

        def flat(bank):
            return bank[:].rearrange("p a b -> p (a b)")

        def rows(dram, b):
            return dram[bass.ds(b * S, S), :].rearrange("(t p) e -> p t e", p=P)

        block = ctx.enter_context(nc.Block())

        @block.sync
        def _(sp):
            for dst, src in weights:
                sp.dma_start(dst[:], src).then_inc(w_in, 16)

            def load_ctx(half):
                for a in range(HALVES):
                    sp.dma_start(ctxT[:, a], d["ctxT"][a * P:(a + 1) * P, half * (B // 2):(half + 1) * (B // 2)]).then_inc(ctx_in, 16)

            def load_attn(b):
                sp.dma_start(attnT_sb[:, bass.ds(b % 2 * HALVES, HALVES), :],
                             attnT[bass.ds(b, 1)].rearrange("b (a p) s -> p (b a) s", p=P)).then_inc(attn_in, 16)

            def load_rel(b):
                sp.dma_start(rel_sb[:], rows(rel, b)).then_inc(rel_in, 16)

            def load_x(b):
                sp.dma_start(x_sb[:], rows(d["x"], b)).then_inc(x_in, 16)

            def store(b):
                sp.wait_ge(x2_ready, b + 1)
                for dram in (x2_rows, acc_rows[0]):
                    sp.dma_start(rows(dram, b), x2[:]).then_inc(stored, 16)
                sp.dma_start(rows(acc_rows[1], b), zeros[:]).then_inc(stored, 16)

            def stored_all(b):
                sp.wait_ge(stored, (b + 1) * 48)
                sp.sem_inc(x2_free, 1)

            load_ctx(0)
            load_attn(0)
            load_rel(0)
            load_x(0)
            sp.sem_inc(x2_free, 1)
            sp.wait_ge(ctx_projected, CTX_STEPS)
            load_ctx(1)
            sp.wait_ge(zeros_ready, 1)
            for dram in (x2_rows, *acc_rows):
                sp.dma_start(dram[TOK:TOK + CAP, :].rearrange("(t p) e -> p t e", p=P), zeros[:, 0:CAP // P, :])\
                    .then_inc(zero_stored, 16)

            def next_x(b):
                sp.wait_ge(xb_ready, b)
                load_x(b)

            def load(b):
                sp.wait_ge(x1_ready, b)
                load_attn(b)
                load_rel(b)

            next_x(1)
            load(1)
            next_x(2)
            load(2)
            next_x(3)
            with sp.Fori(3, B - 1) as b:
                load(b)
                next_x(b + 1)
                store(b - 3)
                stored_all(b - 3)
            load(B - 1)
            store(B - 4)
            stored_all(B - 4)
            for b in range(B - 3, B):
                store(b)
                stored_all(b)
            sp.wait_ge(zero_stored, 48)

        @block.gpsimd
        def _(pool):
            pool.memset(zeros[:], 0.0).then_inc(zeros_ready, 1)
            pool.memset(ones[:], 1.0).then_inc(ones_ready, 1)
            pool.memset(eps[:], EPS).then_inc(eps_ready, 1)
            pool.wait_ge(w_in, N_W)
            pool.wait_ge(mask_ready, 1)

            def inputs(b):
                if not (isinstance(b, int) and b == 0):
                    pool.wait_ge(x1_ready, b)
                pool.wait_ge(x_in, b * 16 + 16)
                nc.gpsimd.tensor_tensor(xb[:], x_sb[:], bo[:].unsqueeze(1).to_broadcast([P, QT, E]), ALU.add).then_inc(xb_ready, 1)

            def residual(b):
                pool.wait_ge(x1_ready, b + 1)
                nc.gpsimd.tensor_tensor(x1b[:, bass.ds(b % 2, 1)].rearrange("p i t e -> p (i t) e"), x1[:],
                                        bo2[:].unsqueeze(1).to_broadcast([P, QT, E]), ALU.add).then_inc(x1b_ready, 1)

            def diag_k(b):
                for a in range(HALVES):
                    mm = nc.gpsimd.tensor_tensor(
                        kdiag[:, a, :, :], kT[:, a, bass.ds(b, 1), :].to_broadcast([P, HH, SK]),
                        half_mask[:].unsqueeze(2).to_broadcast([P, HH, SK]), ALU.mult)
                mm.then_inc(kdiag_ready, 1)

            def diag_v(b):
                nc.gpsimd.tensor_tensor(
                    vdiag[:], v[:, bass.ds(b, 1), :].rearrange("p b (g c) -> p (b g) c", c=2 * D),
                    pair_mask[:].unsqueeze(1).to_broadcast([P, PAIRS, 2 * D]), ALU.mult).then_inc(vdiag_ready, 1)

            def tiles(b, t0):
                for t in (t0, t0 + 1):
                    pool.wait_ge(bankS_empty, b * QT + t + 3)
                    nc.gpsimd.tensor_tensor(sc[t][:], sc[t][:], fill[:, t, :].unsqueeze(1).to_broadcast([P, H, SK]),
                                            ALU.add).then_inc(filled, 1)
                for t in (t0, t0 + 1):
                    pool.wait_ge(max_ready, b * QT + t + 1)
                    nc.gpsimd.tensor_tensor(sc[t][:], sc[t][:], negmax[:, t, :].unsqueeze(2).to_broadcast([P, H, SK]),
                                            ALU.add).then_inc(shifted, 1)

            def turn(b, kinds="qxz"):
                if "x" in kinds:
                    inputs(b + 2)
                tiles(b, 0)
                if "q" in kinds:
                    if not (isinstance(b, int) and b == 0):
                        pool.wait_ge(bankR_empty[1], usesR.at(b, "z_gate", kinds) + 1)
                    residual(b + 1)
                tiles(b, 2)
                if "q" in kinds:
                    diag_k(b + 1)
                    pool.wait_ge(bankT_full, 2 * usesT.at(b, "out", kinds) + 2)
                    diag_v(b + 1)

            inputs(0)
            pool.wait_ge(ctx_kept, 2 * CTX_STEPS)
            diag_k(0)
            diag_v(0)
            residual(0)
            inputs(1)
            turn(0, "qx")
            with pool.Fori(1, B - 2) as b:
                turn(b)
            turn(B - 2, "qz")
            turn(B - 1, "z")

        @block.tensor
        def _(pe):
            pe.wait_ge(w_in, N_W)
            pe.wait_ge(ones_ready, 1)
            n = 0
            for half in range(2):
                pe.wait_ge(ctx_in, 32 * (half + 1))
                for m in range(HALVES):
                    if n >= 2:
                        pe.wait_ge(ctx_kept, n - 1)
                    for a in range(HALVES):
                        mm = nc.tensor.matmul(flat(bankT[n % 2]), wk[:, a, m * P:(m + 1) * P], ctxT[:, a, :, 0, :],
                                              start=a == 0, stop=a == HALVES - 1)
                    mm.then_inc(ctx_projected, 1)
                    n += 1
                for c in range(B // 4):
                    pe.wait_ge(ctx_kept, n - 1)
                    for i in range(2):
                        dst = flat(bankT[n % 2])[:, i * E:(i + 1) * E]
                        for a in range(HALVES):
                            nc.tensor.matmul(dst, ctxT[:, a, 2 * c + i].rearrange("p a b -> p (a b)"), wv[:, a, :], start=a == 0, stop=False)
                        mm = nc.tensor.matmul(dst, ones[:], bv[:], start=False, stop=True)
                    mm.then_inc(ctx_projected, 1)
                    n += 1
            pe.wait_ge(ctx_kept, n)

            def take(kind, at, i):
                banks, empty = {"T": (bankT, bankT_empty), "R": (bankR, bankR_empty)}[kind]
                pe.wait_ge(empty[i], at + 1)
                return banks[i]

            def transpose_rows(src, at):
                for a in range(HALVES):
                    bank = take("T", at, a)
                    for t in range(QT):
                        mm = nc.tensor.transpose(bank[:, t, :], src[:, t, a * P:(a + 1) * P], ident[:])
                    mm.then_inc(bankT_full, 1)

            def in_sbuf(at):
                for i in range(2):
                    pe.wait_ge(bankT_empty[i], at + 2)

            def project(src, w, cols, at):
                for i in range(2):
                    bank = take("R", at, i)
                    for u in range(2):
                        t = 2 * i + u
                        for a in range(HALVES):
                            mm = nc.tensor.matmul(bank[:, u, 0:cols], src[:, a, t * P:(t + 1) * P], w[:, a, :],
                                                  start=a == 0, stop=a == HALVES - 1)
                    mm.then_inc(bankR_full, 1)

            def rel_transposed(b, at):
                pe.wait_ge(rel_in, b * 16 + 16)
                transpose_rows(rel_sb, at)

            def projected(atT, atR):
                in_sbuf(atT)
                project(aT, wo, E, atR)

            def x1_transposed(b, at):
                pe.wait_ge(x1_ready, b + 1)
                transpose_rows(x1, at)

            def queries(at1, at):
                in_sbuf(at1)
                for m in range(HALVES):
                    bank = take("T", at, m)
                    for a in range(HALVES):
                        mm = nc.tensor.matmul(flat(bank), wq[:, a, m * P:(m + 1) * P], x1T[:, a, :],
                                              start=a == 0, stop=a == HALVES - 1)
                    mm.then_inc(bankT_full, 1)

            def first_scores(b):
                pe.wait_ge(kdiag_ready, b + 1)
                scores(b, 0)
                scores(b, 1)

            def scores(b, t):
                pe.wait_ge(bankS_empty, b * QT + t + 1)
                for a in range(HALVES):
                    mm = nc.tensor.matmul(bankS[t % 2][:, a * HH:(a + 1) * HH, :].rearrange("p h k -> p (h k)"),
                                          qT[:, a, t * P:(t + 1) * P], kdiag[:, a, :, :].rearrange("p h k -> p (h k)"),
                                          start=True, stop=True)
                mm.then_inc(bankS_full, 1)

            def transpose_weights(b, t, at):
                pe.wait_ge(weights_ready, b * QT + t + 1)
                for c in range(2):
                    bank = take("T", at, c)
                    for g in range(4):
                        h = 2 * (4 * c + g)
                        mm = nc.tensor.transpose(bank[:, g, :], pr[t][:, h:h + 2, :].rearrange("p h k -> p (h k)"), ident[:])
                    mm.then_inc(bankT_full, 1)

            def outputs(b, at3, at):
                pe.wait_ge(vdiag_ready, b + 1)
                in_sbuf(at3)
                for c in range(2):
                    bank = take("T", at, c)
                    for g in range(4):
                        mm = nc.tensor.matmul(flat(bank)[g * 2 * D:(g + 1) * 2 * D, :], vdiag[:, 4 * c + g, :],
                                              prT[:, 4 * c + g, :, :].rearrange("p t q -> p (t q)"), start=True, stop=True)
                    mm.then_inc(bankT_full, 1)

            def turn(b, kinds="qxz"):
                def atT(name):
                    return usesT.at(b, name, kinds)

                def atR(name):
                    return usesR.at(b, name, kinds)

                if "q" in kinds:
                    x1_transposed(b + 1, atT("q_x1"))
                scores(b, 2)
                scores(b, 3)
                if "q" in kinds:
                    queries(atT("q_x1"), atT("q_q"))
                if "z" in kinds:
                    pe.wait_ge(x2_ready, b)
                    transpose_rows(x2, atT("z_x2"))
                    in_sbuf(atT("z_x2"))
                    project(x2T, wg, NX, atR("z_gate"))
                transpose_weights(b, 0, atT("w0"))
                transpose_weights(b, 1, atT("w1"))
                if "x" in kinds:
                    rel_transposed(b + 2, atT("x_a"))
                if "x" in kinds:
                    projected(atT("x_a"), atR("x_proj"))
                transpose_weights(b, 2, atT("w2"))
                transpose_weights(b, 3, atT("w3"))
                outputs(b, atT("w3"), atT("out"))
                if "q" in kinds:
                    first_scores(b + 1)
                in_sbuf(atT("out"))
                project(oT, wo2, E, atR("proj"))

            def before(b):
                rel_transposed(b, usesT.at(None, f"x_a of {b}"))
                projected(usesT.at(None, f"x_a of {b}"), usesR.at(None, f"x_proj of {b}"))

            before(0)
            x1_transposed(0, usesT.at(None, "q_x1 of 0"))
            queries(usesT.at(None, "q_x1 of 0"), usesT.at(None, "q_q of 0"))
            before(1)
            first_scores(0)
            turn(0, "qx")
            with pe.Fori(1, B - 2) as b:
                turn(b)
            turn(B - 2, "qz")
            turn(B - 1, "z")
            pe.wait_ge(x2_ready, B)
            end = usesT.at(B - 1, "out", "z") + 1
            transpose_rows(x2, end)
            in_sbuf(end)
            project(x2T, wg, NX, usesR.at(B - 1, "proj", "z") + 1)

        @block.scalar
        def _(act):
            act.sem_inc(bankT_empty[0], 1)
            act.wait_ge(mask_ready, 1)
            act.wait_ge(eps_ready, 1)
            act.wait_ge(w_in, N_W)

            def keep_half(at, dst):
                act.wait_ge(bankT_full, 2 * at + 1)
                nc.scalar.activation(dst[:, 0, :], flat(bankT[0]), ACT.Copy).then_inc(bankT_empty[0], 1)

            def keep_both(at, dst):
                for a in range(HALVES):
                    act.wait_ge(bankT_full, 2 * at + a + 1)
                    nc.scalar.activation(dst[:, a, :], flat(bankT[a]), ACT.Copy).then_inc(bankT_empty[a], 1)

            def queries(at):
                for a in range(HALVES):
                    act.wait_ge(bankT_full, 2 * at + a + 1)
                    nc.scalar.activation(qT[:, a, :], flat(bankT[a]), ACT.Identity, bias=bqs[:, a:a + 1], scale=SC).then_inc(bankT_empty[a], 1)

            def exp(b, t):
                act.wait_ge(shifted, b * QT + t + 1)
                nc.scalar.activation(pr[t][:], sc[t][:], ACT.Exp).then_inc(exp_ready, 1)

            def keep_weights(t, at):
                for c in range(2):
                    act.wait_ge(bankT_full, 2 * at + c + 1)
                    nc.scalar.activation(prT[:, 4 * c:4 * c + 4, t, :], bankT[c][:], ACT.Copy).then_inc(bankT_empty[c], 1)

            def gate(at):
                for i in range(2):
                    act.wait_ge(bankR_full, 2 * at + i + 1)
                    nc.scalar.activation(eneg[:, 2 * i:2 * i + 2, :], bankR[i][:, :, 0:NX], ACT.Exp, scale=-1.0).then_inc(bankR_empty[i], 1)

            def turn(b, kinds="qxz"):
                def atT(name):
                    return usesT.at(b, name, kinds)

                if "q" in kinds:
                    keep_both(atT("q_x1"), x1T)
                if "z" in kinds:
                    deviation(nc, act, b - 1, moments2, rstd2, eps, moments2_ready, deviation2_ready)
                exp(b, 0)
                if "q" in kinds:
                    queries(atT("q_q"))
                if "z" in kinds:
                    keep_both(atT("z_x2"), x2T)
                exp(b, 1)
                if "z" in kinds:
                    gate(usesR.at(b, "z_gate", kinds))
                keep_weights(0, atT("w0"))
                keep_weights(1, atT("w1"))
                exp(b, 2)
                exp(b, 3)
                keep_weights(2, atT("w2"))
                keep_weights(3, atT("w3"))
                if "x" in kinds:
                    deviation(nc, act, b + 2, moments1, rstd1, eps, moments1_ready, deviation1_ready)
                keep_half(atT("out"), oT)

            deviation(nc, act, 0, moments1, rstd1, eps, moments1_ready, deviation1_ready)
            keep_both(usesT.at(None, "q_x1 of 0"), x1T)
            queries(usesT.at(None, "q_q of 0"))
            deviation(nc, act, 1, moments1, rstd1, eps, moments1_ready, deviation1_ready)
            turn(0, "qx")
            with act.Fori(1, B - 2) as b:
                turn(b)
            turn(B - 2, "qz")
            turn(B - 1, "z")
            deviation(nc, act, B - 1, moments2, rstd2, eps, moments2_ready, deviation2_ready)
            keep_both(usesT.at(B - 1, "out", "z") + 1, x2T)
            gate(usesR.at(B - 1, "proj", "z") + 1)

        @block.vector
        def _(dve):
            dve.sem_inc(bankT_empty[1], 1)
            dve.sem_inc(bankR_empty[0], 1)
            dve.sem_inc(bankR_empty[1], 1)
            dve.sem_inc(bankS_empty, 2)
            dve.wait_ge(w_in, N_W)
            nc.vector.tensor_scalar(bqs[:], bq[:], SC, None, ALU.mult)
            nc.vector.tensor_scalar(keep[:], mask_in[:], 0, None, ALU.not_equal)
            nc.vector.tensor_scalar(fill[:], mask_in[:], 0, NEG, ALU.is_equal, ALU.mult).then_inc(mask_ready, 1)
            n = 0
            for half in range(2):
                for m in range(HALVES):
                    n += 1
                    dve.wait_ge(ctx_projected, n)
                    nc.vector.tensor_scalar(
                        kT[:, m, half * (B // 2):(half + 1) * (B // 2), :].rearrange("p b k -> p (b k)"),
                        flat(bankT[(n - 1) % 2]), bk[:, m:m + 1], None, ALU.add).then_inc(ctx_kept, 1)
                for c in range(B // 4):
                    n += 1
                    dve.wait_ge(ctx_projected, n)
                    at = half * (B // 2) + 2 * c
                    nc.vector.tensor_copy(v[:, at:at + 2, :].rearrange("p b e -> p (b e)"), flat(bankT[(n - 1) % 2])).then_inc(ctx_kept, 1)
            dve.wait_ge(mask_ready, 1)

            def keep_half(at, dst):
                dve.wait_ge(bankT_full, 2 * at + 2)
                nc.vector.tensor_copy(dst[:, 1, :], flat(bankT[1])).then_inc(bankT_empty[1], 1)

            def add_parts(b, at):
                dve.wait_ge(attn_in, b * 16 + 16)
                for a in range(HALVES):
                    dve.wait_ge(bankT_full, 2 * at + a + 1)
                    nc.vector.tensor_tensor(
                        aT[:, a, :], flat(bankT[a]), attnT_sb[:, bass.ds(b % 2 * HALVES + a, 1), :].rearrange("p a s -> p (a s)"),
                        ALU.add).then_inc(bankT_empty[a], 1)

            def residual(at, x, r):
                for i in range(2):
                    dve.wait_ge(bankR_full, 2 * at + i + 1)
                    nc.vector.tensor_tensor(r[:, 2 * i:2 * i + 2, :], bankR[i][:], x(i), ALU.add).then_inc(bankR_empty[i], 1)
                for i in range(2):
                    dve.wait_ge(bankR_empty[i], at + 2)

            def first_moments(b, at):
                dve.wait_ge(xb_ready, b + 1)
                residual(at, lambda i: xb[:, 2 * i:2 * i + 2, :], r1)
                take_moments(nc, r1, stats1, moments1, dve, norm1_step, b * NORM_STEPS, moments1_ready)

            def first_norm(b):
                if not (isinstance(b, int) and b == 0):
                    dve.wait_ge(x1b_ready, b)
                apply_norm(nc, r1, x1, moments1, rstd1, dve, norm1_step, b * NORM_STEPS, b, deviation1_ready).then_inc(x1_ready, 1)

            def second_residual(b, at):
                dve.wait_ge(x1b_ready, b + 1)
                residual(at, lambda i: x1b[:, bass.ds(b % 2, 1), 2 * i:2 * i + 2, :].rearrange("p o t e -> p (o t) e"), r2)

            def second_moments(b):
                take_moments(nc, r2, stats2, moments2, dve, norm2_step, b * NORM_STEPS, moments2_ready)

            def second_norm(b):
                dve.wait_ge(x2_free, b + 1)
                apply_norm(nc, r2, x2, moments2, rstd2, dve, norm2_step, b * NORM_STEPS, b, deviation2_ready).then_inc(x2_ready, 1)

            def take_scores(b, t):
                dve.wait_ge(bankS_full, b * QT + t + 1)
                nc.vector.tensor_tensor(sc[t][:], bankS[t % 2][:], keep[:, t, :].unsqueeze(1).to_broadcast([P, H, SK]),
                                        ALU.mult).then_inc(bankS_empty, 1)

            def rowmax(b, t):
                dve.wait_ge(filled, b * QT + t + 1)
                nc.vector.tensor_reduce(negmax[:, t, :], sc[t][:], AX_X, ALU.max, negate=True).then_inc(max_ready, 1)

            def divide(b, t):
                step = b * 2 * QT + 2 * t
                dve.wait_ge(exp_ready, b * QT + t + 1)
                nc.vector.tensor_reduce(inv[:, t, :], pr[t][:], AX_X, ALU.add).then_inc(soft_step, 1)
                dve.wait_ge(soft_step, step + 1)
                nc.vector.reciprocal(inv[:, t, :], inv[:, t, :]).then_inc(soft_step, 1)
                dve.wait_ge(soft_step, step + 2)
                nc.vector.tensor_tensor(pr[t][:], pr[t][:], inv[:, t, :].unsqueeze(2).to_broadcast([P, H, SK]),
                                        ALU.mult).then_inc(weights_ready, 1)

            def gate(b, at):
                for i in range(2):
                    dve.wait_ge(bankR_empty[i], at + 2)
                nc.vector.tensor_scalar(eneg[:], eneg[:], 1.0, None, ALU.add).then_inc(gate_step, 1)
                dve.wait_ge(gate_step, 2 * b + 1)
                nc.vector.reciprocal(gate_scores[:, bass.ds(b * QT, QT), :], eneg[:]).then_inc(gate_step, 1)

            def turn(b, kinds="qxz"):
                def atT(name):
                    return usesT.at(b, name, kinds)

                def atR(name):
                    return usesR.at(b, name, kinds)

                if "z" in kinds:
                    second_moments(b - 1)
                rowmax(b, 0)
                rowmax(b, 1)
                if "z" in kinds:
                    second_norm(b - 1)
                take_scores(b, 2)
                take_scores(b, 3)
                divide(b, 0)
                divide(b, 1)
                rowmax(b, 2)
                rowmax(b, 3)
                if "x" in kinds:
                    add_parts(b + 2, atT("x_a"))
                divide(b, 2)
                divide(b, 3)
                if "x" in kinds:
                    first_moments(b + 2, atR("x_proj"))
                if "z" in kinds:
                    gate(b - 1, atR("z_gate"))
                if "x" in kinds:
                    first_norm(b + 2)
                keep_half(atT("out"), oT)
                if "q" in kinds:
                    take_scores(b + 1, 0)
                    take_scores(b + 1, 1)
                second_residual(b, atR("proj"))

            def before(b):
                add_parts(b, usesT.at(None, f"x_a of {b}"))
                first_moments(b, usesR.at(None, f"x_proj of {b}"))
                first_norm(b)

            before(0)
            before(1)
            take_scores(0, 0)
            take_scores(0, 1)
            turn(0, "qx")
            with dve.Fori(1, B - 2) as b:
                turn(b)
            turn(B - 2, "qz")
            turn(B - 1, "z")
            second_moments(B - 1)
            second_norm(B - 1)
            gate(B - 1, usesR.at(B - 1, "proj", "z") + 1)


def route(nc, d, gate_scores, slot_token, slot_weight, slot_index, slot_scale):
    with ExitStack() as ctx:
        def sb(name, shape, dt=F32):
            return ctx.enter_context(nc.sbuf_tensor("r_" + name, shape, dt))

        def sem(name):
            return ctx.enter_context(nc.semaphore("r_" + name))

        G = NX // GE
        CH = 512 // NX
        bias = sb("bias", [P, NX])
        before = sb("before", [P, P])
        ones = sb("ones", [P, P])
        ident = sb("ident", [P, P])
        lower = sb("lower", [P, G, G])
        iota = sb("iota", [P, SLOT_B])
        token1 = sb("token1", [P, NT])
        row_empty = sb("row_empty", [P, 2 * NX])
        own_expert = sb("own_expert", [P, GE])

        sfc = sb("sfc", [P, NT, NX])
        hi, lo = sb("hi", [P, NT * G, 4]), sb("lo", [P, NT * G, 4])
        hi2, lo2, lo2b = (sb(n, [P, NT * G, 2]) for n in ("hi2", "lo2", "lo2b"))
        lo3, lo3b = sb("lo3", [P, NT * G]), sb("lo3b", [P, NT * G])
        gscore = sb("gscore", [P, NT, G])
        rank = sb("rank", [P, NT, G])
        work = sb("work", [P, NT, NX])
        work2 = sb("work2", [P, NT, NX])
        top = sb("top", [P, NT, 8])
        mask = sb("mask", [P, NT, NX])
        wsum = sb("wsum", [P, NT])
        ai, bi = sb("ai", [P, NT, NX], I32), sb("bi", [P, NT, NX], I32)
        first = [sb(f"first{i}", [P, CH, GE, SLOT_A]) for i in range(2)]
        second = [sb(f"second{i}", [P, 3, CH, GE, SLOT_B]) for i in range(2)]
        picked = sb("picked", [P, 2, GE, SLOT_B])
        lists = sb("lists", [P, 2, G, SLOT_B])
        block_rows = sb("block_rows", [P, 2, P])

        banks = [ctx.enter_context(nc.psum_tensor(f"r_bank{i}", [P, 512], F32)) for i in range(8)]

        const_in = sem("const_in")
        ones_ready = sem("ones_ready")
        step = sem("step")
        mask_ready = sem("mask_ready")
        counted = sem("counted")
        kept = sem("kept")
        onehot_ready = sem("onehot_ready")
        second_ready = sem("second_ready")
        token_ready = sem("token_ready")
        chunk_done = sem("chunk_done")
        picked_out = sem("picked_out")
        lists_ready = sem("lists_ready")
        lists_stored = sem("lists_stored")
        rows_in = sem("rows_in")
        flipped = sem("flipped")

        consts = [(bias, d["gate_bias"]), (before, d["before"]), (ident, d["ident"]), (lower, d["lower"]),
                  (iota, d["iota"]), (token1, d["token1"]), (row_empty, d["row_empty"]),
                  (own_expert, d["own_expert"])]
        NCHUNK = NT // CH

        block = ctx.enter_context(nc.Block())

        @block.sync
        def _(sp):
            for dst, src in consts:
                sp.dma_start(dst[:], src).then_inc(const_in, 16)
            sp.wait_ge(lists_ready, 1)
            for i, dram in enumerate((slot_token, slot_weight)):
                sp.dma_start(dram.rearrange("(g p b) -> p g b", g=G, b=SLOT_B), lists[:, i]).then_inc(lists_stored, 16)
            sp.wait_ge(lists_stored, 32)
            for i, dram in enumerate((slot_token, slot_weight)):
                sp.dma_start(block_rows[:, i], dram.rearrange("(n q) -> n q", q=P)).then_inc(rows_in, 16)

        @block.tensor
        def _(pe):
            pe.wait_ge(const_in, 16 * len(consts))
            pe.wait_ge(ones_ready, 1)
            pe.wait_ge(mask_ready, 1)
            for c in range(NCHUNK):
                if c >= 4:
                    pe.wait_ge(kept, 2 * (c - 3))
                src = mask[:, c * CH:(c + 1) * CH, :].rearrange("p t e -> p (t e)")
                nc.tensor.matmul(banks[2 * c % 8][:], before[:], src, start=True, stop=True)
                nc.tensor.matmul(banks[(2 * c + 1) % 8][:], ones[:], src, start=True, stop=True).then_inc(counted, 1)
            pe.wait_ge(kept, 2 * NCHUNK)
            n = 0
            for g in range(G):
                if g >= 2:
                    pe.wait_ge(picked_out, g - 1)
                for c in range(NCHUNK):
                    pe.wait_ge(second_ready, n + 1)
                    pe.wait_ge(token_ready, n + 1)
                    for t in range(CH):
                        mm = nc.tensor.matmul(banks[g % 2][:, 0:2 * P], first[n % 2][:, t].rearrange("p e a -> p (e a)"),
                                              second[n % 2][:, 1:3, t].rearrange("p i e b -> p i (e b)"),
                                              start=c == 0 and t == 0, stop=c == NCHUNK - 1 and t == CH - 1)
                    mm.then_inc(chunk_done, 1)
                    n += 1
            pe.wait_ge(rows_in, 32)
            for i in range(2):
                mm = nc.tensor.transpose(banks[2][:, i * P:(i + 1) * P], block_rows[:, i], ident[:])
            mm.then_inc(flipped, 1)

        @block.gpsimd
        def _(pool):
            pool.memset(ones[:], 1.0).then_inc(ones_ready, 1)
            pool.wait_ge(const_in, 16 * len(consts))
            n = 0
            for g in range(G):
                for c in range(NCHUNK):
                    pool.wait_ge(onehot_ready, n + 1)
                    s = second[n % 2]
                    nc.gpsimd.tensor_tensor(
                        s[:, 1].rearrange("p t e b -> p t (e b)"), s[:, 0].rearrange("p t e b -> p t (e b)"),
                        token1[:, c * CH:(c + 1) * CH].unsqueeze(2).to_broadcast([P, CH, GE * SLOT_B]),
                        ALU.mult).then_inc(token_ready, 1)
                    n += 1

        @block.vector
        def _(dve):
            chain = Chain(dve, step, 0, 0)
            link = chain.link
            v = nc.vector
            dve.wait_ge(const_in, 16 * len(consts))
            link(v.tensor_tensor(sfc[:], gate_scores[:], bias[:].unsqueeze(1).to_broadcast([P, NT, NX]), ALU.add))
            x = sfc[:].rearrange("p t (g k) -> p (t g) k", k=GE)
            v.tensor_tensor(hi[:], x[:, :, 0:4], x[:, :, 4:8], ALU.max)
            link(v.tensor_tensor(lo[:], x[:, :, 0:4], x[:, :, 4:8], ALU.min))
            v.tensor_tensor(hi2[:], hi[:, :, 0:2], hi[:, :, 2:4], ALU.max)
            v.tensor_tensor(lo2[:], hi[:, :, 0:2], hi[:, :, 2:4], ALU.min)
            link(v.tensor_tensor(lo2b[:], lo[:, :, 0:2], lo[:, :, 2:4], ALU.max))
            link(v.tensor_tensor(lo2[:], lo2[:], lo2b[:], ALU.max))
            flat = gscore[:].rearrange("p t g -> p (t g)")
            v.tensor_tensor(flat, hi2[:, :, 0], hi2[:, :, 1], ALU.max)
            v.tensor_tensor(lo3[:], hi2[:, :, 0], hi2[:, :, 1], ALU.min)
            link(v.tensor_tensor(lo3b[:], lo2[:, :, 0], lo2[:, :, 1], ALU.max))
            link(v.tensor_tensor(lo3[:], lo3[:], lo3b[:], ALU.max))
            link(v.tensor_tensor(flat, flat, lo3[:], ALU.add))
            other = gscore[:].unsqueeze(2).to_broadcast([P, NT, G, G])
            own = gscore[:].unsqueeze(3).to_broadcast([P, NT, G, G])
            w4 = work[:].rearrange("p t (g k) -> p t g k", k=G)
            w4b = work2[:].rearrange("p t (g k) -> p t g k", k=G)
            v.tensor_tensor(w4, other, own, ALU.is_gt)
            link(v.tensor_tensor(w4b, other, own, ALU.is_equal))
            link(v.tensor_tensor(w4b, w4b, lower[:].unsqueeze(1).to_broadcast([P, NT, G, G]), ALU.mult))
            link(v.tensor_tensor(work[:], work[:], work2[:], ALU.add))
            link(v.tensor_reduce(rank[:], w4, AX_X, ALU.add))
            link(v.tensor_scalar(rank[:], rank[:], float(TOP_GROUPS), -FAR, ALU.is_ge, ALU.mult))
            link(v.tensor_tensor(work[:].rearrange("p t (g k) -> p (t g) k", k=GE), x,
                                 rank[:].rearrange("p t g -> p (t g)").unsqueeze(2).to_broadcast([P, NT * G, GE]), ALU.add))
            for t in range(NT):
                last = v.max(top[:, t, :], work[:, t, :])
            link(last)
            for t in range(NT):
                last = v.match_replace(work2[:, t, :], top[:, t, :], work[:, t, :], TAKEN)
            link(last)
            v.tensor_scalar(mask[:], work2[:], TAKEN, None, ALU.is_equal).then_inc(mask_ready, 1)
            dve.wait_ge(mask_ready, 1)
            link(v.tensor_tensor(gate_scores[:], gate_scores[:], mask[:], ALU.mult))
            link(v.tensor_reduce(wsum[:], gate_scores[:], AX_X, ALU.add))
            link(v.tensor_scalar(wsum[:], wsum[:], 1e-20, None, ALU.add))
            link(v.reciprocal(wsum[:], wsum[:]))
            link(v.tensor_scalar(wsum[:], wsum[:], ROUTE_SCALE, None, ALU.mult))
            v.tensor_tensor(gate_scores[:], gate_scores[:], wsum[:].unsqueeze(2).to_broadcast([P, NT, NX]), ALU.mult)
            pos = sfc
            total = work[:].rearrange("p t e -> p (t e)").rearrange("p (e t) -> p e t", t=NT)
            reset = work2[:].rearrange("p t e -> p (t e)").rearrange("p (e t) -> p e t", t=NT)
            for c in range(NCHUNK):
                dve.wait_ge(counted, c + 1)
                v.tensor_copy(pos[:, c * CH:(c + 1) * CH, :].rearrange("p t e -> p (t e)"), banks[2 * c % 8][:]).then_inc(kept, 1)
                v.tensor_copy(total[:, :, c * CH:(c + 1) * CH],
                              banks[(2 * c + 1) % 8][:].rearrange("p (t e) -> p e t", e=NX)).then_inc(kept, 1)
            dve.wait_ge(kept, 2 * NCHUNK)
            link(v.memset(reset, 1.0))
            link(v.memset(reset[:, :, 0:1], 0.0))
            running = ai[:].bitcast(F32)
            link(v.tensor_tensor_scan(running.rearrange("p t e -> p (t e)"), work2[:].rearrange("p t e -> p (t e)"),
                                      work[:].rearrange("p t e -> p (t e)"), 0.0, ALU.mult, ALU.add))
            link(v.tensor_tensor(work[:], running, work[:], ALU.subtract))
            link(v.tensor_tensor(pos[:], pos[:], total.rearrange("p e t -> p t e"), ALU.add))
            link(v.tensor_scalar(work2[:], mask[:], -UNCHOSEN, UNCHOSEN, ALU.mult, ALU.add))
            link(v.tensor_tensor(pos[:], pos[:], work2[:], ALU.add))
            link(v.tensor_copy(ai[:], pos[:]))
            v.tensor_scalar(bi[:], ai[:], SLOT_B - 1, None, ALU.bitwise_and)
            link(v.tensor_scalar(work2[:].bitcast(I32), ai[:], SLOT_BITS, None, ALU.arith_shift_right))
            high, low = work, pos
            v.tensor_copy(high[:], work2[:].bitcast(I32))
            link(v.tensor_copy(low[:], bi[:]))
            n = 0
            for g in range(G):
                e = slice(g * GE, (g + 1) * GE)
                for c in range(NCHUNK):
                    t = slice(c * CH, (c + 1) * CH)
                    if n >= 2:
                        dve.wait_ge(chunk_done, n - 1)
                    shape = [P, CH, GE, SLOT_B]
                    s = second[n % 2]
                    codes = iota[:].unsqueeze(1).unsqueeze(1).to_broadcast(shape)
                    v.tensor_tensor(s[:, 0], low[:, t, e].unsqueeze(3).to_broadcast(shape), codes, ALU.is_equal).then_inc(onehot_ready, 1)
                    v.tensor_tensor(first[n % 2][:], high[:, t, e].unsqueeze(3).to_broadcast(shape), codes, ALU.is_equal)
                    dve.wait_ge(onehot_ready, n + 1)
                    v.tensor_tensor(s[:, 2], s[:, 0], gate_scores[:, t, e].unsqueeze(3).to_broadcast(shape), ALU.mult).then_inc(second_ready, 1)
                    n += 1
                dve.wait_ge(chunk_done, n)
                v.tensor_tensor(picked[:], banks[g % 2][:, 0:2 * P].rearrange("p (i e b) -> p i e b", i=2, b=SLOT_B),
                                own_expert[:].unsqueeze(1).unsqueeze(3).to_broadcast([P, 2, GE, SLOT_B]), ALU.mult)\
                    .then_inc(picked_out, 1)
                dve.wait_ge(picked_out, g + 1)
                last = link(v.tensor_reduce(lists[:, :, g, :], picked[:].rearrange("p i e b -> p i b e"), AX_X, ALU.add))
            dve.sem_inc(lists_ready, 1)
            dve.wait_ge(flipped, 1)
            v.tensor_copy(slot_scale[:], banks[2][:, P:2 * P])
            link(v.tensor_scalar(hi[:, 0:NX // 2, :].rearrange("p a b -> p (a b)"), banks[2][:, 0:P], 0.0, None, ALU.is_equal))
            hole = hi[:, 0:NX // 2, :].rearrange("p a b -> p (a b)")
            link(v.tensor_tensor(hole, hole, row_empty[:], ALU.mult))
            link(v.tensor_tensor(hole, hole, banks[2][:, 0:P], ALU.add))
            link(v.tensor_scalar(slot_index[:], hole, -1.0, None, ALU.add))


def experts(nc, d, x2_rows, acc_rows, slot_index, slot_scale):
    with ExitStack() as ctx:
        def sb(name, shape, dt=F32):
            return ctx.enter_context(nc.sbuf_tensor("e_" + name, shape, dt))

        def sem(name):
            return ctx.enter_context(nc.semaphore("e_" + name))

        NS = 8
        ident = sb("ident", [P, P])
        wg, wu, wd = ([sb(f"{n}{i}", s) for i in range(NS)]
                      for n, s in (("wg", [P, HALVES, P]), ("wu", [P, HALVES, P]), ("wd", [P, E])))
        rows = [sb(f"rows{i}", [P, 2, E]) for i in range(NS)]
        rowsT = [sb(f"rowsT{i}", [P, HALVES, CAP]) for i in range(2)]
        silu = [sb(f"silu{i}", [P, CAP]) for i in range(2)]
        hidden = [sb(f"hidden{i}", [P, CAP]) for i in range(2)]
        y = [sb(f"y{i}", [P, 2, E]) for i in range(NS)]
        bankT, bankH, bankY = ([ctx.enter_context(nc.psum_tensor(f"e_{n}{i}", [P, 2, CAP], F32)) for i in range(2)]
                               for n in ("bankT", "bankH", "bankY"))
        ident_in = sem("ident_in")
        w_in = [sem(f"w_in{i}") for i in range(NS)]
        rows_in = [sem(f"rows_in{i}") for i in range(NS)]
        added = [sem(f"added{i}") for i in range(NS)]
        flipped, rowsT_ready, up_done, silu_ready, hidden_ready, down_done, y_ready = (
            sem(n) for n in ("flipped", "rowsT_ready", "up_done", "silu_ready", "hidden_ready", "down_done", "y_ready"))

        block = ctx.enter_context(nc.Block())

        @block.sync
        def _(sp):
            sp.dma_start(ident[:], d["ident"]).then_inc(ident_in, 16)

            def load(e, s):
                for dst, src in ((wg, "w_gate"), (wu, "w_up")):
                    sp.dma_start(dst[s][:], d[src][bass.ds(e, 1)].rearrange("e (a p) i -> p (e a) i", p=P)).then_inc(w_in[s], 16)
                sp.dma_start(wd[s][:], d["w_down"][bass.ds(e, 1)].rearrange("e i h -> (e i) h")).then_inc(w_in[s], 16)

            for s in range(NS):
                load(s, s)
            with sp.Fori(0, NX // NS - 1) as t:
                for s in range(NS):
                    sp.wait_ge(down_done, t * NS + s + 1)
                    load(t * NS + s + NS, s)

        @block.gpsimd
        def _(pool):
            def gather(e):
                s = e % NS
                if e >= NS:
                    pool.wait_ge(flipped, e - NS + 1)
                for i in range(2):
                    at = slot_index[:, 2 * e + i:2 * e + i + 1]
                    nc.gpsimd.indirect_dma_start(
                        out=rows[s][:, i, :], out_offset=None, in_=x2_rows,
                        in_offset=bass.IndirectOffsetOnAxis(ap=at, axis=0)).then_inc(rows_in[s], 16)

            def scatter(e):
                s = e % NS
                pool.wait_ge(y_ready, e + 1)
                if e >= 2:
                    pool.wait_ge(added[(e - 2) % NS], 32 * ((e - 2) // NS + 1))
                for i in range(2):
                    at = slot_index[:, 2 * e + i:2 * e + i + 1]
                    nc.gpsimd.indirect_dma_start(
                        out=acc_rows[e % 2], out_offset=bass.IndirectOffsetOnAxis(ap=at, axis=0),
                        in_=y[s][:, i, :], in_offset=None, compute_op=ALU.add).then_inc(added[s], 16)

            AHEAD = NS - 2
            for e in range(AHEAD):
                gather(e)
            for e in range(NX):
                if e + AHEAD < NX:
                    gather(e + AHEAD)
                scatter(e)
            for s in range(NS):
                pool.wait_ge(added[s], 32 * NX // NS)

        @block.tensor
        def _(pe):
            pe.wait_ge(ident_in, 16)

            def flip(e, t, s, first=False):
                pe.wait_ge(rows_in[s], t * 32 + 32)
                for a in range(HALVES):
                    for i in range(2):
                        mm = nc.tensor.transpose(bankT[s % 2][:, a, i * P:(i + 1) * P], rows[s][:, i, a * P:(a + 1) * P], ident[:])
                mm.then_inc(flipped, 1)

            def up(e, t, s, first=False):
                pe.wait_ge(w_in[s], t * 48 + 48)
                pe.wait_ge(rowsT_ready, e + 1)
                for n, w in enumerate((wg, wu)):
                    for a in range(HALVES):
                        mm = nc.tensor.matmul(bankH[s % 2][:, n, :], w[s][:, a, :], rowsT[s % 2][:, a, :],
                                              start=a == 0, stop=a == HALVES - 1)
                mm.then_inc(up_done, 1)

            def down(e, t, s, first=False):
                pe.wait_ge(hidden_ready, e + 1)
                if not first:
                    pe.wait_ge(y_ready, e - 1)
                for i in range(2):
                    mm = nc.tensor.matmul(bankY[s % 2][:, i, :], hidden[s % 2][:, i * P:(i + 1) * P], wd[s][:], start=True, stop=True)
                mm.then_inc(down_done, 1)

            flip(0, 0, 0)
            flip(1, 0, 1)
            up(0, 0, 0)

            def turn(t, last=False, head=False):
                for s in range(NS):
                    e = t * NS + s
                    more = s + 2 >= NS
                    if not (last and more):
                        flip(e + 2, t + 1 if more else t, (s + 2) % NS)
                    if not (last and s == NS - 1):
                        up(e + 1, t + 1 if s == NS - 1 else t, (s + 1) % NS)
                    down(e, t, s, first=head and s < 2)

            turn(0, head=True)
            with pe.Fori(1, NX // NS - 1) as t:
                turn(t)
            turn(NX // NS - 1, last=True)

        @block.scalar
        def _(act):
            def keep(e, s, first=False):
                act.wait_ge(flipped, e + 1)
                if not first:
                    act.wait_ge(up_done, e - 1)
                nc.scalar.activation(rowsT[s % 2][:], bankT[s % 2][:], ACT.Copy).then_inc(rowsT_ready, 1)

            def gate(e, s, first=False):
                act.wait_ge(up_done, e + 1)
                if not first:
                    act.wait_ge(hidden_ready, e - 1)
                nc.scalar.activation(silu[s % 2][:], bankH[s % 2][:, 0, :], ACT.Silu).then_inc(silu_ready, 1)

            keep(0, 0, True)
            keep(1, 1, True)
            gate(0, 0, True)

            def turn(t, last=False, head=False):
                for s in range(NS):
                    e = t * NS + s
                    if not (last and s + 2 >= NS):
                        keep(e + 2, s)
                    if not (last and s == NS - 1):
                        gate(e + 1, s + 1, first=head and s == 0)

            turn(0, head=True)
            with act.Fori(1, NX // NS - 1) as t:
                turn(t)
            turn(NX // NS - 1, last=True)

        @block.vector
        def _(dve):
            def product(e, s, first=False):
                dve.wait_ge(silu_ready, e + 1)
                if not first:
                    dve.wait_ge(down_done, e - 1)
                nc.vector.tensor_tensor(hidden[s % 2][:], silu[s % 2][:], bankH[s % 2][:, 1, :], ALU.mult).then_inc(hidden_ready, 1)

            def scale(e, t, s, first=False):
                dve.wait_ge(down_done, e + 1)
                if not first:
                    dve.wait_ge(added[s], t * 32)
                for i in range(2):
                    mm = nc.vector.tensor_scalar(y[s][:, i, :], bankY[s % 2][:, i, :], slot_scale[:, bass.ds(e * 2 + i, 1)], None, ALU.mult)
                mm.then_inc(y_ready, 1)

            product(0, 0, True)

            def turn(t, last=False, head=False):
                for s in range(NS):
                    e = t * NS + s
                    if not (last and s == NS - 1):
                        product(e + 1, s + 1, first=head and s == 0)
                    scale(e, t, s, first=head)

            turn(0, head=True)
            with dve.Fori(1, NX // NS - 1) as t:
                turn(t)
            turn(NX // NS - 1, last=True)


def final_norm(nc, acc_rows, out):
    with ExitStack() as ctx:
        def sb(name, shape, dt=F32):
            return ctx.enter_context(nc.sbuf_tensor("f_" + name, shape, dt))

        def sem(name):
            return ctx.enter_context(nc.semaphore("f_" + name))

        parts = [[sb(f"part{i}{j}", [P, QT, E]) for j in range(2)] for i in range(2)]
        r = [sb(f"r{i}", [P, QT, E]) for i in range(2)]
        normed = [sb(f"normed{i}", [P, QT, E]) for i in range(2)]
        stats, moments, rstd = ([sb(f"{n}{i}", [P, QT, w]) for i in range(2)] for n, w in (("stats", 6), ("moments", 2), ("rstd", 1)))
        eps = sb("eps", [P, 1])
        parts_in = [sem(f"parts_in{i}") for i in range(2)]
        stored = [sem(f"stored{i}") for i in range(2)]
        eps_ready, summed, moments_ready, deviation_ready, normed_ready, step = (
            sem(n) for n in ("eps_ready", "summed", "moments_ready", "deviation_ready", "normed_ready", "step"))

        def rows(dram, b):
            return dram[bass.ds(b * S, S), :].rearrange("(t p) e -> p t e", p=P)

        block = ctx.enter_context(nc.Block())

        @block.sync
        def _(sp):
            def load(b, i):
                for j in range(2):
                    sp.dma_start(parts[i][j][:], rows(acc_rows[j], b)).then_inc(parts_in[i], 16)

            load(0, 0)
            load(1, 1)
            with sp.Fori(0, B // 2 - 1) as t:
                for i in range(2):
                    sp.wait_ge(summed, t * 2 + i + 1)
                    load(t * 2 + i + 2, i)

        @block.gpsimd
        def _(pool):
            pool.memset(eps[:], EPS).then_inc(eps_ready, 1)
            with pool.Fori(0, B // 2) as t:
                for i in range(2):
                    pool.wait_ge(normed_ready, t * 2 + i + 1)
                    pool.dma_start(rows(out, t * 2 + i), normed[i][:]).then_inc(stored[i], 16)
            for i in range(2):
                pool.wait_ge(stored[i], 16 * B // 2)

        @block.scalar
        def _(act):
            act.wait_ge(eps_ready, 1)
            with act.Fori(0, B // 2) as t:
                for i in range(2):
                    deviation(nc, act, t * 2 + i, moments[i], rstd[i][:, :, 0], eps, moments_ready, deviation_ready)

        @block.vector
        def _(dve):
            def turn(t, i, first=False):
                b = t * 2 + i
                if not first:
                    dve.wait_ge(stored[i], t * 16)
                dve.wait_ge(parts_in[i], t * 32 + 32)
                nc.vector.tensor_tensor(r[i][:], parts[i][0][:], parts[i][1][:], ALU.add).then_inc(summed, 1)
                dve.wait_ge(summed, b + 1)
                take_moments(nc, r[i], stats[i], moments[i], dve, step, b * NORM_STEPS, moments_ready)
                apply_norm(nc, r[i], normed[i], moments[i], rstd[i][:, :, 0], dve, step, b * NORM_STEPS, b, deviation_ready).then_inc(normed_ready, 1)

            turn(0, 0, True)
            turn(0, 1, True)
            with dve.Fori(1, B // 2) as t:
                turn(t, 0)
                turn(t, 1)


def layouts(x, ctx_1024, mask_1x1xSxS2_ik0, **w):
    def c(a):
        return np.ascontiguousarray(a)

    def columns(v):
        return c(v.reshape(HALVES, P).T)

    out = {}
    out["a_xT"] = c(np.transpose(x, (0, 2, 1)))
    wq, bq = w["L0_attn_Wq"], w["L0_attn_bq"]
    out["a_wqT"], out["a_wkT"], out["a_wvT"] = c(wq.T), c(w["L0_attn_Wk"].T), c(w["L0_attn_Wv"].T)
    out["a_bq"], out["a_bk"], out["a_bv"] = columns(bq), columns(w["L0_attn_bk"]), c(w["L0_attn_bv"].reshape(1, E))
    r, k = w["L0_attn_rel_k_emb"], w["L0_attn_rel_v_emb"]
    j = np.arange(QG)[:, None]
    at = np.clip(j + (S - QG) - np.arange(TKW)[None, :], -MAXREL, MAXREL) + MAXREL
    out["relk"] = c(np.transpose(r[at], (0, 2, 1)).reshape(P, TKW))
    at = np.clip(np.arange(TVZ)[None, :] - P - np.arange(P)[:, None], -MAXREL, MAXREL) + MAXREL
    out["relv"] = c(k[at].reshape(P, TVZ * D))
    p = np.arange(P)
    hm = np.zeros((P, HH), np.float32)
    hm[p, p // D] = 1
    out["head_mask"] = hm
    qm = np.zeros((P, QG), np.float32)
    qm[p, p // D] = 1
    out["query_mask"] = qm
    om = np.zeros((P, QG, D), np.float32)
    om[p, p // HH % QG, :] = 1
    out["out_mask"] = om.reshape(P, P)
    kf = np.zeros((P, HALVES, 2, H), np.float32)
    for a in range(HALVES):
        for side in range(2):
            kf[p, a, side, a * HH + p // D] = r[side * 2 * MAXREL, p % D]
    out["relk_far"] = kf.reshape(P, HALVES * 2 * H)
    out["relv_far"] = c(np.broadcast_to(k[[0, 2 * MAXREL]], (P, 2, D)))
    out["ident"] = np.eye(P, dtype=np.float32)
    out["x"] = c(x.reshape(TOK, E))
    out["a_woT"], out["a_bo"] = c(w["L0_attn_Wo"].T), c(np.broadcast_to(w["L0_attn_bo"], (P, E)))
    for n in ("q", "k", "v", "o"):
        out[f"x_w{n}T"] = c(w[f"L0_xattn_W{n}"].T)
    out["x_bq"], out["x_bk"] = columns(w["L0_xattn_bq"]), columns(w["L0_xattn_bk"])
    out["x_bv"], out["x_bo"] = c(w["L0_xattn_bv"].reshape(1, E)), c(np.broadcast_to(w["L0_xattn_bo"], (P, E)))
    out["ctxT"] = c(np.repeat(np.transpose(ctx_1024, (2, 0, 1))[:, :, None, :], 2, axis=2))
    out["mask"] = c(mask_1x1xSxS2_ik0.reshape(S, SK))
    out["gate_wT"] = c(w["L0_ffn_gate_w"].T)
    half = np.zeros((P, H // HALVES), np.float32)
    half[p, p // D] = 1
    out["half_mask"] = half
    pair = np.zeros((P, 2, D), np.float32)
    pair[p, p // SK, :] = 1
    out["pair_mask"] = pair.reshape(P, 2 * D)
    out["gate_bias"] = c(np.broadcast_to(w["L0_ffn_gate_bias"], (P, NX)))
    out["before"] = np.triu(np.ones((P, P), np.float32), 1)
    out["lower"] = c(np.broadcast_to(np.tril(np.ones((NX // GE, NX // GE), np.float32), -1), (P, NX // GE, NX // GE)))
    out["iota"] = c(np.broadcast_to(np.arange(SLOT_B, dtype=np.float32), (P, SLOT_B)))
    out["token1"] = (p[:, None] + P * np.arange(NT)[None, :] + 1).astype(np.float32)
    out["row_empty"] = (TOK + 1 + p[:, None] + P * (np.arange(2 * NX)[None, :] % 2)).astype(np.float32)
    own = np.zeros((P, GE), np.float32)
    own[p, p // SLOT_A] = 1
    out["own_expert"] = own
    for n in ("w_gate", "w_up", "w_down"):
        out[n] = w[f"L0_ffn_{n}"]
    return out


def program(nc, d, out):
    qs = nc.dram_tensor("q_scratch", [B, E, S], F32).ap()
    far_scores = nc.dram_tensor("far_scores_scratch", [B, H, QG, NG], F32).ap()
    attnT = nc.dram_tensor("attn_scratch", [B, E, S], F32).ap()
    rel = nc.dram_tensor("rel_scratch", [B, S, E], F32).ap()
    x2_rows = nc.dram_tensor("x2_scratch", [TOK + CAP, E], F32).ap()
    acc_rows = [nc.dram_tensor(f"acc_scratch{i}", [TOK + CAP, E], F32).ap() for i in range(2)]
    slot_token = nc.dram_tensor("slot_token_scratch", [NX * CAP], F32).ap()
    slot_weight = nc.dram_tensor("slot_weight_scratch", [NX * CAP], F32).ap()
    project_queries(nc, d, qs, far_scores)
    self_attention(nc, d, qs, far_scores, attnT, rel)
    with (nc.sbuf_tensor("gate_scores", [P, NT, NX], F32) as gate_scores,
          nc.sbuf_tensor("slot_index", [P, 2 * NX], U32) as slot_index,
          nc.sbuf_tensor("slot_scale", [P, 2 * NX], F32) as slot_scale):
        cross_attention(nc, d, attnT, rel.rearrange("b s e -> (b s) e"), x2_rows, acc_rows,
                        gate_scores)
        route(nc, d, gate_scores, slot_token, slot_weight, slot_index, slot_scale)
        experts(nc, d, x2_rows, acc_rows, slot_index, slot_scale)
    final_norm(nc, acc_rows, out.rearrange("b s e -> (b s) e"))


def kernel(**inputs):
    import concourse.bacc as bacc
    from concourse.bass_utils import run_bass_kernel_spmd

    arrays = layouts(**{k: np.asarray(v) for k, v in inputs.items()})
    nc = bacc.Bacc("TRN2", target_bir_lowering=False, num_devices=1)
    named = {f"in_{k}": v for k, v in arrays.items()}
    d = {k: nc.dram_tensor(f"in_{k}", v.shape, mybir.dt.from_np(v.dtype), kind="ExternalInput").ap()
         for k, v in arrays.items()}
    out = nc.dram_tensor("out", [B, S, E], F32, kind="ExternalOutput").ap()
    program(nc, d, out)
    r = run_bass_kernel_spmd(nc, [named], core_ids=[0])
    return r.results[0]["out"]
```
